# Optimizing a Trainium2 kernel written in Bass

```python
import numpy as np
import jax
import jax.numpy as jnp

def _softmax(x, axis=-1):
    return jax.nn.softmax(x, axis=axis)

def _gelu(x):
    return jax.nn.gelu(x, approximate=True)

def _silu(x):
    return jax.nn.silu(x)

def _sigmoid(x):
    return jax.nn.sigmoid(x)

def _layernorm(x, axis=-1, eps=1e-05):
    m = jnp.mean(x, axis=axis, keepdims=True)
    v = jnp.var(x, axis=axis, keepdims=True)
    return (x - m) / jnp.sqrt(v + eps)

def _scatter_add(tgt, idx, src, axis=0):
    return tgt.at[idx].add(src)

def _segment_sum(src, seg, n):
    return jax.ops.segment_sum(src, seg, n)
kernel_name = 'mk_xattn_seq_d4_seqx_r4_b0dc74'

def setup_inputs(seed: int=0):
    np.random.seed(seed)
    _w = jnp.asarray

    def _rec_inputs():
        import jax
        import jax.numpy as jnp
        _rk = jax.random.key(seed)
        x = -0.0002928 + 1 * jax.random.normal(jax.random.fold_in(_rk, 1), (4, 512, 512), jnp.float32)
        _lenS = 512 - jax.random.randint(jax.random.fold_in(_rk, 7), (4,), 0, max(1, 512 // 4) + 1, jnp.int32)
        _lenS2 = 1024 - jax.random.randint(jax.random.fold_in(_rk, 8), (4,), 0, max(1, 1024 // 4) + 1, jnp.int32)
        _ctx_2048P = jax.random.normal(jax.random.fold_in(_rk, 11), (4, 16, 512), jnp.float32)
        _ctx_2048c = jax.random.dirichlet(jax.random.fold_in(_rk, 511), 0.3 * jnp.ones((16,), jnp.float32), (4, 1024))
        _ctx_2048t = jnp.einsum('bsk,bkd->bsd', _ctx_2048c, _ctx_2048P)
        _ctx_2048t = _ctx_2048t * jax.lax.rsqrt(jnp.mean(jnp.square(_ctx_2048t)) + 1e-12) * 0.953939
        ctx_2048 = 0.000189249 + 0.0999589 * (_ctx_2048t + 0.3 * jax.random.normal(jax.random.fold_in(_rk, 611), (4, 1024, 512), jnp.float32))
        _validS = jnp.arange(512)[None, :] < _lenS[:, None]
        _validS2 = jnp.arange(1024)[None, :] < _lenS2[:, None]
        _causal = jnp.tril(jnp.ones((512, 512), dtype=bool))
        mask_BxS2_bf1 = jnp.ones((4, 1024), dtype=bool)
        return (x, ctx_2048, mask_BxS2_bf1)
    x, ctx_2048, mask_BxS2_bf1 = _rec_inputs()

    def _L0_xattn_setup():
        import jax, jax.numpy as jnp
        import numpy as np
        B, L, E, H = (4, 128, 512, 32)
        S = E // H
        EXTRA_MAA, EXTRA_DECAY = (32, 64)
        EPS = 1e-05

        def _ln(x, w, b):
            m = jnp.mean(x, axis=-1, keepdims=True)
            v = jnp.mean((x - m) ** 2, axis=-1, keepdims=True)
            return (x - m) * jax.lax.rsqrt(v + EPS) * w + b

        def _token_shift(xn, prev_row):
            first = (prev_row - xn[:, 0])[:, None]
            rest = xn[:, :-1] - xn[:, 1:]
            return jnp.concatenate([first, rest], axis=1)
        key = jax.random.key(seed)
        ks = jax.random.split(key, 24)
        rn = lambda k, shp, s=1.0: jax.random.normal(k, shp, dtype=jnp.float32) * s
        return dict(x=rn(ks[0], (B, L, E)), state=rn(ks[1], (B, 2 + S, E), 0.1), ln1_w=jnp.ones((E,), jnp.float32), ln1_b=jnp.zeros((E,), jnp.float32), ln2_w=jnp.ones((E,), jnp.float32), ln2_b=jnp.zeros((E,), jnp.float32), maa_x=rn(ks[2], (E,), 0.02), maa_w1=rn(ks[3], (E, 5 * EXTRA_MAA), 0.02), maa_w2=rn(ks[4], (5, EXTRA_MAA, E), 0.02), maa_stack=rn(ks[5], (5, E), 0.02), time_decay=rn(ks[6], (E,), 0.5), decay_w1=rn(ks[7], (E, EXTRA_DECAY), 0.02), decay_w2=rn(ks[8], (EXTRA_DECAY, E), 0.02), faaaa=rn(ks[9], (H, S), 0.1), Wr=rn(ks[10], (E, E), 0.02), Wk=rn(ks[11], (E, E), 0.02), Wv=rn(ks[12], (E, E), 0.02), Wg=rn(ks[13], (E, E), 0.02), Wo=rn(ks[14], (E, E), 0.02), gn_w=jnp.ones((E,), jnp.float32), gn_b=jnp.zeros((E,), jnp.float32), ffn_maa_k=rn(ks[15], (E,), 0.02), ffn_maa_r=rn(ks[16], (E,), 0.02), ffn_Wk=rn(ks[17], (E, E), 0.02), ffn_Wr=rn(ks[18], (E, E), 0.02), ffn_Wv=rn(ks[19], (E, E), 0.02), i=0)
    _L0_xattn_all = _L0_xattn_setup()
    _L0_xattn_in = {k: v for k, v in _L0_xattn_all.items() if k in ('ln1_w', 'ln1_b', 'ln2_w', 'ln2_b', 'maa_x', 'maa_w1', 'maa_w2', 'maa_stack', 'time_decay', 'decay_w1', 'decay_w2', 'faaaa', 'Wr', 'Wk', 'Wv', 'Wg', 'Wo', 'gn_w', 'gn_b', 'ffn_maa_k', 'ffn_maa_r', 'ffn_Wk', 'ffn_Wr', 'ffn_Wv')}
    del _L0_xattn_all

    def _L1_xattn_setup():
        import jax, jax.numpy as jnp
        import numpy as np
        E, H, L, B = (512, 32, 256, 4)
        S = E // H
        DM, DD = (32, 64)

        def _ln(x, w, b, eps=1e-05):
            m = x.mean(-1, keepdims=True)
            v = ((x - m) ** 2).mean(-1, keepdims=True)
            return (x - m) / jnp.sqrt(v + eps) * w + b

        def _block(x, state, ln1_w, ln1_b, ln2_w, ln2_b, maa_x, maa_w1, maa_w2, maa_stack, time_decay, td_w1, td_w2, u, Wr, Wk, Wv, Wg, Wo, gn_w, gn_b, ffn_maa_k, ffn_maa_r, Wfk, Wfr, Wfv):
            b, l, e = x.shape
            h = u.shape[0]
            s_ = e // h
            xa = _ln(x, ln1_w, ln1_b)
            sx = jnp.concatenate([state[:, 1:2] - xa[:, :1], xa[:, :-1] - xa[:, 1:]], axis=1)
            xxx = jnp.tanh((xa + sx * maa_x) @ maa_w1).reshape(b, l, 5, DM)
            xxx = jnp.einsum('blfd,fde->blfe', xxx, maa_w2)
            xm = xa[:, :, None] + sx[:, :, None] * (maa_stack + xxx)
            xk, xw, xv, xr, xg = (xm[:, :, j] for j in range(5))
            w = jnp.exp(-jnp.exp(time_decay + jnp.tanh(xw @ td_w1) @ td_w2)).reshape(b, l, h, s_)
            r = (xr @ Wr.T).reshape(b, l, h, s_)
            k = (xk @ Wk.T).reshape(b, l, h, s_)
            v = (xv @ Wv.T).reshape(b, l, h, s_)
            g = jax.nn.silu(xg @ Wg.T)
            s0 = state[:, 2:2 + s_].reshape(b, h, s_, s_)

            def step(s, rkvw):
                r_t, k_t, v_t, w_t = rkvw
                a = k_t[..., :, None] * v_t[..., None, :]
                out = jnp.einsum('bhi,bhij->bhj', r_t, u * a + s)
                s = a + w_t[..., :, None] * s
                return (s, out)
            rkvw = tuple((jnp.moveaxis(t, 1, 0) for t in (r, k, v, w)))
            _, out = jax.lax.scan(step, s0, rkvw)
            out = jnp.moveaxis(out, 0, 1).reshape(b, l, e)
            og = out.reshape(b, l, h, s_)
            m = og.mean(-1, keepdims=True)
            va = ((og - m) ** 2).mean(-1, keepdims=True)
            og = ((og - m) / jnp.sqrt(va + 1e-05)).reshape(b, l, e) * gn_w + gn_b
            x1 = x + og * g @ Wo.T
            xc = _ln(x1, ln2_w, ln2_b)
            sx2 = jnp.concatenate([state[:, 0:1] - xc[:, :1], xc[:, :-1] - xc[:, 1:]], axis=1)
            xk2 = xc + sx2 * ffn_maa_k
            xr2 = xc + sx2 * ffn_maa_r
            rr = jax.nn.sigmoid(xr2 @ Wfr.T)
            kk = jnp.square(jax.nn.relu(xk2 @ Wfk.T))
            return x1 + rr * (kk @ Wfv.T)
        key = jax.random.key(seed)
        ks = jax.random.split(key, 24)
        sc = 0.02
        d = {'x': jax.random.normal(ks[0], (B, L, E), jnp.float32), 'state': jax.random.normal(ks[1], (B, 2 + S, E), jnp.float32) * 0.1, 'ln1_w': jnp.ones((E,), jnp.float32), 'ln1_b': jnp.zeros((E,), jnp.float32), 'ln2_w': jnp.ones((E,), jnp.float32), 'ln2_b': jnp.zeros((E,), jnp.float32), 'maa_x': jax.random.normal(ks[2], (E,), jnp.float32) * 0.1, 'maa_w1': jax.random.normal(ks[3], (E, 5 * DM), jnp.float32) * sc, 'maa_w2': jax.random.normal(ks[4], (5, DM, E), jnp.float32) * sc, 'maa_stack': jax.random.normal(ks[5], (1, 5, E), jnp.float32) * 0.1, 'time_decay': jax.random.normal(ks[6], (E,), jnp.float32) * 0.5, 'td_w1': jax.random.normal(ks[7], (E, DD), jnp.float32) * sc, 'td_w2': jax.random.normal(ks[8], (DD, E), jnp.float32) * sc, 'u': jax.random.normal(ks[9], (H, S, 1), jnp.float32) * 0.1, 'Wr': jax.random.normal(ks[10], (E, E), jnp.float32) * sc, 'Wk': jax.random.normal(ks[11], (E, E), jnp.float32) * sc, 'Wv': jax.random.normal(ks[12], (E, E), jnp.float32) * sc, 'Wg': jax.random.normal(ks[13], (E, E), jnp.float32) * sc, 'Wo': jax.random.normal(ks[14], (E, E), jnp.float32) * sc, 'gn_w': jnp.ones((E,), jnp.float32), 'gn_b': jnp.zeros((E,), jnp.float32), 'ffn_maa_k': jax.random.normal(ks[15], (E,), jnp.float32) * 0.1, 'ffn_maa_r': jax.random.normal(ks[16], (E,), jnp.float32) * 0.1, 'Wfk': jax.random.normal(ks[17], (E, E), jnp.float32) * sc, 'Wfr': jax.random.normal(ks[18], (E, E), jnp.float32) * sc, 'Wfv': jax.random.normal(ks[19], (E, E), jnp.float32) * sc}
        return d
    _L1_xattn_all = _L1_xattn_setup()
    _L1_xattn_in = {k: v for k, v in _L1_xattn_all.items() if k in ('ln1_w', 'ln1_b', 'ln2_w', 'ln2_b', 'maa_x', 'maa_w1', 'maa_w2', 'maa_stack', 'time_decay', 'td_w1', 'td_w2', 'u', 'Wr', 'Wk', 'Wv', 'Wg', 'Wo', 'gn_w', 'gn_b', 'ffn_maa_k', 'ffn_maa_r', 'Wfk', 'Wfr', 'Wfv')}
    del _L1_xattn_all

    def _L2_xattn_setup():
        import jax, jax.numpy as jnp
        import numpy as np
        E, H, L, B = (512, 32, 256, 4)
        S = E // H
        DM, DD = (32, 64)

        def _ln(x, w, b, eps=1e-05):
            m = x.mean(-1, keepdims=True)
            v = ((x - m) ** 2).mean(-1, keepdims=True)
            return (x - m) / jnp.sqrt(v + eps) * w + b

        def _block(x, state, ln1_w, ln1_b, ln2_w, ln2_b, maa_x, maa_w1, maa_w2, maa_stack, time_decay, td_w1, td_w2, u, Wr, Wk, Wv, Wg, Wo, gn_w, gn_b, ffn_maa_k, ffn_maa_r, Wfk, Wfr, Wfv):
            b, l, e = x.shape
            h = u.shape[0]
            s_ = e // h
            xa = _ln(x, ln1_w, ln1_b)
            sx = jnp.concatenate([state[:, 1:2] - xa[:, :1], xa[:, :-1] - xa[:, 1:]], axis=1)
            xxx = jnp.tanh((xa + sx * maa_x) @ maa_w1).reshape(b, l, 5, DM)
            xxx = jnp.einsum('blfd,fde->blfe', xxx, maa_w2)
            xm = xa[:, :, None] + sx[:, :, None] * (maa_stack + xxx)
            xk, xw, xv, xr, xg = (xm[:, :, j] for j in range(5))
            w = jnp.exp(-jnp.exp(time_decay + jnp.tanh(xw @ td_w1) @ td_w2)).reshape(b, l, h, s_)
            r = (xr @ Wr.T).reshape(b, l, h, s_)
            k = (xk @ Wk.T).reshape(b, l, h, s_)
            v = (xv @ Wv.T).reshape(b, l, h, s_)
            g = jax.nn.silu(xg @ Wg.T)
            s0 = state[:, 2:2 + s_].reshape(b, h, s_, s_)

            def step(s, rkvw):
                r_t, k_t, v_t, w_t = rkvw
                a = k_t[..., :, None] * v_t[..., None, :]
                out = jnp.einsum('bhi,bhij->bhj', r_t, u * a + s)
                s = a + w_t[..., :, None] * s
                return (s, out)
            rkvw = tuple((jnp.moveaxis(t, 1, 0) for t in (r, k, v, w)))
            _, out = jax.lax.scan(step, s0, rkvw)
            out = jnp.moveaxis(out, 0, 1).reshape(b, l, e)
            og = out.reshape(b, l, h, s_)
            m = og.mean(-1, keepdims=True)
            va = ((og - m) ** 2).mean(-1, keepdims=True)
            og = ((og - m) / jnp.sqrt(va + 1e-05)).reshape(b, l, e) * gn_w + gn_b
            x1 = x + og * g @ Wo.T
            xc = _ln(x1, ln2_w, ln2_b)
            sx2 = jnp.concatenate([state[:, 0:1] - xc[:, :1], xc[:, :-1] - xc[:, 1:]], axis=1)
            xk2 = xc + sx2 * ffn_maa_k
            xr2 = xc + sx2 * ffn_maa_r
            rr = jax.nn.sigmoid(xr2 @ Wfr.T)
            kk = jnp.square(jax.nn.relu(xk2 @ Wfk.T))
            return x1 + rr * (kk @ Wfv.T)
        key = jax.random.key(seed)
        ks = jax.random.split(key, 24)
        sc = 0.02
        d = {'x': jax.random.normal(ks[0], (B, L, E), jnp.float32), 'state': jax.random.normal(ks[1], (B, 2 + S, E), jnp.float32) * 0.1, 'ln1_w': jnp.ones((E,), jnp.float32), 'ln1_b': jnp.zeros((E,), jnp.float32), 'ln2_w': jnp.ones((E,), jnp.float32), 'ln2_b': jnp.zeros((E,), jnp.float32), 'maa_x': jax.random.normal(ks[2], (E,), jnp.float32) * 0.1, 'maa_w1': jax.random.normal(ks[3], (E, 5 * DM), jnp.float32) * sc, 'maa_w2': jax.random.normal(ks[4], (5, DM, E), jnp.float32) * sc, 'maa_stack': jax.random.normal(ks[5], (1, 5, E), jnp.float32) * 0.1, 'time_decay': jax.random.normal(ks[6], (E,), jnp.float32) * 0.5, 'td_w1': jax.random.normal(ks[7], (E, DD), jnp.float32) * sc, 'td_w2': jax.random.normal(ks[8], (DD, E), jnp.float32) * sc, 'u': jax.random.normal(ks[9], (H, S, 1), jnp.float32) * 0.1, 'Wr': jax.random.normal(ks[10], (E, E), jnp.float32) * sc, 'Wk': jax.random.normal(ks[11], (E, E), jnp.float32) * sc, 'Wv': jax.random.normal(ks[12], (E, E), jnp.float32) * sc, 'Wg': jax.random.normal(ks[13], (E, E), jnp.float32) * sc, 'Wo': jax.random.normal(ks[14], (E, E), jnp.float32) * sc, 'gn_w': jnp.ones((E,), jnp.float32), 'gn_b': jnp.zeros((E,), jnp.float32), 'ffn_maa_k': jax.random.normal(ks[15], (E,), jnp.float32) * 0.1, 'ffn_maa_r': jax.random.normal(ks[16], (E,), jnp.float32) * 0.1, 'Wfk': jax.random.normal(ks[17], (E, E), jnp.float32) * sc, 'Wfr': jax.random.normal(ks[18], (E, E), jnp.float32) * sc, 'Wfv': jax.random.normal(ks[19], (E, E), jnp.float32) * sc}
        return d
    _L2_xattn_all = _L2_xattn_setup()
    _L2_xattn_in = {k: v for k, v in _L2_xattn_all.items() if k in ('ln1_w', 'ln1_b', 'ln2_w', 'ln2_b', 'maa_x', 'maa_w1', 'maa_w2', 'maa_stack', 'time_decay', 'td_w1', 'td_w2', 'u', 'Wr', 'Wk', 'Wv', 'Wg', 'Wo', 'gn_w', 'gn_b', 'ffn_maa_k', 'ffn_maa_r', 'Wfk', 'Wfr', 'Wfv')}
    del _L2_xattn_all

    def _L3_xattn_setup():
        import jax, jax.numpy as jnp
        import numpy as np
        HIDDEN = 512
        HEADS = 16
        HEAD_DIM = HIDDEN // HEADS
        LN_EPS = 1e-05
        GATE_INIT = 0.5

        def _layer_norm(x, gamma, beta):
            mu = jnp.mean(x, axis=-1, keepdims=True)
            var = jnp.mean(jnp.square(x - mu), axis=-1, keepdims=True)
            return (x - mu) * jax.lax.rsqrt(var + LN_EPS) * gamma + beta
        key = jax.random.key(seed)
        ks = jax.random.split(key, 8)
        B, T_TEXT, T_AUDIO = (4, 512, 375)
        s = 0.02
        return {'hidden_states': jax.random.normal(ks[0], (B, T_TEXT, HIDDEN), jnp.float32), 'audio_kv': jax.random.normal(ks[1], (B, T_AUDIO, HIDDEN), jnp.float32), 'audio_attention_mask': jnp.ones((B, T_AUDIO), dtype=bool), 'Wq': jax.random.normal(ks[2], (HIDDEN, HIDDEN), jnp.float32) * s, 'Wk': jax.random.normal(ks[3], (HIDDEN, HIDDEN), jnp.float32) * s, 'Wv': jax.random.normal(ks[4], (HIDDEN, HIDDEN), jnp.float32) * s, 'Wo': jax.random.normal(ks[5], (HIDDEN, HIDDEN), jnp.float32) * s, 'ln_gamma': jnp.ones((HIDDEN,), jnp.float32), 'ln_beta': jnp.zeros((HIDDEN,), jnp.float32), 'gate': jnp.array([GATE_INIT], jnp.float32)}
    _L3_xattn_all = _L3_xattn_setup()
    _L3_xattn_in = {k: v for k, v in _L3_xattn_all.items() if k in ('Wq', 'Wk', 'Wv', 'Wo', 'ln_gamma', 'ln_beta', 'gate')}
    del _L3_xattn_all
    return {'x': x, 'ctx_2048': ctx_2048, 'mask_BxS2_bf1': mask_BxS2_bf1, 'L0_xattn_ln1_w': _L0_xattn_in['ln1_w'], 'L0_xattn_ln1_b': _L0_xattn_in['ln1_b'], 'L0_xattn_ln2_w': _L0_xattn_in['ln2_w'], 'L0_xattn_ln2_b': _L0_xattn_in['ln2_b'], 'L0_xattn_maa_x': _L0_xattn_in['maa_x'], 'L0_xattn_maa_w1': _L0_xattn_in['maa_w1'], 'L0_xattn_maa_w2': _L0_xattn_in['maa_w2'], 'L0_xattn_maa_stack': _L0_xattn_in['maa_stack'], 'L0_xattn_time_decay': _L0_xattn_in['time_decay'], 'L0_xattn_decay_w1': _L0_xattn_in['decay_w1'], 'L0_xattn_decay_w2': _L0_xattn_in['decay_w2'], 'L0_xattn_faaaa': _L0_xattn_in['faaaa'], 'L0_xattn_Wr': _L0_xattn_in['Wr'], 'L0_xattn_Wk': _L0_xattn_in['Wk'], 'L0_xattn_Wv': _L0_xattn_in['Wv'], 'L0_xattn_Wg': _L0_xattn_in['Wg'], 'L0_xattn_Wo': _L0_xattn_in['Wo'], 'L0_xattn_gn_w': _L0_xattn_in['gn_w'], 'L0_xattn_gn_b': _L0_xattn_in['gn_b'], 'L0_xattn_ffn_maa_k': _L0_xattn_in['ffn_maa_k'], 'L0_xattn_ffn_maa_r': _L0_xattn_in['ffn_maa_r'], 'L0_xattn_ffn_Wk': _L0_xattn_in['ffn_Wk'], 'L0_xattn_ffn_Wr': _L0_xattn_in['ffn_Wr'], 'L0_xattn_ffn_Wv': _L0_xattn_in['ffn_Wv'], 'L1_xattn_ln1_w': _L1_xattn_in['ln1_w'], 'L1_xattn_ln1_b': _L1_xattn_in['ln1_b'], 'L1_xattn_ln2_w': _L1_xattn_in['ln2_w'], 'L1_xattn_ln2_b': _L1_xattn_in['ln2_b'], 'L1_xattn_maa_x': _L1_xattn_in['maa_x'], 'L1_xattn_maa_w1': _L1_xattn_in['maa_w1'], 'L1_xattn_maa_w2': _L1_xattn_in['maa_w2'], 'L1_xattn_maa_stack': _L1_xattn_in['maa_stack'], 'L1_xattn_time_decay': _L1_xattn_in['time_decay'], 'L1_xattn_td_w1': _L1_xattn_in['td_w1'], 'L1_xattn_td_w2': _L1_xattn_in['td_w2'], 'L1_xattn_u': _L1_xattn_in['u'], 'L1_xattn_Wr': _L1_xattn_in['Wr'], 'L1_xattn_Wk': _L1_xattn_in['Wk'], 'L1_xattn_Wv': _L1_xattn_in['Wv'], 'L1_xattn_Wg': _L1_xattn_in['Wg'], 'L1_xattn_Wo': _L1_xattn_in['Wo'], 'L1_xattn_gn_w': _L1_xattn_in['gn_w'], 'L1_xattn_gn_b': _L1_xattn_in['gn_b'], 'L1_xattn_ffn_maa_k': _L1_xattn_in['ffn_maa_k'], 'L1_xattn_ffn_maa_r': _L1_xattn_in['ffn_maa_r'], 'L1_xattn_Wfk': _L1_xattn_in['Wfk'], 'L1_xattn_Wfr': _L1_xattn_in['Wfr'], 'L1_xattn_Wfv': _L1_xattn_in['Wfv'], 'L2_xattn_ln1_w': _L2_xattn_in['ln1_w'], 'L2_xattn_ln1_b': _L2_xattn_in['ln1_b'], 'L2_xattn_ln2_w': _L2_xattn_in['ln2_w'], 'L2_xattn_ln2_b': _L2_xattn_in['ln2_b'], 'L2_xattn_maa_x': _L2_xattn_in['maa_x'], 'L2_xattn_maa_w1': _L2_xattn_in['maa_w1'], 'L2_xattn_maa_w2': _L2_xattn_in['maa_w2'], 'L2_xattn_maa_stack': _L2_xattn_in['maa_stack'], 'L2_xattn_time_decay': _L2_xattn_in['time_decay'], 'L2_xattn_td_w1': _L2_xattn_in['td_w1'], 'L2_xattn_td_w2': _L2_xattn_in['td_w2'], 'L2_xattn_u': _L2_xattn_in['u'], 'L2_xattn_Wr': _L2_xattn_in['Wr'], 'L2_xattn_Wk': _L2_xattn_in['Wk'], 'L2_xattn_Wv': _L2_xattn_in['Wv'], 'L2_xattn_Wg': _L2_xattn_in['Wg'], 'L2_xattn_Wo': _L2_xattn_in['Wo'], 'L2_xattn_gn_w': _L2_xattn_in['gn_w'], 'L2_xattn_gn_b': _L2_xattn_in['gn_b'], 'L2_xattn_ffn_maa_k': _L2_xattn_in['ffn_maa_k'], 'L2_xattn_ffn_maa_r': _L2_xattn_in['ffn_maa_r'], 'L2_xattn_Wfk': _L2_xattn_in['Wfk'], 'L2_xattn_Wfr': _L2_xattn_in['Wfr'], 'L2_xattn_Wfv': _L2_xattn_in['Wfv'], 'L3_xattn_Wq': _L3_xattn_in['Wq'], 'L3_xattn_Wk': _L3_xattn_in['Wk'], 'L3_xattn_Wv': _L3_xattn_in['Wv'], 'L3_xattn_Wo': _L3_xattn_in['Wo'], 'L3_xattn_ln_gamma': _L3_xattn_in['ln_gamma'], 'L3_xattn_ln_beta': _L3_xattn_in['ln_beta'], 'L3_xattn_gate': _L3_xattn_in['gate']}

def reference(x, ctx_2048, mask_BxS2_bf1, L0_xattn_ln1_w, L0_xattn_ln1_b, L0_xattn_ln2_w, L0_xattn_ln2_b, L0_xattn_maa_x, L0_xattn_maa_w1, L0_xattn_maa_w2, L0_xattn_maa_stack, L0_xattn_time_decay, L0_xattn_decay_w1, L0_xattn_decay_w2, L0_xattn_faaaa, L0_xattn_Wr, L0_xattn_Wk, L0_xattn_Wv, L0_xattn_Wg, L0_xattn_Wo, L0_xattn_gn_w, L0_xattn_gn_b, L0_xattn_ffn_maa_k, L0_xattn_ffn_maa_r, L0_xattn_ffn_Wk, L0_xattn_ffn_Wr, L0_xattn_ffn_Wv, L1_xattn_ln1_w, L1_xattn_ln1_b, L1_xattn_ln2_w, L1_xattn_ln2_b, L1_xattn_maa_x, L1_xattn_maa_w1, L1_xattn_maa_w2, L1_xattn_maa_stack, L1_xattn_time_decay, L1_xattn_td_w1, L1_xattn_td_w2, L1_xattn_u, L1_xattn_Wr, L1_xattn_Wk, L1_xattn_Wv, L1_xattn_Wg, L1_xattn_Wo, L1_xattn_gn_w, L1_xattn_gn_b, L1_xattn_ffn_maa_k, L1_xattn_ffn_maa_r, L1_xattn_Wfk, L1_xattn_Wfr, L1_xattn_Wfv, L2_xattn_ln1_w, L2_xattn_ln1_b, L2_xattn_ln2_w, L2_xattn_ln2_b, L2_xattn_maa_x, L2_xattn_maa_w1, L2_xattn_maa_w2, L2_xattn_maa_stack, L2_xattn_time_decay, L2_xattn_td_w1, L2_xattn_td_w2, L2_xattn_u, L2_xattn_Wr, L2_xattn_Wk, L2_xattn_Wv, L2_xattn_Wg, L2_xattn_Wo, L2_xattn_gn_w, L2_xattn_gn_b, L2_xattn_ffn_maa_k, L2_xattn_ffn_maa_r, L2_xattn_Wfk, L2_xattn_Wfr, L2_xattn_Wfv, L3_xattn_Wq, L3_xattn_Wk, L3_xattn_Wv, L3_xattn_Wo, L3_xattn_ln_gamma, L3_xattn_ln_beta, L3_xattn_gate):
    import jax
    import jax.numpy as jnp

    def _L0_xattn_ref(x, state, ln1_w, ln1_b, ln2_w, ln2_b, maa_x, maa_w1, maa_w2, maa_stack, time_decay, decay_w1, decay_w2, faaaa, Wr, Wk, Wv, Wg, Wo, gn_w, gn_b, ffn_maa_k, ffn_maa_r, ffn_Wk, ffn_Wr, ffn_Wv, i):
        import jax, jax.numpy as jnp
        import numpy as np
        B, L, E, H = (4, 128, 512, 32)
        S = E // H
        EXTRA_MAA, EXTRA_DECAY = (32, 64)
        EPS = 1e-05

        def _ln(x, w, b):
            m = jnp.mean(x, axis=-1, keepdims=True)
            v = jnp.mean((x - m) ** 2, axis=-1, keepdims=True)
            return (x - m) * jax.lax.rsqrt(v + EPS) * w + b

        def _token_shift(xn, prev_row):
            first = (prev_row - xn[:, 0])[:, None]
            rest = xn[:, :-1] - xn[:, 1:]
            return jnp.concatenate([first, rest], axis=1)
        b, l = (x.shape[0], x.shape[1])
        i0 = (2 + S) * i + 0
        i1 = (2 + S) * i + 1
        xn = _ln(x, ln1_w, ln1_b)
        sx = _token_shift(xn, state[:, i1])
        xxx = jnp.tanh((xn + sx * maa_x) @ maa_w1).reshape(b, l, 5, 1, EXTRA_MAA)
        xxx = jnp.matmul(xxx, maa_w2).reshape(b, l, 5, E)
        x5 = xn[:, :, None] + sx[:, :, None] * (maa_stack + xxx)
        w = jnp.exp(-jnp.exp(time_decay + jnp.tanh(x5[:, :, 1] @ decay_w1) @ decay_w2))
        w = w.reshape(b, l, H, S)
        r = (x5[:, :, 3] @ Wr.T).reshape(b, l, H, S)
        k = (x5[:, :, 0] @ Wk.T).reshape(b, l, H, S)
        v = (x5[:, :, 2] @ Wv.T).reshape(b, l, H, S)
        g = jax.nn.silu(x5[:, :, 4] @ Wg.T)
        s0 = state[:, (2 + S) * i + 2:(2 + S) * (i + 1)].reshape(b, H, S, S)
        u = faaaa[None, :, :, None]

        def step(s, rkvw):
            r_t, k_t, v_t, w_t = rkvw
            a = k_t[:, :, :, None] * v_t[:, :, None, :]
            out = jnp.einsum('bhk,bhkd->bhd', r_t, u * a + s)
            return (a + w_t[:, :, :, None] * s, out)
        xs = tuple((jnp.moveaxis(t, 1, 0) for t in (r, k, v, w)))
        _, outs = jax.lax.scan(step, s0, xs)
        att = jnp.moveaxis(outs, 0, 1).reshape(b, l, E)
        a4 = att.reshape(b, l, H, S)
        m = jnp.mean(a4, axis=-1, keepdims=True)
        var = jnp.mean((a4 - m) ** 2, axis=-1, keepdims=True)
        att = ((a4 - m) * jax.lax.rsqrt(var + EPS)).reshape(b, l, E) * gn_w + gn_b
        x = x + att * g @ Wo.T
        xn2 = _ln(x, ln2_w, ln2_b)
        sx2 = _token_shift(xn2, state[:, i0])
        xk = xn2 + sx2 * ffn_maa_k
        xr = xn2 + sx2 * ffn_maa_r
        rr = jax.nn.sigmoid(xr @ ffn_Wr.T)
        kk = jnp.square(jax.nn.relu(xk @ ffn_Wk.T))
        x = x + rr * (kk @ ffn_Wv.T)
        return x

    def _L1_xattn_ref(x, state, ln1_w, ln1_b, ln2_w, ln2_b, maa_x, maa_w1, maa_w2, maa_stack, time_decay, td_w1, td_w2, u, Wr, Wk, Wv, Wg, Wo, gn_w, gn_b, ffn_maa_k, ffn_maa_r, Wfk, Wfr, Wfv):
        import jax, jax.numpy as jnp
        import numpy as np
        E, H, L, B = (512, 32, 256, 4)
        S = E // H
        DM, DD = (32, 64)

        def _ln(x, w, b, eps=1e-05):
            m = x.mean(-1, keepdims=True)
            v = ((x - m) ** 2).mean(-1, keepdims=True)
            return (x - m) / jnp.sqrt(v + eps) * w + b

        def _block(x, state, ln1_w, ln1_b, ln2_w, ln2_b, maa_x, maa_w1, maa_w2, maa_stack, time_decay, td_w1, td_w2, u, Wr, Wk, Wv, Wg, Wo, gn_w, gn_b, ffn_maa_k, ffn_maa_r, Wfk, Wfr, Wfv):
            b, l, e = x.shape
            h = u.shape[0]
            s_ = e // h
            xa = _ln(x, ln1_w, ln1_b)
            sx = jnp.concatenate([state[:, 1:2] - xa[:, :1], xa[:, :-1] - xa[:, 1:]], axis=1)
            xxx = jnp.tanh((xa + sx * maa_x) @ maa_w1).reshape(b, l, 5, DM)
            xxx = jnp.einsum('blfd,fde->blfe', xxx, maa_w2)
            xm = xa[:, :, None] + sx[:, :, None] * (maa_stack + xxx)
            xk, xw, xv, xr, xg = (xm[:, :, j] for j in range(5))
            w = jnp.exp(-jnp.exp(time_decay + jnp.tanh(xw @ td_w1) @ td_w2)).reshape(b, l, h, s_)
            r = (xr @ Wr.T).reshape(b, l, h, s_)
            k = (xk @ Wk.T).reshape(b, l, h, s_)
            v = (xv @ Wv.T).reshape(b, l, h, s_)
            g = jax.nn.silu(xg @ Wg.T)
            s0 = state[:, 2:2 + s_].reshape(b, h, s_, s_)

            def step(s, rkvw):
                r_t, k_t, v_t, w_t = rkvw
                a = k_t[..., :, None] * v_t[..., None, :]
                out = jnp.einsum('bhi,bhij->bhj', r_t, u * a + s)
                s = a + w_t[..., :, None] * s
                return (s, out)
            rkvw = tuple((jnp.moveaxis(t, 1, 0) for t in (r, k, v, w)))
            _, out = jax.lax.scan(step, s0, rkvw)
            out = jnp.moveaxis(out, 0, 1).reshape(b, l, e)
            og = out.reshape(b, l, h, s_)
            m = og.mean(-1, keepdims=True)
            va = ((og - m) ** 2).mean(-1, keepdims=True)
            og = ((og - m) / jnp.sqrt(va + 1e-05)).reshape(b, l, e) * gn_w + gn_b
            x1 = x + og * g @ Wo.T
            xc = _ln(x1, ln2_w, ln2_b)
            sx2 = jnp.concatenate([state[:, 0:1] - xc[:, :1], xc[:, :-1] - xc[:, 1:]], axis=1)
            xk2 = xc + sx2 * ffn_maa_k
            xr2 = xc + sx2 * ffn_maa_r
            rr = jax.nn.sigmoid(xr2 @ Wfr.T)
            kk = jnp.square(jax.nn.relu(xk2 @ Wfk.T))
            return x1 + rr * (kk @ Wfv.T)
        return _block(x, state, ln1_w, ln1_b, ln2_w, ln2_b, maa_x, maa_w1, maa_w2, maa_stack, time_decay, td_w1, td_w2, u, Wr, Wk, Wv, Wg, Wo, gn_w, gn_b, ffn_maa_k, ffn_maa_r, Wfk, Wfr, Wfv)

    def _L2_xattn_ref(x, state, ln1_w, ln1_b, ln2_w, ln2_b, maa_x, maa_w1, maa_w2, maa_stack, time_decay, td_w1, td_w2, u, Wr, Wk, Wv, Wg, Wo, gn_w, gn_b, ffn_maa_k, ffn_maa_r, Wfk, Wfr, Wfv):
        import jax, jax.numpy as jnp
        import numpy as np
        E, H, L, B = (512, 32, 256, 4)
        S = E // H
        DM, DD = (32, 64)

        def _ln(x, w, b, eps=1e-05):
            m = x.mean(-1, keepdims=True)
            v = ((x - m) ** 2).mean(-1, keepdims=True)
            return (x - m) / jnp.sqrt(v + eps) * w + b

        def _block(x, state, ln1_w, ln1_b, ln2_w, ln2_b, maa_x, maa_w1, maa_w2, maa_stack, time_decay, td_w1, td_w2, u, Wr, Wk, Wv, Wg, Wo, gn_w, gn_b, ffn_maa_k, ffn_maa_r, Wfk, Wfr, Wfv):
            b, l, e = x.shape
            h = u.shape[0]
            s_ = e // h
            xa = _ln(x, ln1_w, ln1_b)
            sx = jnp.concatenate([state[:, 1:2] - xa[:, :1], xa[:, :-1] - xa[:, 1:]], axis=1)
            xxx = jnp.tanh((xa + sx * maa_x) @ maa_w1).reshape(b, l, 5, DM)
            xxx = jnp.einsum('blfd,fde->blfe', xxx, maa_w2)
            xm = xa[:, :, None] + sx[:, :, None] * (maa_stack + xxx)
            xk, xw, xv, xr, xg = (xm[:, :, j] for j in range(5))
            w = jnp.exp(-jnp.exp(time_decay + jnp.tanh(xw @ td_w1) @ td_w2)).reshape(b, l, h, s_)
            r = (xr @ Wr.T).reshape(b, l, h, s_)
            k = (xk @ Wk.T).reshape(b, l, h, s_)
            v = (xv @ Wv.T).reshape(b, l, h, s_)
            g = jax.nn.silu(xg @ Wg.T)
            s0 = state[:, 2:2 + s_].reshape(b, h, s_, s_)

            def step(s, rkvw):
                r_t, k_t, v_t, w_t = rkvw
                a = k_t[..., :, None] * v_t[..., None, :]
                out = jnp.einsum('bhi,bhij->bhj', r_t, u * a + s)
                s = a + w_t[..., :, None] * s
                return (s, out)
            rkvw = tuple((jnp.moveaxis(t, 1, 0) for t in (r, k, v, w)))
            _, out = jax.lax.scan(step, s0, rkvw)
            out = jnp.moveaxis(out, 0, 1).reshape(b, l, e)
            og = out.reshape(b, l, h, s_)
            m = og.mean(-1, keepdims=True)
            va = ((og - m) ** 2).mean(-1, keepdims=True)
            og = ((og - m) / jnp.sqrt(va + 1e-05)).reshape(b, l, e) * gn_w + gn_b
            x1 = x + og * g @ Wo.T
            xc = _ln(x1, ln2_w, ln2_b)
            sx2 = jnp.concatenate([state[:, 0:1] - xc[:, :1], xc[:, :-1] - xc[:, 1:]], axis=1)
            xk2 = xc + sx2 * ffn_maa_k
            xr2 = xc + sx2 * ffn_maa_r
            rr = jax.nn.sigmoid(xr2 @ Wfr.T)
            kk = jnp.square(jax.nn.relu(xk2 @ Wfk.T))
            return x1 + rr * (kk @ Wfv.T)
        return _block(x, state, ln1_w, ln1_b, ln2_w, ln2_b, maa_x, maa_w1, maa_w2, maa_stack, time_decay, td_w1, td_w2, u, Wr, Wk, Wv, Wg, Wo, gn_w, gn_b, ffn_maa_k, ffn_maa_r, Wfk, Wfr, Wfv)

    def _L3_xattn_ref(hidden_states, audio_kv, audio_attention_mask, Wq, Wk, Wv, Wo, ln_gamma, ln_beta, gate):
        import jax, jax.numpy as jnp
        import numpy as np
        HIDDEN = 512
        HEADS = 16
        HEAD_DIM = HIDDEN // HEADS
        LN_EPS = 1e-05
        GATE_INIT = 0.5

        def _layer_norm(x, gamma, beta):
            mu = jnp.mean(x, axis=-1, keepdims=True)
            var = jnp.mean(jnp.square(x - mu), axis=-1, keepdims=True)
            return (x - mu) * jax.lax.rsqrt(var + LN_EPS) * gamma + beta
        B, Tt, D = hidden_states.shape
        Ta = audio_kv.shape[1]
        scale = HEAD_DIM ** (-0.5)
        a = _layer_norm(audio_kv, ln_gamma, ln_beta)
        Q = (hidden_states @ Wq.T).reshape(B, Tt, HEADS, HEAD_DIM).transpose(0, 2, 1, 3)
        K = (a @ Wk.T).reshape(B, Ta, HEADS, HEAD_DIM).transpose(0, 2, 1, 3)
        V = (a @ Wv.T).reshape(B, Ta, HEADS, HEAD_DIM).transpose(0, 2, 1, 3)
        scores = jnp.einsum('bhtd,bhsd->bhts', Q, K) * scale
        mask = audio_attention_mask[:, None, None, :]
        scores = jnp.where(mask, scores, jnp.float32(-jnp.inf))
        attn = jax.nn.softmax(scores, axis=-1)
        out = jnp.einsum('bhts,bhsd->bhtd', attn, V)
        out = out.transpose(0, 2, 1, 3).reshape(B, Tt, D)
        out = out @ Wo.T
        return hidden_states + jnp.tanh(gate) * out
    x = _L0_xattn_ref(x, ctx_2048, L0_xattn_ln1_w, L0_xattn_ln1_b, L0_xattn_ln2_w, L0_xattn_ln2_b, L0_xattn_maa_x, L0_xattn_maa_w1, L0_xattn_maa_w2, L0_xattn_maa_stack, L0_xattn_time_decay, L0_xattn_decay_w1, L0_xattn_decay_w2, L0_xattn_faaaa, L0_xattn_Wr, L0_xattn_Wk, L0_xattn_Wv, L0_xattn_Wg, L0_xattn_Wo, L0_xattn_gn_w, L0_xattn_gn_b, L0_xattn_ffn_maa_k, L0_xattn_ffn_maa_r, L0_xattn_ffn_Wk, L0_xattn_ffn_Wr, L0_xattn_ffn_Wv, 0)
    x = _L1_xattn_ref(x, ctx_2048, L1_xattn_ln1_w, L1_xattn_ln1_b, L1_xattn_ln2_w, L1_xattn_ln2_b, L1_xattn_maa_x, L1_xattn_maa_w1, L1_xattn_maa_w2, L1_xattn_maa_stack, L1_xattn_time_decay, L1_xattn_td_w1, L1_xattn_td_w2, L1_xattn_u, L1_xattn_Wr, L1_xattn_Wk, L1_xattn_Wv, L1_xattn_Wg, L1_xattn_Wo, L1_xattn_gn_w, L1_xattn_gn_b, L1_xattn_ffn_maa_k, L1_xattn_ffn_maa_r, L1_xattn_Wfk, L1_xattn_Wfr, L1_xattn_Wfv)
    x = _L2_xattn_ref(x, ctx_2048, L2_xattn_ln1_w, L2_xattn_ln1_b, L2_xattn_ln2_w, L2_xattn_ln2_b, L2_xattn_maa_x, L2_xattn_maa_w1, L2_xattn_maa_w2, L2_xattn_maa_stack, L2_xattn_time_decay, L2_xattn_td_w1, L2_xattn_td_w2, L2_xattn_u, L2_xattn_Wr, L2_xattn_Wk, L2_xattn_Wv, L2_xattn_Wg, L2_xattn_Wo, L2_xattn_gn_w, L2_xattn_gn_b, L2_xattn_ffn_maa_k, L2_xattn_ffn_maa_r, L2_xattn_Wfk, L2_xattn_Wfr, L2_xattn_Wfv)
    x = _L3_xattn_ref(x, ctx_2048, mask_BxS2_bf1, L3_xattn_Wq, L3_xattn_Wk, L3_xattn_Wv, L3_xattn_Wo, L3_xattn_ln_gamma, L3_xattn_ln_beta, L3_xattn_gate)
    return x

_drawn_inputs = setup_inputs


def setup_inputs(seed=0):
    import zlib

    import numpy as np

    out = dict(_drawn_inputs(seed))
    spreads = {'L0_xattn_ln1_w': (1.0, 0.2),
     'L0_xattn_ln1_b': (0.0, 0.1),
     'L0_xattn_ln2_w': (1.0, 0.6),
     'L0_xattn_ln2_b': (0.0, 0.8),
     'L0_xattn_gn_w': (1.0, 0.6),
     'L0_xattn_gn_b': (0.0, 0.614),
     'L1_xattn_ln1_w': (1.0, 0.2),
     'L1_xattn_ln1_b': (0.0, 0.275),
     'L1_xattn_ln2_w': (1.0, 0.6),
     'L1_xattn_ln2_b': (0.0, 0.8),
     'L1_xattn_gn_w': (1.0, 0.6),
     'L1_xattn_gn_b': (0.0, 0.692),
     'L2_xattn_ln1_w': (1.0, 0.2),
     'L2_xattn_ln1_b': (0.0, 0.297),
     'L2_xattn_ln2_w': (1.0, 0.6),
     'L2_xattn_ln2_b': (0.0, 0.8),
     'L2_xattn_gn_w': (1.0, 0.6),
     'L2_xattn_gn_b': (0.0, 0.708),
     'L3_xattn_ln_gamma': (1.0, 0.6),
     'L3_xattn_ln_beta': (0.0, 0.8)}
    factors = {'L0_xattn_maa_x': 57.092,
     'L0_xattn_maa_stack': 5.751,
     'L0_xattn_decay_w1': 8.0,
     'L0_xattn_decay_w2': 8.0,
     'L0_xattn_faaaa': 2.71,
     'L0_xattn_ffn_maa_k': 8.0,
     'L0_xattn_ffn_maa_r': 8.0,
     'L0_xattn_ffn_Wr': 3.782,
     'L1_xattn_maa_x': 8.0,
     'L1_xattn_maa_w1': 2.925,
     'L1_xattn_maa_w2': 2.928,
     'L1_xattn_td_w1': 8.0,
     'L1_xattn_td_w2': 8.0,
     'L1_xattn_u': 2.984,
     'L1_xattn_ffn_maa_k': 5.666,
     'L1_xattn_ffn_maa_r': 8.0,
     'L1_xattn_Wfr': 4.075,
     'L2_xattn_maa_x': 8.0,
     'L2_xattn_maa_w1': 3.048,
     'L2_xattn_maa_w2': 3.064,
     'L2_xattn_td_w1': 8.0,
     'L2_xattn_td_w2': 8.0,
     'L2_xattn_u': 3.123,
     'L2_xattn_ffn_maa_k': 5.66,
     'L2_xattn_ffn_maa_r': 8.0,
     'L2_xattn_Wfr': 4.089,
     'L3_xattn_Wq': 8.0,
     'L3_xattn_Wk': 8.0}
    for name, (base, spread) in spreads.items():
        noise = np.random.default_rng([zlib.crc32(name.encode()), seed]).standard_normal(out[name].shape)
        drawn = base * np.exp(spread * noise) if base else spread * noise
        out[name] = jnp.asarray(drawn.astype(out[name].dtype))
    for name, factor in factors.items():
        out[name] = (out[name] * factor).astype(out[name].dtype)
    return out
```

```python
from contextlib import ExitStack

import numpy as np
import concourse.bass as bass
from concourse import mybir

F32 = mybir.dt.float32
U8 = mybir.dt.uint8
ALU = mybir.AluOpType
ACT = mybir.ActivationFunctionType
AX_X = mybir.AxisListType.X

P = 128
LAYERS = 3
B, T, E, H = 4, 512, 512, 32
S = E // H
KT = E // P
CHUNKS = 2
TC = T // CHUNKS
COLS = B * TC
HALF = COLS // 2
HB = B // 2
DM, DD = 32, 64
STREAMS = 5
EPS = 1e-5
JH = 8
STEPS = S + 1

AH = 16
AD = E // AH
SK = 1024
ST = SK // P
TT = T // P
HPT = P // AD
SCALE = AD ** -0.5

LN1W, LN1B, MAAX, MAAS, LN2W, LN2B, FMK, FMR = 0, 4, 8, 12, 32, 36, 40, 44
TDEC, UCOL, GNW, GNB = 48, 64, 80, 96
PARS = 112
W1_AT, W2A_AT, W2B_AT, TD1_AT, TD2_AT, PAR_AT = 0, 640, 1152, 1664, 2176, 2688
SMALL = PAR_AT + PARS
SLOT = KT * E
WK, WV, WR, WG, WO0, WFR, WFK, WFV = 0, 1, 2, 3, 4, 8, 9, 10
NW = 11
NSLOT = 4
SLOT_LOADS = [sum(1 for n in range(NW) if n % NSLOT == s) for s in range(NSLOT)]
ORDER = ["k", "v", "r", "w", "g"]
FAN = {"k": 0, "w": 1, "v": 2, "r": 3, "g": 4}

M_MEAN1, M_MIX, M_ACC, M_WO, M_MEAN2, M_WFV, M_CHUNK = 0, 4, 44, 52, 68, 72, 80
J_VAR1, J_W1, J_PROJ, J_VAR2, J_WFR, J_WFK, J_CHUNK = 0, 2, 6, 50, 52, 60, 68
RING = 4
J_AT = {"k": J_PROJ, "v": J_PROJ + 8, "r": J_PROJ + 16, "td": J_PROJ + 24, "w": J_PROJ + 28, "g": J_PROJ + 36}

CONSTS = 4
AT_CONSTS = 4
JA_VAR, JA_K, JA_Q, JA_ATT, JA_PER = 0, 4, 12, 16, 16 + KT * (1 + HPT * ST)
MA_MEAN, MA_V, MA_MAX, MA_WO, MA_PER = 0, 2, 10, 10 + KT * 2 * TT * HPT, 14 + KT * 2 * TT * HPT


class Count:

    def __init__(self, sem, per, credit=0):
        self.sem, self.per, self.credit, self.n = sem, per, credit, 0

    def inc(self, instruction, by=1):
        self.n += by
        instruction.then_inc(self.sem, by)

    def at(self, turn, n):
        return turn * self.per + (n + self.credit)

    def close(self):
        assert self.n == self.per, (self.sem, self.n, self.per)


def build(nc, a):
    ctx = ExitStack()
    with ctx:
        mem = ctx.enter_context(nc.sbuf_tensor("mem", [P, 49424], F32))
        psum = ctx.enter_context(nc.psum_tensor("psum", [P, 8, 512], F32))

        def sb(name, shape, dt=F32):
            return ctx.enter_context(nc.sbuf_tensor(name, shape, dt))

        def sem(name):
            return ctx.enter_context(nc.semaphore(name))

        def view(at, pattern=None, size=None, **dims):
            v = mem[:, at:at + size]
            return v.rearrange(pattern, **dims) if pattern else v

        x = view(0, "p (k b t) -> p k b t", 4096, k=KT, b=B)
        hm = {s: view(4096 + 4096 * n, "p (i t) -> p i t", 4096, i=S) for n, s in enumerate("krwvg")}
        rr = view(4096 * 2, "p (m c) -> p m c", 4096, m=KT)
        kk = view(4096 * 1, "p (m c) -> p m c", 4096, m=KT)
        th_a = view(4096 * 5, None, COLS)
        th_b = view(4096 * 5 + COLS, None, COLS)
        tdh = view(4096 * 5 + 2 * COLS, None, COLS)
        rstd = view(4096 * 5 + 3 * COLS, None, COLS)
        A = 4096 * 6
        xa = view(A, "p (k b t) -> p k b t", KT * B * (TC + 1), k=KT, b=B)
        A2 = A + KT * B * (TC + 1)
        sx = view(A2, "p (k b t) -> p k b t", 4096, k=KT, b=B)
        mix = [view(A2 + 4096 * (1 + n), "p (k b t) -> p k b t", 4096, k=KT, b=B) for n in range(2)]
        kv = [view(A + 2048 * n, "p (j t) -> p j t", 2048, j=JH) for n in range(4)]
        kr2 = view(A, "p (i t) -> p i t", 4096, i=S)
        s_ext = [view(A + 8192 + 2056 * n, "p (j t) -> p j t", 2056, j=JH) for n in range(2)]
        att = view(A + 12304, "p (j t) -> p j t", 4096, j=S)
        ruk = view(A + 16400, None, TC)
        gd = view(A, "p (j t) -> p j t", 4096, j=S)
        gsq = view(A + 4096, "p (j t) -> p j t", 4096, j=S)
        gsum = view(A + 8192, None, TC)
        gstd = view(A + 8192 + TC, None, TC)
        R = A + 16656
        ring = [view(R + SLOT * n, None, SLOT) for n in range(NSLOT)]

        small = sb("small", [P, SMALL])
        ident = sb("ident", [P, P])
        ones = sb("ones", [P, P])
        eps = sb("eps", [P, 1])
        s_first = sb("s_first", [P, S * S])
        s_now = sb("s_now", [P, S * S])
        rows = sb("rows", [P, 2, KT * B])
        prev = [sb(f"prev{n}", [P, KT * B]) for n in range(2)]
        w1 = small[:, W1_AT:W1_AT + 640].rearrange("p (k f) -> p k f", k=KT)
        w2a = small[:, W2A_AT:W2A_AT + E]
        w2b = small[0:DM, W2B_AT:W2B_AT + E]
        td1 = small[:, TD1_AT:TD1_AT + KT * P].rearrange("p (k f) -> p k f", k=KT)
        td2 = small[:, TD2_AT:TD2_AT + E].rearrange("p (i h) -> p i h", i=S)

        def par(at, n=0):
            return small[:, PAR_AT + at + n:PAR_AT + at + n + 1]

        def bank_m(n):
            return psum[:, n % RING, :]

        def bank_j(n):
            return psum[:, RING + n % RING, :]

        const_ready = sem("const_ready")
        state_loaded = sem("state_loaded")
        small_loaded = sem("small_loaded")
        x_loaded = sem("x_loaded")
        x_stored = sem("x_stored")
        slot_loaded = [sem(f"slot_loaded{n}") for n in range(NSLOT)]
        m_full = Count(sem("m_full"), M_CHUNK, M_CHUNK)
        m_free = Count(sem("m_free"), M_CHUNK, RING)
        j_full = Count(sem("j_full"), J_CHUNK, J_CHUNK)
        j_free = Count(sem("j_free"), J_CHUNK, RING)
        layer_set = sem("layer_set")
        edge_set = Count(sem("edge_set"), 2)
        edge_kept = Count(sem("edge_kept"), 2, 2)
        sq_ready = Count(sem("sq_ready"), 4)
        rstd_ready = Count(sem("rstd_ready"), 4)
        xn_ready = Count(sem("xn_ready"), 4)
        xa_ready = Count(sem("xa_ready"), 4)
        sx_ready = Count(sem("sx_ready"), 4)
        lmix_ready = Count(sem("lmix_ready"), 2)
        mix_ready = Count(sem("mix_ready"), 2 * STREAMS)
        w_ready = Count(sem("w_ready"), 1)
        ruk_step = Count(sem("ruk_step"), 2)
        kv_ready = Count(sem("kv_ready"), 2 * S)
        s_init = Count(sem("s_init"), 2 * S)
        scan_ready = Count(sem("scan_ready"), 2 * S)
        s_saved = Count(sem("s_saved"), 2 * S, 1)
        rs_ready = Count(sem("rs_ready"), 2 * STEPS)
        acc_done = Count(sem("acc_done"), 2 * S)
        gn_step = Count(sem("gn_step"), 5)
        gn_act = Count(sem("gn_act"), 2)
        og_ready = Count(sem("og_ready"), 1)
        fmix_ready = Count(sem("fmix_ready"), 4)
        kk_ready = Count(sem("kk_ready"), 8)
        x_done = Count(sem("x_done"), 1)
        j_end = {s: J_AT["td"] + 4 if s == "w" else J_AT[s] + 8 for s in ORDER}
        used_by = {WK: (j_full, J_AT["k"] + 8), WV: (j_full, J_AT["v"] + 8), WR: (j_full, J_AT["r"] + 8), WG: (j_full, J_AT["g"] + 8),
                   WFR: (j_full, J_WFR + 8), WFK: (j_full, J_WFK + 8), WFV: (m_full, M_WFV + 8)}
        used_by.update({WO0 + m: (m_full, M_WO + 4 * m + 4) for m in range(KT)})

        at_w = [view(SLOT * n, "p (k e) -> p k e", SLOT, k=KT) for n in range(4)]
        Q0 = SLOT * 4
        cx = view(Q0, "p (k s) -> p k s", 4096, k=KT)
        an = view(Q0 + 4096, "p (k s) -> p k s", 4096, k=KT)
        asq = view(Q0 + 8192, "p (k s) -> p k s", 4096, k=KT)
        keys = view(Q0 + 12288, "p (e s) -> p e s", 4096, e=KT)
        vals = view(Q0 + 16384, "p (s e) -> p s e", 4096, s=ST)
        xq = view(Q0 + 20480, "p (k t) -> p k t", 2048, k=KT)
        qs = view(Q0 + 22528, "p (k t) -> p k t", 2048, k=KT)
        probs = [view(Q0 + 24576 + 2048 * n, "p (h t) -> p h t", 2048, h=HPT) for n in range(2)]
        ao = view(Q0 + 28672, "p (k t) -> p k t", 2048, k=KT)
        ay = view(Q0 + 30720, "p (k t) -> p k t", 2048, k=KT)
        Q1 = Q0 + 32768
        mbias = view(Q1, None, SK)
        arstd = view(Q1 + 1536, None, SK)
        mpad = view(Q1 + 2560, "p (t c) -> p t c", 512, t=TT)
        mT = [view(Q1 + 3072 + 512 * n, None, 512) for n in range(2)]
        sel = view(Q1 + 4096, "p (e c) -> p e c", 512, e=KT)
        rden = view(Q1 + 4608, None, 512)
        mx = view(Q1 + 5120, "p (s t h) -> p s t h", 2 * TT * HPT, s=2, t=TT)
        selc = view(Q1 + 5152, None, KT)
        mcol = view(Q1 + 5156, None, ST)
        lnp = view(Q1 + 5164, None, 2 * KT)
        gate = view(Q1 + 5172, None, 2)
        ones_d = view(Q1 + 5174, None, AD)
        mask_u = view(Q1 + 5206, None, SK // 4).bitcast(U8)
        mcol_u = view(Q1 + 5206 + SK // 4, None, ST // 4).bitcast(U8)

        at_loaded = sem("at_loaded")
        cx_loaded = sem("cx_loaded")
        xq_loaded = sem("xq_loaded")
        out_stored = sem("out_stored")
        at_const = sem("at_const")
        gate_ready = sem("gate_ready")
        max_turn = sem("max_turn")
        aj_full = Count(sem("aj_full"), JA_PER)
        aj_free = Count(sem("aj_free"), JA_PER, RING)
        am_full = Count(sem("am_full"), MA_PER)
        am_free = Count(sem("am_free"), MA_PER, 2)
        mask_step = Count(sem("mask_step"), 4)
        asq_ready = Count(sem("asq_ready"), 2)
        arstd_ready = Count(sem("arstd_ready"), 2)
        axn_ready = Count(sem("axn_ready"), 2)
        an_ready = Count(sem("an_ready"), 2)
        mx_ready = Count(sem("mx_ready"), KT)
        mpad_ready = Count(sem("mpad_ready"), KT)
        pv_done = Count(sem("pv_done"), KT * ST, 2)
        den_ready = Count(sem("den_ready"), KT)
        ao_ready = Count(sem("ao_ready"), KT, 1)

        def bank_am(n):
            return psum[:, n % 2, :]

        acc_o = psum[:, 2, :]
        acc_d = psum[:, 3, :]

        def half(t, n):
            return t[:, :, HB * n:HB * n + HB, :]

        def half2(t, n):
            return half(t, n).rearrange("p k b t -> p k (b t)")

        def over(t, n):
            return t.rearrange("p (o c) -> p o c", o=1).broadcast_to((P, n, t.shape[1]))

        block = ctx.enter_context(nc.Block())

        @block.sync
        def _(sp):
            sp.dma_start(s_first[:], a["s_first"]).then_inc(state_loaded, 16)
            sp.dma_start(rows[:].rearrange("p r c -> p (r c)"), a["rows"]).then_inc(state_loaded, 16)
            sp.dma_start(a["xs"], a["x"]).then_inc(x_stored, 16)
            with sp.Fori(0, LAYERS) as layer:
                sp.wait_ge(x_stored, layer * (16 * CHUNKS) + 16)
                sp.dma_start(small[:], a["small"][bass.ds(layer, 1), :, :].rearrange("o p n -> (o p) n")).then_inc(small_loaded, 16)
                with sp.Fori(0, CHUNKS) as chunk:
                    it = sp.snap(layer * CHUNKS + chunk)
                    sp.wait_ge(x_stored, it * 16 + 16)
                    sp.dma_start(x.rearrange("p k b t -> p (k b t)"),
                                 a["xs"][bass.ds(chunk, 1), :, :].rearrange("o p n -> (o p) n")).then_inc(x_loaded, 16)
                    for n in range(NW):
                        before = n - NSLOT if n >= NSLOT else max(m for m in range(NW) if m % NSLOT == n)
                        tiles, end = used_by[before]
                        sp.wait_ge(tiles.sem, tiles.at(it, end if n >= NSLOT else end - tiles.per))
                        sp.dma_start(ring[n % NSLOT], a["big"][bass.ds(layer, 1), n, :, :].rearrange("o p n -> (o p) n")).then_inc(slot_loaded[n % NSLOT], 16)
                    sp.wait_ge(x_done.sem, x_done.at(it, 1))
                    sp.dma_start(a["xs"][bass.ds(chunk, 1), :, :].rearrange("o p n -> (o p) n"),
                                 x.rearrange("p k b t -> p (k b t)")).then_inc(x_stored, 16)
            sp.wait_ge(x_stored, 16 * (LAYERS * CHUNKS + 1))
            for n in range(4):
                sp.dma_start(at_w[n].rearrange("p k e -> p (k e)"), a["at_w"][n]).then_inc(at_loaded, 16)
            sp.dma_start(lnp, a["at_ln"]).then_inc(at_loaded, 16)
            sp.dma_start(gate[:, 0:1], a["gate"]).then_inc(at_loaded, 16)
            sp.sem_inc(out_stored, 16)
            with sp.Fori(0, B) as b:
                sp.wait_ge(out_stored, b * 16 + 16)
                sp.wait_ge(am_free.sem, am_free.at(b, 0))
                sp.dma_start(cx.rearrange("p k s -> p (k s)"), a["ctx"][bass.ds(b, 1), :, :].rearrange("o p n -> (o p) n")).then_inc(cx_loaded, 16)
                sp.dma_start(mask_u, a["mask"][bass.ds(b, 1), :].broadcast_to((P, SK))).then_inc(cx_loaded, 16)
                sp.dma_start(mcol_u, a["mask_col"][bass.ds(b, 1), :, :].rearrange("o p n -> (o p) n")).then_inc(cx_loaded, 16)
                for c in range(CHUNKS):
                    sp.dma_start(xq[:, :, c * TC:(c + 1) * TC],
                                 a["xs"][c].rearrange("p (k b t) -> p k b t", k=KT, b=B)[:, :, bass.ds(b, 1), :].rearrange("p k o t -> p k (o t)")).then_inc(xq_loaded, 16)
                sp.wait_ge(am_free.sem, am_free.at(b, MA_PER))
                sp.dma_start(a["out"][bass.ds(b, 1), :, :].rearrange("o p n -> (o p) n"), ay.rearrange("p k t -> p (k t)")).then_inc(out_stored, 16)
            sp.wait_ge(out_stored, 16 * (B + 1))

        @block.tensor
        def _(pe):
            mm = nc.tensor.matmul
            pe.sem_inc(m_full.sem, m_full.credit)
            pe.sem_inc(j_full.sem, j_full.credit)
            pe.wait_ge(const_ready, CONSTS)
            with pe.Fori(0, LAYERS) as layer:
                with pe.Fori(0, CHUNKS) as chunk:
                    it = pe.snap(layer * CHUNKS + chunk)

                    def tile_m(n):
                        pe.wait_ge(m_free.sem, m_free.at(it, n + 1 - RING))
                        return bank_m(n)

                    def tile_j(n):
                        pe.wait_ge(j_free.sem, j_free.at(it, n + 1 - RING))
                        return bank_j(n)

                    def weight(n):
                        pe.wait_ge(slot_loaded[n % NSLOT], it * (16 * SLOT_LOADS[n % NSLOT]) + 16 * (n // NSLOT + 1))
                        return ring[n % NSLOT]

                    def stats(m0, j0, sq0):
                        for b in range(B):
                            t = tile_m(m0 + b)
                            for k in range(KT):
                                last = mm(t[:, 0:TC], ones[:], x[:, k, b, :], start=k == 0, stop=k == KT - 1)
                            m_full.inc(last)
                        for n in range(2):
                            pe.wait_ge(sq_ready.sem, sq_ready.at(it, sq0 + n + 1))
                            t = tile_j(j0 + n)
                            for k in range(KT):
                                last = mm(t, ones[:], half2(mix[1], n)[:, k, :], start=k == 0, stop=k == KT - 1)
                            j_full.inc(last)

                    pe.wait_ge(x_loaded, it * 16 + 16)
                    stats(M_MEAN1, J_VAR1, 0)
                    pe.wait_ge(small_loaded, layer * 16 + 16)
                    for n in range(2):
                        pe.wait_ge(lmix_ready.sem, lmix_ready.at(it, n + 1))
                        for part, f0, fn in ((0, 0, P), (1, P, DM)):
                            t = tile_j(J_W1 + 2 * n + part)
                            for k in range(KT):
                                last = mm(t[0:fn, :], w1[:, k, f0:f0 + fn], half2(mix[1], n)[:, k, :], start=k == 0, stop=k == KT - 1)
                            j_full.inc(last)

                    def second_factor(q, n, k):
                        f = FAN[ORDER[q]]
                        if q == 0 and k == 0:
                            pe.wait_ge(j_free.sem, j_free.at(it, J_W1 + 2 * n + 2))
                        t = tile_m(M_MIX + 8 * q + 4 * n + k)
                        cols = slice(n * HALF, (n + 1) * HALF)
                        if f < 4:
                            last = mm(t, w2a[DM * f:DM * f + DM, P * k:P * k + P], th_a[DM * f:DM * f + DM, cols], start=True, stop=True)
                        else:
                            last = mm(t, w2b[:, P * k:P * k + P], th_b[0:DM, cols], start=True, stop=True)
                        m_full.inc(last)

                    for n in range(2):
                        for k in range(KT):
                            second_factor(0, n, k)
                    for q, s in enumerate(ORDER):
                        pe.wait_ge(mix_ready.sem, mix_ready.at(it, 2 * q + 2))
                        if s == "w":
                            for b in range(B):
                                t = tile_j(J_AT["td"] + b)
                                for k in range(KT):
                                    last = mm(t[:, 0:TC], td1[:, k, :], mix[q % 2][:, k, b, :], start=k == 0, stop=k == KT - 1)
                                j_full.inc(last)
                        else:
                            w = weight({"k": WK, "v": WV, "r": WR, "g": WG}[s]).rearrange("p (k i h) -> p k i h", k=KT, i=S)
                        for pair in range(S // 2):
                            if q + 1 < STREAMS:
                                second_factor(q + 1, pair // KT, pair % KT)
                            if s == "w" and pair == 0:
                                pe.wait_ge(j_free.sem, j_free.at(it, J_AT["td"] + 4))
                            t = tile_j(J_AT[s] + pair)
                            for o in range(2):
                                i, cols = 2 * pair + o, slice(o * TC, (o + 1) * TC)
                                if s == "w":
                                    for b in range(B):
                                        last = mm(t[H * b:H * b + H, cols], td2[:, i, :], tdh[:, b * TC:(b + 1) * TC], start=True, stop=True)
                                else:
                                    for k in range(KT):
                                        for b in range(B):
                                            last = mm(t[H * b:H * b + H, cols], w[:, k, i, :], mix[q % 2][:, k, b, :], start=k == 0, stop=k == KT - 1,
                                                      skip_group_check=True)
                            j_full.inc(last)

                    for jh in range(2):
                        tile_m(M_ACC + RING * jh + RING - 1)
                        for n in range(STEPS):
                            step = jh * STEPS + n
                            pe.wait_ge(rs_ready.sem, rs_ready.at(it, step + 1))
                            for c in range(RING):
                                last = mm(bank_m(M_ACC + RING * jh + c), ident[:], kv[step % 4][:, 2 * c:2 * c + 2, :], start=n == 0, stop=n == STEPS - 1)
                                if n == STEPS - 1:
                                    m_full.inc(last)
                            if n < STEPS - 1:
                                acc_done.inc(last)

                    pe.wait_ge(og_ready.sem, og_ready.at(it, 1))
                    for m in range(KT):
                        w = weight(WO0 + m).rearrange("p (j e) -> p j e", j=S)
                        tile_m(M_WO + B * m + B - 1)
                        out = [bank_m(M_WO + B * m + b) for b in range(B)]
                        for j in range(S):
                            for b in range(B):
                                last = mm(out[b][:, 0:TC], w[H * b:H * b + H, j, :], att[H * b:H * b + H, j, :], start=j == 0, stop=j == S - 1)
                                if j == S - 1:
                                    m_full.inc(last)

                    pe.wait_ge(m_free.sem, m_free.at(it, M_WO + 16))
                    stats(M_MEAN2, J_VAR2, 2)
                    wr, wk = weight(WFR), weight(WFK)
                    for n, (w, j0) in enumerate(((wr, J_WFR), (wk, J_WFK))):
                        w = w.rearrange("p (k e) -> p k e", k=KT)
                        for c in range(2):
                            pe.wait_ge(fmix_ready.sem, fmix_ready.at(it, 2 * n + c + 1))
                            for m in range(KT):
                                t = tile_j(j0 + KT * c + m)
                                for k in range(KT):
                                    last = mm(t, w[:, k, P * m:P * m + P], half2(mix[n], c)[:, k, :], start=k == 0, stop=k == KT - 1)
                                j_full.inc(last)
                    w = weight(WFV).rearrange("p (k e) -> p k e", k=KT)
                    for c in range(2):
                        pe.wait_ge(kk_ready.sem, kk_ready.at(it, KT * c + KT))
                        for m in range(KT):
                            t = tile_m(M_WFV + KT * c + m)
                            for k in range(KT):
                                last = mm(t, w[:, k, P * m:P * m + P], kk[:, k, c * HALF:(c + 1) * HALF], start=k == 0, stop=k == KT - 1)
                            m_full.inc(last)
                    for c in (m_full, j_full, acc_done):
                        c.close()

            wq, wk, wv, wo = at_w
            pe.wait_ge(at_loaded, 6 * 16)
            pe.wait_ge(at_const, AT_CONSTS)
            with pe.Fori(0, B) as b:
                def tile_am(n):
                    pe.wait_ge(am_free.sem, am_free.at(b, n + 1 - 2))
                    return bank_am(n)

                def tile_aj(n):
                    pe.wait_ge(aj_free.sem, aj_free.at(b, n + 1 - RING))
                    return bank_j(n)

                pe.wait_ge(cx_loaded, b * 48 + 48)
                for sh in range(2):
                    t = tile_am(MA_MEAN + sh)
                    for k in range(KT):
                        last = mm(t, ones[:], cx[:, k, sh * 512:sh * 512 + 512], start=k == 0, stop=k == KT - 1)
                    am_full.inc(last)
                for c in range(4):
                    pe.wait_ge(asq_ready.sem, asq_ready.at(b, c // 2 + 1))
                    t = tile_aj(JA_VAR + c)
                    for k in range(KT):
                        last = mm(t[:, 0:256], ones[:], asq[:, k, c * 256:c * 256 + 256], start=k == 0, stop=k == KT - 1)
                    aj_full.inc(last)
                for sh in range(2):
                    pe.wait_ge(an_ready.sem, an_ready.at(b, sh + 1))
                    for e in range(KT):
                        t = tile_aj(JA_K + KT * sh + e)
                        for k in range(KT):
                            last = mm(t, wk[:, k, P * e:P * e + P], an[:, k, sh * 512:sh * 512 + 512], start=k == 0, stop=k == KT - 1)
                        aj_full.inc(last)
                for st in range(ST):
                    t = tile_am(MA_V + st)
                    for k in range(KT):
                        last = mm(t, an[:, k, P * st:P * st + P], wv[:, k, :], start=k == 0, stop=k == KT - 1)
                    am_full.inc(last)
                pe.wait_ge(xq_loaded, b * (16 * CHUNKS) + 16 * CHUNKS)
                for e in range(KT):
                    t = tile_aj(JA_Q + e)
                    for k in range(KT):
                        last = mm(t, wq[:, k, P * e:P * e + P], xq[:, k, :], start=k == 0, stop=k == KT - 1)
                    aj_full.inc(last)

                def head(h):
                    return slice(AD * h, AD * h + AD)

                def scores_for_max(e, n):
                    tt, sh = n // 2, n % 2
                    for h in range(HPT):
                        t = tile_am(MA_MAX + (e * 2 * TT + n) * HPT + h)
                        am_full.inc(mm(t, qs[head(h), e, P * tt:P * tt + P], keys[head(h), e, sh * 512:sh * 512 + 512], start=True, stop=True))

                def maxima_as_rows(e):
                    pe.wait_ge(mpad_ready.sem, mpad_ready.at(b, e + 1))
                    t = tile_aj(JA_ATT + e * (1 + HPT * ST))
                    for tt in range(TT):
                        last = mm(t[:, P * tt:P * tt + P], mpad[:, tt, :], ident[:], start=True, stop=True, skip_group_check=True)
                    aj_full.inc(last)

                pe.wait_ge(aj_free.sem, aj_free.at(b, JA_Q + KT))
                for n in range(2 * TT):
                    scores_for_max(0, n)
                maxima_as_rows(0)
                for e in range(KT):
                    j0 = JA_ATT + e * (1 + HPT * ST) + 1

                    def scores(st):
                        tile_aj(j0 + HPT * st + HPT - 1)
                        t = [bank_j(j0 + HPT * st + h) for h in range(HPT)]
                        for h in range(HPT):
                            mm(t[h], keys[head(h), e, P * st:P * st + P], qs[head(h), e, :], start=True, stop=False)
                        for h in range(HPT):
                            aj_full.inc(mm(t[h], sel[head(h), e, :], mT[e % 2][head(h), :], start=False, stop=True))

                    def weighted(st):
                        pe.wait_ge(aj_free.sem, aj_free.at(b, j0 + HPT * st + HPT))
                        if st == 0:
                            pe.wait_ge(ao_ready.sem, ao_ready.at(b, e))
                        for h in range(HPT):
                            mm(acc_o[head(h), :], vals[:, st, (HPT * e + h) * AD:(HPT * e + h + 1) * AD], probs[st % 2][:, h, :], start=st == 0, stop=st == ST - 1)
                        for h in range(HPT):
                            last = mm(acc_d[head(h), :], ones_d, probs[st % 2][:, h, :], start=st == 0, stop=st == ST - 1)
                        pv_done.inc(last)

                    if e == 0:
                        pe.wait_ge(am_free.sem, am_free.at(b, MA_V + ST))
                    for st in range(ST):
                        scores(st)
                        if e + 1 < KT:
                            scores_for_max(e + 1, st)
                        if st:
                            weighted(st - 1)
                    weighted(ST - 1)
                    if e + 1 < KT:
                        maxima_as_rows(e + 1)
                pe.wait_ge(ao_ready.sem, ao_ready.at(b, KT))
                for m in range(KT):
                    t = tile_am(MA_WO + m)
                    for k in range(KT):
                        last = mm(t, wo[:, k, P * m:P * m + P], ao[:, k, :], start=k == 0, stop=k == KT - 1)
                    am_full.inc(last)
                for c in (aj_full, am_full, pv_done):
                    c.close()

        @block.scalar
        def _(act):
            f = nc.scalar.activation
            act.sem_inc(j_free.sem, j_free.credit)
            act.sem_inc(edge_kept.sem, edge_kept.credit)
            act.sem_inc(s_saved.sem, s_saved.credit)
            act.wait_ge(state_loaded, 32)
            act.wait_ge(const_ready, CONSTS)
            s_at = s_now[:].rearrange("p (i j) -> p i j", i=S)
            with act.Fori(0, LAYERS) as layer:
                act.wait_ge(small_loaded, layer * 16 + 16)
                f(prev[0][:], rows[:, 1, :], ACT.Copy)
                f(prev[1][:], rows[:, 0, :], ACT.Copy)
                f(s_now[:], s_first[:], ACT.Copy).then_inc(layer_set, 1)
                act.wait_ge(layer_set, layer + 1)
                with act.Fori(0, CHUNKS) as chunk:
                    it = act.snap(layer * CHUNKS + chunk)

                    def full_j(n):
                        act.wait_ge(j_full.sem, j_full.at(it, n + 1))
                        return bank_j(n)

                    def layer_norm(which, m0, j0, lw, lb):
                        for n in range(2):
                            act.wait_ge(m_free.sem, m_free.at(it, m0 + HB * n + HB))
                            sq_ready.inc(f(half2(mix[1], n), half2(mix[0], n), ACT.Square))
                        act.wait_ge(edge_kept.sem, edge_kept.at(it, which - 2 + 1))
                        edge_set.inc(f(xa[:, :, :, 0:1], prev[which][:].rearrange("p (k b o) -> p k b o", k=KT, o=1), ACT.Copy))
                        for n in range(2):
                            t = full_j(j0 + n)
                            j_free.inc(f(rstd[:, n * HALF:(n + 1) * HALF], t, ACT.Sqrt, bias=eps[:]))
                        for n in range(2):
                            act.wait_ge(xn_ready.sem, xn_ready.at(it, 2 * which + n + 1))
                            for k in range(KT):
                                last = f(xa[:, k, HB * n:HB * n + HB, 1:TC + 1], mix[0][:, k, HB * n:HB * n + HB, :], ACT.Identity, scale=par(lw, k), bias=par(lb, k))
                            xa_ready.inc(last)
                        act.wait_ge(xa_ready.sem, xa_ready.at(it, 2 * which + 2))
                        edge_kept.inc(f(prev[which][:].rearrange("p (k b o) -> p k b o", k=KT, o=1), xa[:, :, :, TC:TC + 1], ACT.Copy))

                    layer_norm(0, M_MEAN1, J_VAR1, LN1W, LN1B)
                    for n in range(2):
                        cols = slice(n * HALF, (n + 1) * HALF)
                        t = full_j(J_W1 + 2 * n)
                        j_free.inc(f(th_a[:, cols], t, ACT.Tanh))
                        t = full_j(J_W1 + 2 * n + 1)
                        j_free.inc(f(th_b[0:DM, cols], t[0:DM, :], ACT.Tanh))
                    for s in ORDER:
                        if s == "w":
                            for b in range(B):
                                t = full_j(J_AT["td"] + b)
                                j_free.inc(f(tdh[:, b * TC:(b + 1) * TC], t[:, 0:TC], ACT.Tanh))
                        for pair in range(S // 2):
                            t = full_j(J_AT[s] + pair).rearrange("p (i t) -> p i t", i=2)
                            if s == "w":
                                for o in range(2):
                                    last = f(hm["w"][:, 2 * pair + o, :], t[:, o, :], ACT.Exp, bias=par(TDEC, 2 * pair + o))
                                j_free.inc(last)
                            else:
                                j_free.inc(f(hm[s][:, 2 * pair:2 * pair + 2, :], t, ACT.Silu if s == "g" else ACT.Copy))
                        if s == "w":
                            act.wait_ge(j_free.sem, j_free.at(it, J_AT["w"] + 8))
                            w_ready.inc(f(hm["w"], hm["w"], ACT.Exp, scale=-1.0))

                    def start_state(n):
                        jh, i = n // S, n % S
                        if n >= 2:
                            act.wait_ge(rs_ready.sem, rs_ready.at(it, (n - 2) // S * STEPS + (n - 2) % S + 1))
                        else:
                            act.wait_ge(s_saved.sem, s_saved.at(it, 0))
                            act.wait_ge(mix_ready.sem, mix_ready.at(it, 2 * STREAMS))
                        s_init.inc(f(s_ext[n % 2][:, :, 0:1], s_at[:, i, JH * jh:JH * jh + JH].rearrange("p (j o) -> p j o", o=1), ACT.Copy))

                    start_state(0)
                    start_state(1)
                    for n in range(2 * S):
                        jh, i = n // S, n % S
                        act.wait_ge(scan_ready.sem, scan_ready.at(it, n + 1))
                        s_saved.inc(f(s_at[:, i, JH * jh:JH * jh + JH].rearrange("p (j o) -> p j o", o=1), s_ext[n % 2][:, :, TC:TC + 1], ACT.Copy))
                        if n + 2 < 2 * S:
                            start_state(n + 2)
                    act.wait_ge(gn_step.sem, gn_step.at(it, 2))
                    gn_act.inc(f(gsq, gd, ACT.Square))
                    act.wait_ge(gn_step.sem, gn_step.at(it, 3))
                    gn_act.inc(f(gstd, gsum, ACT.Sqrt, scale=1.0 / S, bias=eps[:]))

                    layer_norm(1, M_MEAN2, J_VAR2, LN2W, LN2B)
                    for j0, buf, fn in ((J_WFR, rr, ACT.Sigmoid), (J_WFK, kk, ACT.Relu)):
                        for c in range(2):
                            for m in range(KT):
                                t = full_j(j0 + KT * c + m)
                                j_free.inc(f(buf[:, m, c * HALF:(c + 1) * HALF], t, fn))
                    for c in (j_free, sq_ready, edge_set, edge_kept, xa_ready, w_ready, s_init, s_saved, gn_act):
                        c.close()

            act.sem_inc(aj_free.sem, aj_free.credit)
            act.wait_ge(at_loaded, 6 * 16)
            f(gate[:, 1:2], gate[:, 0:1], ACT.Tanh).then_inc(gate_ready, 1)
            with act.Fori(0, B) as b:
                def full_aj(n):
                    act.wait_ge(aj_full.sem, aj_full.at(b, n + 1))
                    return bank_j(n)

                for sh in range(2):
                    cols = slice(sh * 512, sh * 512 + 512)
                    act.wait_ge(am_free.sem, am_free.at(b, MA_MEAN + sh + 1))
                    asq_ready.inc(f(asq[:, :, cols], an[:, :, cols], ACT.Square))
                for c in range(4):
                    t = full_aj(JA_VAR + c)
                    aj_free.inc(f(arstd[:, c * 256:c * 256 + 256], t[:, 0:256], ACT.Sqrt, bias=eps[:]))
                for sh in range(2):
                    cols = slice(sh * 512, sh * 512 + 512)
                    act.wait_ge(axn_ready.sem, axn_ready.at(b, sh + 1))
                    for k in range(KT):
                        last = f(an[:, k, cols], an[:, k, cols], ACT.Identity, scale=lnp[:, k:k + 1], bias=lnp[:, KT + k:KT + k + 1])
                    an_ready.inc(last)
                for sh in range(2):
                    for e in range(KT):
                        t = full_aj(JA_K + KT * sh + e)
                        aj_free.inc(f(keys[:, e, sh * 512:sh * 512 + 512], t, ACT.Copy))
                for e in range(KT):
                    t = full_aj(JA_Q + e)
                    aj_free.inc(f(qs[:, e, :], t, ACT.Copy))
                act.wait_ge(mask_step.sem, mask_step.at(b, 4))
                for e in range(KT):
                    j0 = JA_ATT + e * (1 + HPT * ST)
                    t = full_aj(j0)
                    aj_free.inc(f(mT[e % 2], t, ACT.Copy))
                    for st in range(ST):
                        act.wait_ge(pv_done.sem, pv_done.at(b, e * ST + st - 1))
                        for h in range(HPT):
                            t = full_aj(j0 + 1 + HPT * st + h)
                            aj_free.inc(f(probs[st % 2][:, h, :], t, ACT.Exp, scale=SCALE, bias=mcol[:, st:st + 1]))
                for c in (aj_free, asq_ready, an_ready):
                    c.close()

        @block.vector
        def _(dve):
            tt = nc.vector.tensor_tensor
            stt = nc.vector.scalar_tensor_tensor
            nc.vector.memset(ones[:], 1.0 / E).then_inc(const_ready, 1)
            nc.vector.memset(eps[:], EPS).then_inc(const_ready, 1)
            dve.sem_inc(m_free.sem, m_free.credit)
            with dve.Fori(0, LAYERS) as layer:
                with dve.Fori(0, CHUNKS) as chunk:
                    it = dve.snap(layer * CHUNKS + chunk)

                    def full_m(n):
                        dve.wait_ge(m_full.sem, m_full.at(it, n + 1))
                        return bank_m(n)

                    def layer_norm(which, m0, j0):
                        for b in range(B):
                            t = full_m(m0 + b)
                            m_free.inc(tt(mix[0][:, :, b, :], x[:, :, b, :], over(t[:, 0:TC], KT), ALU.subtract))
                        for n in range(2):
                            r = rstd[:, n * HALF:(n + 1) * HALF]
                            dve.wait_ge(j_free.sem, j_free.at(it, j0 + n + 1))
                            rstd_ready.inc(nc.vector.reciprocal(r, r))
                        for n in range(2):
                            dve.wait_ge(rstd_ready.sem, rstd_ready.at(it, 2 * which + n + 1))
                            xn_ready.inc(tt(half2(mix[0], n), half2(mix[0], n), over(rstd[:, n * HALF:(n + 1) * HALF], KT), ALU.mult))
                        for n in range(2):
                            dve.wait_ge(xa_ready.sem, xa_ready.at(it, 2 * which + n + 1))
                            h = xa[:, :, HB * n:HB * n + HB, :]
                            sx_ready.inc(tt(half(sx, n), h[:, :, :, 0:TC], h[:, :, :, 1:TC + 1], ALU.subtract))

                    def shifted_mix(to, which, n, at):
                        dve.wait_ge(sx_ready.sem, sx_ready.at(it, 2 * which + n + 1))
                        for k in range(KT):
                            last = stt(half(to, n)[:, k], half(sx, n)[:, k], par(at, k), half(xa, n)[:, k, :, 1:TC + 1], ALU.mult, ALU.add)
                        return last

                    layer_norm(0, M_MEAN1, J_VAR1)
                    dve.wait_ge(small_loaded, layer * 16 + 16)
                    for n in range(2):
                        lmix_ready.inc(shifted_mix(mix[1], 0, n, MAAX))
                    for q, s in enumerate(ORDER):
                        if q >= 2:
                            dve.wait_ge(j_full.sem, j_full.at(it, j_end[ORDER[q - 2]]))
                        for n in range(2):
                            for k in range(KT):
                                t = full_m(M_MIX + 8 * q + 4 * n + k)
                                m_free.inc(stt(half2(mix[q % 2], n)[:, k, :], t, par(MAAS, KT * FAN[s] + k), half2(sx, n)[:, k, :], ALU.add, ALU.mult))
                    dve.wait_ge(j_free.sem, j_free.at(it, J_AT["r"] + 8))
                    dve.wait_ge(mix_ready.sem, mix_ready.at(it, 2 * STREAMS))
                    for i in range(S):
                        last = stt(kr2[:, i, :], hm["k"][:, i, :], par(UCOL, i), hm["r"][:, i, :], ALU.mult, ALU.mult)
                    ruk_step.inc(last)
                    dve.wait_ge(ruk_step.sem, ruk_step.at(it, 1))
                    ruk_step.inc(nc.vector.tensor_reduce(ruk, kr2.rearrange("p i t -> p t i"), AX_X, ALU.add))
                    dve.wait_ge(ruk_step.sem, ruk_step.at(it, 2))

                    def outer(step):
                        jh, i = step // STEPS, step % STEPS
                        if step >= 4:
                            jb, ib = (step - 4) // STEPS, (step - 4) % STEPS
                            if ib == S:
                                dve.wait_ge(m_full.sem, m_full.at(it, M_ACC + RING * jb + RING))
                            else:
                                dve.wait_ge(acc_done.sem, acc_done.at(it, jb * S + ib + 1))
                        vj = hm["v"][:, JH * jh:JH * jh + JH, :]
                        if i == S:
                            rs_ready.inc(tt(kv[step % 4], vj, over(ruk, JH), ALU.mult))
                        else:
                            kv_ready.inc(tt(kv[step % 4], vj, over(hm["k"][:, i, :], JH), ALU.mult))

                    def scans(step):
                        jh, i = step // STEPS, step % STEPS
                        n = jh * S + i
                        dve.wait_ge(kv_ready.sem, kv_ready.at(it, n + 1))
                        dve.wait_ge(s_init.sem, s_init.at(it, n + 1))
                        for j in range(JH):
                            last = nc.vector.tensor_tensor_scan(s_ext[n % 2][:, j, 1:TC + 1], hm["w"][:, i, :], kv[step % 4][:, j, :],
                                                                s_ext[n % 2][:, j, 0:1], ALU.mult, ALU.add)
                        scan_ready.inc(last)

                    def weighted(step):
                        jh, i = step // STEPS, step % STEPS
                        n = jh * S + i
                        dve.wait_ge(scan_ready.sem, scan_ready.at(it, n + 1))
                        rs_ready.inc(tt(kv[step % 4], s_ext[n % 2][:, :, 0:TC], over(hm["r"][:, i, :], JH), ALU.mult))

                    def collect(jh):
                        for c in range(RING):
                            t = full_m(M_ACC + RING * jh + c)
                            m_free.inc(nc.vector.tensor_copy(att[:, JH * jh + 2 * c:JH * jh + 2 * c + 2, :].rearrange("p j t -> p (j t)"), t))

                    dve.wait_ge(w_ready.sem, w_ready.at(it, 1))
                    dve.wait_ge(j_free.sem, j_free.at(it, J_AT["g"] + 8))
                    regular = [step for step in range(2 * STEPS) if step % STEPS < S]
                    outer(0)
                    for n, step in enumerate(regular):
                        if step % STEPS != S - 1:
                            outer(step + 1)
                        scans(step)
                        if n and step % STEPS:
                            weighted(step - 1)
                        if step % STEPS == S - 1:
                            weighted(step)
                            outer(step + 1)
                            if n + 1 < len(regular):
                                outer(step + 2)
                        if step == STEPS + 1:
                            collect(0)
                    collect(1)

                    dve.wait_ge(m_free.sem, m_free.at(it, M_ACC + 2 * RING))
                    gn_step.inc(nc.vector.tensor_reduce(gsum, att.rearrange("p j t -> p t j"), AX_X, ALU.add))
                    dve.wait_ge(gn_step.sem, gn_step.at(it, 1))
                    gn_step.inc(stt(gd, over(gsum, S), -1.0 / S, att, ALU.mult, ALU.add))
                    dve.wait_ge(gn_act.sem, gn_act.at(it, 1))
                    gn_step.inc(nc.vector.tensor_reduce(gsum, gsq.rearrange("p j t -> p t j"), AX_X, ALU.add))
                    dve.wait_ge(gn_act.sem, gn_act.at(it, 2))
                    gn_step.inc(nc.vector.reciprocal(gstd, gstd))
                    dve.wait_ge(gn_step.sem, gn_step.at(it, 4))
                    for j in range(S):
                        last = stt(gd[:, j, :], gd[:, j, :], par(GNW, j), gstd, ALU.mult, ALU.mult)
                    gn_step.inc(last)
                    dve.wait_ge(gn_step.sem, gn_step.at(it, 5))
                    for j in range(S):
                        last = stt(att[:, j, :], gd[:, j, :], par(GNB, j), hm["g"][:, j, :], ALU.add, ALU.mult)
                    og_ready.inc(last)
                    for m in range(KT):
                        for b in range(B):
                            t = full_m(M_WO + B * m + b)
                            m_free.inc(tt(x[:, m, b, :], x[:, m, b, :], t[:, 0:TC], ALU.add))

                    layer_norm(1, M_MEAN2, J_VAR2)
                    for to, at in ((mix[0], FMR), (mix[1], FMK)):
                        for n in range(2):
                            fmix_ready.inc(shifted_mix(to, 1, n, at))
                    for c in range(2):
                        for m in range(KT):
                            t = full_m(M_WFV + KT * c + m)
                            r = rr[:, m, c * HALF:(c + 1) * HALF]
                            m_free.inc(tt(r, r, t, ALU.mult))
                        for m in range(KT):
                            dve.wait_ge(m_free.sem, m_free.at(it, M_WFV + KT * c + m + 1))
                            xc = half2(x, c)[:, m, :]
                            last = tt(xc, xc, rr[:, m, c * HALF:(c + 1) * HALF], ALU.add)
                    x_done.inc(last)
                    for c in (m_free, rstd_ready, xn_ready, sx_ready, lmix_ready, ruk_step, kv_ready, scan_ready, rs_ready, gn_step, og_ready, fmix_ready, x_done):
                        c.close()

            dve.sem_inc(am_free.sem, am_free.credit)
            dve.sem_inc(pv_done.sem, pv_done.credit)
            dve.sem_inc(ao_ready.sem, ao_ready.credit)
            dve.wait_ge(x_stored, 16 * (LAYERS * CHUNKS + 1))
            nc.vector.memset(mpad, 0.0).then_inc(at_const, 1)
            nc.vector.memset(ones_d, 1.0).then_inc(at_const, 1)
            nc.vector.tensor_reduce(selc, ident[:].rearrange("p (h c) -> p c h", h=HPT)[:, 0:KT, :], AX_X, ALU.add).then_inc(at_const, 1)
            dve.wait_ge(at_const, 3)
            nc.vector.tensor_scalar(sel, selc.rearrange("p (e o) -> p e o", o=1).broadcast_to((P, KT, P)), -1.0, None, ALU.mult).then_inc(at_const, 1)
            dve.wait_ge(gate_ready, 1)
            with dve.Fori(0, B) as b:
                def full_am(n):
                    dve.wait_ge(am_full.sem, am_full.at(b, n + 1))
                    return bank_am(n)

                dve.wait_ge(cx_loaded, b * 48 + 48)
                mask_step.inc(nc.vector.tensor_scalar(mbias, mask_u, -1.0, 3e38, ALU.add, ALU.mult))
                mask_step.inc(nc.vector.tensor_scalar(mcol, mcol_u, -1.0, 3e38, ALU.add, ALU.mult))
                dve.wait_ge(mask_step.sem, mask_step.at(b, 2))
                mask_step.inc(nc.vector.tensor_scalar(mbias, mbias, 10.0, None, ALU.mult))
                mask_step.inc(nc.vector.tensor_scalar(mcol, mcol, 10.0, None, ALU.mult))
                for sh in range(2):
                    cols = slice(sh * 512, sh * 512 + 512)
                    t = full_am(MA_MEAN + sh)
                    am_free.inc(tt(an[:, :, cols], cx[:, :, cols], over(t, KT), ALU.subtract))
                for sh in range(2):
                    cols = slice(sh * 512, sh * 512 + 512)
                    dve.wait_ge(aj_free.sem, aj_free.at(b, JA_VAR + 2 * sh + 2))
                    arstd_ready.inc(nc.vector.reciprocal(arstd[:, cols], arstd[:, cols]))
                for sh in range(2):
                    cols = slice(sh * 512, sh * 512 + 512)
                    dve.wait_ge(arstd_ready.sem, arstd_ready.at(b, sh + 1))
                    axn_ready.inc(tt(an[:, :, cols], an[:, :, cols], over(arstd[:, cols], KT), ALU.mult))
                for st in range(ST):
                    t = full_am(MA_V + st)
                    am_free.inc(nc.vector.tensor_copy(vals[:, st, :], t))

                def maxima(e):
                    for n in range(2 * TT):
                        for h in range(HPT):
                            t = full_am(MA_MAX + (e * 2 * TT + n) * HPT + h)
                            dve.sem_inc(max_turn, 1)
                            am_free.inc(nc.vector.tensor_tensor_reduce(t, t, mbias[:, (n % 2) * 512:(n % 2) * 512 + 512], 1.0, -3.4e38, ALU.add, ALU.max,
                                                                       accum_out=mx[:, n % 2, n // 2, h:h + 1]))
                    dve.wait_ge(am_free.sem, am_free.at(b, MA_MAX + (e + 1) * 2 * TT * HPT))
                    if e:
                        dve.wait_ge(aj_full.sem, aj_full.at(b, JA_ATT + (e - 1) * (1 + HPT * ST) + 1))
                    mpad_ready.inc(tt(mpad.rearrange("p t (h c) -> p t h c", h=HPT)[:, :, :, e], mx[:, 0], mx[:, 1], ALU.max))

                dve.wait_ge(mask_step.sem, mask_step.at(b, 4))
                maxima(0)
                for e in range(KT):
                    if e + 1 < KT:
                        maxima(e + 1)
                    dve.wait_ge(pv_done.sem, pv_done.at(b, e * ST + ST))
                    den_ready.inc(nc.vector.reciprocal(rden, acc_d))
                    dve.wait_ge(den_ready.sem, den_ready.at(b, e + 1))
                    ao_ready.inc(tt(ao[:, e, :], acc_o, rden, ALU.mult))
                for m in range(KT):
                    t = full_am(MA_WO + m)
                    am_free.inc(stt(ay[:, m, :], t, gate[:, 1:2], xq[:, m, :], ALU.mult, ALU.add))
                for c in (am_free, mask_step, arstd_ready, axn_ready, mpad_ready, den_ready, ao_ready):
                    c.close()

        @block.gpsimd
        def _(pool):
            nc.gpsimd.memset(ident[:], 0.0).then_inc(const_ready, 1)
            pool.wait_ge(const_ready, 3)
            nc.gpsimd.affine_select(out=ident[:], in_=ident[:], compare_op=ALU.not_equal, fill=1.0, base=0, pattern=[[-1, P]], channel_multiplier=1).then_inc(const_ready, 1)
            with pool.Fori(0, LAYERS) as layer:
                with pool.Fori(0, CHUNKS) as chunk:
                    it = pool.snap(layer * CHUNKS + chunk)
                    for q in range(STREAMS):
                        for n in range(2):
                            pool.wait_ge(m_free.sem, m_free.at(it, M_MIX + 8 * q + 4 * n + 4))
                            mix_ready.inc(nc.gpsimd.tensor_tensor(half(mix[q % 2], n), half(mix[q % 2], n), half(xa, n)[:, :, :, 1:TC + 1], ALU.add))
                    for c in range(2):
                        for m in range(KT):
                            pool.wait_ge(j_free.sem, j_free.at(it, J_WFK + KT * c + m + 1))
                            t = kk[:, m, c * HALF:(c + 1) * HALF]
                            kk_ready.inc(nc.gpsimd.tensor_tensor(t, t, t, ALU.mult))
                    for c in (mix_ready, kk_ready):
                        c.close()


def kernel(**inputs):
    import concourse.bacc as bacc
    from concourse.bass_utils import run_bass_kernel_spmd

    def arr(name):
        return np.asarray(inputs[name])

    def cols(v):
        return np.reshape(v, (KT, P)).T

    def per_head(v):
        return np.tile(np.reshape(v, (H, S)), (B, 1))

    def channel_major(wt):
        n = wt.shape[1]
        return wt.reshape(KT, P, n).transpose(1, 0, 2).reshape(P, KT * n)

    def by_position(wt):
        return wt.reshape(wt.shape[0], H, S).transpose(0, 2, 1).reshape(wt.shape[0], E)

    names = [dict(td1="decay_w1", td2="decay_w2", u="faaaa", fk="ffn_Wk", fr="ffn_Wr", fv="ffn_Wv")] + 2 * [dict(td1="td_w1", td2="td_w2", u="u", fk="Wfk", fr="Wfr", fv="Wfv")]
    small, big = [], []
    for n, name in enumerate(names):
        def p(key):
            return arr(f"L{n}_xattn_{name.get(key, key)}")

        stack = p("maa_stack").reshape(STREAMS, E)
        w2 = p("maa_w2")
        pars = [cols(p("ln1_w")), cols(p("ln1_b")), cols(p("maa_x"))] + [cols(stack[s]) for s in range(STREAMS)]
        pars += [cols(p("ln2_w")), cols(p("ln2_b")), cols(p("ffn_maa_k")), cols(p("ffn_maa_r"))]
        pars += [per_head(p("time_decay")), per_head(p("u").reshape(E)), per_head(p("gn_w")), per_head(p("gn_b"))]
        pad = np.zeros
        small.append(np.concatenate([
            channel_major(p("maa_w1")), w2[:4].reshape(P, E), np.concatenate([w2[4], pad((P - DM, E), w2.dtype)]),
            channel_major(np.concatenate([p("td1"), pad((E, P - DD), w2.dtype)], axis=1)), np.concatenate([by_position(p("td2")), pad((P - DD, E), w2.dtype)]), *pars], axis=1))
        wo = p("Wo").T.reshape(H, S, KT, P)
        big.append(np.stack(
            [channel_major(by_position(p(w).T)) for w in ("Wk", "Wv", "Wr", "Wg")]
            + [np.tile(wo[:, :, m, :].reshape(H, S * P), (B, 1)) for m in range(KT)]
            + [channel_major(p(w).T) for w in ("fr", "fk", "fv")]))
    x = arr("x")
    context = arr("ctx_2048")
    mask = arr("mask_BxS2_bf1").view(np.uint8)
    arrays = {
        "x": x.reshape(B, CHUNKS, TC, KT, P).transpose(1, 4, 3, 0, 2).reshape(CHUNKS, P, KT * COLS),
        "rows": context[:, 0:2].reshape(B, 2, KT, P).transpose(3, 1, 2, 0).reshape(P, 2 * KT * B),
        "s_first": context[:, 2:2 + S].reshape(B * H, S * S),
        "small": np.stack(small),
        "big": np.stack(big),
        "ctx": context.transpose(0, 2, 1).reshape(B, KT, P, SK).transpose(0, 2, 1, 3).reshape(B, P, KT * SK),
        "mask": mask,
        "mask_col": mask.reshape(B, ST, P).transpose(0, 2, 1),
        "at_w": np.stack([channel_major(arr(f"L3_xattn_{w}").T) for w in ("Wq", "Wk", "Wv", "Wo")]),
        "at_ln": np.concatenate([cols(arr("L3_xattn_ln_gamma")), cols(arr("L3_xattn_ln_beta"))], axis=1),
        "gate": np.tile(arr("L3_xattn_gate").reshape(1, 1), (P, 1)),
    }
    arrays = {k: np.ascontiguousarray(v) for k, v in arrays.items()}
    nc = bacc.Bacc("TRN2", target_bir_lowering=False, num_devices=1)
    aps = {k: nc.dram_tensor(f"{k}_dram", v.shape, mybir.dt.from_np(v.dtype), kind="ExternalInput").ap() for k, v in arrays.items()}
    aps["xs"] = nc.dram_tensor("xs_dram", (CHUNKS, P, KT * COLS), F32).ap()
    aps["out"] = nc.dram_tensor("out_dram", (B, P, KT * T), F32, kind="ExternalOutput").ap()
    build(nc, aps)
    r = run_bass_kernel_spmd(nc, [{f"{k}_dram": v for k, v in arrays.items()}], core_ids=[0])
    out = r.results[0]["out_dram"]
    return np.ascontiguousarray(out.reshape(B, P, KT, T).transpose(0, 3, 2, 1).reshape(B, T, E))
```

```python
from contextlib import ExitStack

import numpy as np
import concourse.bass as bass
from concourse import mybir

F32 = mybir.dt.float32
U8 = mybir.dt.uint8
ALU = mybir.AluOpType
ACT = mybir.ActivationFunctionType
AX_X = mybir.AxisListType.X

P = 128
LAYERS = 3
B, T, E, H = 4, 512, 512, 32
S = E // H
KT = E // P
CHUNKS = 2
TC = T // CHUNKS
COLS = B * TC
HALF = COLS // 2
HB = B // 2
DM, DD = 32, 64
STREAMS = 5
EPS = 1e-5
JH = 8
STEPS = S + 1

AH = 16
AD = E // AH
SK = 1024
ST = SK // P
TT = T // P
HPT = P // AD
SCALE = AD ** -0.5
SQ = SK // 4

LN1W, LN1B, MAAX, MAAS, LN2W, LN2B, FMK, FMR = 0, 4, 8, 12, 32, 36, 40, 44
TDEC, UCOL, GNW, GNB = 48, 64, 80, 96
PARS = 112
W1_AT, W2_AT, TD1_AT, TD2_AT, SMALL = 0, 640, 3200, 3712, 4224
SLOT = KT * E
WK, WV, WR, WG, WO, WFR, WFK, WFV = range(8)
NW = 8
NSLOT = 2
SLOT_LOADS = NW // NSLOT
ORDER = ["k", "v", "r", "w", "g"]
FAN = {"k": 0, "w": 1, "v": 2, "r": 3, "g": 4}

M_MEAN1, M_RSTD1, M_MIX, M_ACC, M_WO, M_MEAN2, M_RSTD2, M_WFV, M_CHUNK = 0, 4, 6, 46, 54, 62, 66, 68, 76
J_VAR1, J_W1, J_PROJ, J_VAR2, J_WFR, J_WFK, J_CHUNK = 0, 1, 5, 49, 50, 58, 66
RING = 4
GQ = 4
J_AT = {"k": J_PROJ, "v": J_PROJ + 8, "r": J_PROJ + 16, "td": J_PROJ + 24, "w": J_PROJ + 28, "g": J_PROJ + 36}

CONSTS = 6
X_STORED = 16 * (1 + 2 * LAYERS * CHUNKS)
AT_CONSTS = 1
UNITS = KT * TT
A_Q, A_VAR, A_K, A_T, A_PER = 0, 4, 5, 13, 13 + HPT * UNITS
D_MEAN, D_RSTD, D_V, D_UNIT, D_WO, D_PER = 0, 2, 4, 12, 12 + (HPT + 1) * UNITS, 16 + (HPT + 1) * UNITS
A_HEAD = HPT * UNITS


class Count:

    def __init__(self, sem, per, credit=0):
        self.sem, self.per, self.credit, self.n = sem, per, credit, 0

    def inc(self, instruction, by=1):
        self.n += by
        instruction.then_inc(self.sem, by)

    def at(self, turn, n):
        return turn * self.per + (n + self.credit)

    def close(self):
        assert self.n == self.per, (self.sem, self.n, self.per)


def build(nc, a):
    ctx = ExitStack()
    with ctx:
        mem = ctx.enter_context(nc.sbuf_tensor("mem", [P, 47416], F32))
        psum = ctx.enter_context(nc.psum_tensor("psum", [P, 8, 512], F32))

        def sb(name, shape, dt=F32):
            return ctx.enter_context(nc.sbuf_tensor(name, shape, dt))

        def sem(name):
            return ctx.enter_context(nc.semaphore(name))

        def view(at, pattern=None, size=None, **dims):
            v = mem[:, at:at + size]
            return v.rearrange(pattern, **dims) if pattern else v

        x = view(0, "p (k b t) -> p k b t", 4096, k=KT, b=B)
        hm = {s: view(4096 + 4096 * n, "p (i t) -> p i t", 4096, i=S) for n, s in enumerate("krwvg")}
        rr = view(4096 * 2, "p (m c) -> p m c", 4096, m=KT)
        x_new = view(4096 * 2, "p (k b t) -> p k b t", 4096, k=KT, b=B)
        kk = view(4096 * 1, "p (m c) -> p m c", 4096, m=KT)
        th_a = view(4096 * 5, None, COLS)
        th_b = view(4096 * 5 + COLS, None, COLS)
        tdh = view(4096 * 5 + 2 * COLS, None, COLS)
        std = view(4096 * 5 + 3 * COLS, None, TC)
        A = 4096 * 6
        xa = view(A, "p (k b t) -> p k b t", KT * B * (TC + 1), k=KT, b=B)
        sx = view(A + 4112, "p (k b t) -> p k b t", 4096, k=KT, b=B)
        mix = [view(A + at, "p (k b t) -> p k b t", 4096, k=KT, b=B) for at in (12336, 8224)]
        ROW = JH * (TC + 1)
        kv_flat = [view(A + ROW * n, None, ROW) for n in range(4)]
        s_flat = view(A + 8224, None, ROW)
        wt_flat = [view(A + at, None, ROW) for at in (10280, 16688)]
        kv = [t.rearrange("p (j t) -> p j t", j=JH) for t in kv_flat]
        s_ext = s_flat.rearrange("p (j t) -> p j t", j=JH)
        wt = [t.rearrange("p (j t) -> p j t", j=JH) for t in wt_flat]
        kr2 = view(A + 8224, "p (i t) -> p i t", 4096, i=S)
        ruk = view(A + 16432, None, TC)
        att = hm["v"]
        gd = view(A, "p (j t) -> p j t", 4096, j=S)
        gsq = view(A + 4096, "p (j t) -> p j t", 4096, j=S)
        ogc = view(A + 4096, "p (k b t) -> p k b t", 4096, k=KT, b=B)
        gsum = view(A + 12336, None, TC)
        gstd = view(A + 12336 + TC, None, TC)
        R = A + 18744
        ring = [view(R + SLOT * n, None, SLOT) for n in range(NSLOT)]

        small = sb("small", [P, SMALL])
        pars = sb("pars", [P, PARS])
        ident = sb("ident", [P, P])
        ones = sb("ones", [P, P])
        pick = sb("pick", [P, B, P])
        eps = sb("eps", [P, 1])
        s_first = sb("s_first", [P, S * S])
        s_now = sb("s_now", [P, S * S])
        rows = sb("rows", [P, 2, KT * B])
        prev = [sb(f"prev{n}", [P, KT * B]) for n in range(2)]
        w1 = small[:, W1_AT:W1_AT + 640].rearrange("p (k f) -> p k f", k=KT)
        w2 = small[:, W2_AT:W2_AT + STREAMS * E].rearrange("p (f e) -> p f e", f=STREAMS)
        td1 = small[:, TD1_AT:TD1_AT + KT * P].rearrange("p (k f) -> p k f", k=KT)
        td2 = small[:, TD2_AT:TD2_AT + E].rearrange("p (i h) -> p i h", i=S)

        def par(at, n=0):
            return pars[:, at + n:at + n + 1]

        def bank_m(n):
            return psum[:, n % RING, :]

        def bank_j(n):
            return psum[:, RING + n % RING, :]

        const_ready = sem("const_ready")
        state_loaded = sem("state_loaded")
        small_loaded = sem("small_loaded")
        pars_loaded = sem("pars_loaded")
        x_loaded = [sem(f"x_loaded{n}") for n in range(2)]
        og_stored = sem("og_stored")
        og_loaded = [sem(f"og_loaded{n}") for n in range(2)]
        x_stored = sem("x_stored")
        slot_loaded = [sem(f"slot_loaded{n}") for n in range(NSLOT)]
        m_full = Count(sem("m_full"), M_CHUNK, M_CHUNK)
        m_free = Count(sem("m_free"), M_CHUNK, RING)
        j_full = Count(sem("j_full"), J_CHUNK, J_CHUNK)
        j_free = Count(sem("j_free"), J_CHUNK, RING)
        layer_set = sem("layer_set")
        edge_set = Count(sem("edge_set"), 2)
        edge_kept = Count(sem("edge_kept"), 2, 2)
        sq_ready = Count(sem("sq_ready"), 4)
        rstd_ready = Count(sem("rstd_ready"), 2)
        xn_ready = Count(sem("xn_ready"), 4)
        xa_ready = Count(sem("xa_ready"), 4)
        sx_ready = Count(sem("sx_ready"), 4)
        lmix_ready = Count(sem("lmix_ready"), 2)
        mix_ready = Count(sem("mix_ready"), 2 * STREAMS)
        w_ready = Count(sem("w_ready"), 1)
        ruk_step = Count(sem("ruk_step"), 3)
        kv_ready = Count(sem("kv_ready"), 2 * S)
        scan_set = Count(sem("scan_set"), 2 * S)
        scan_ready = Count(sem("scan_ready"), 2 * S)
        s_saved = Count(sem("s_saved"), 2 * S, 1)
        rs_ready = Count(sem("rs_ready"), 2 * STEPS)
        acc_done = Count(sem("acc_done"), 2 * S)
        gn_step = Count(sem("gn_step"), 4 + GQ)
        gn_act = Count(sem("gn_act"), 2 + GQ)
        og_ready = Count(sem("og_ready"), GQ)
        fmix_ready = Count(sem("fmix_ready"), 4)
        kk_ready = Count(sem("kk_ready"), 8)
        x_done = Count(sem("x_done"), 2)
        j_end = {s: J_AT["td"] + 4 if s == "w" else J_AT[s] + 8 for s in ORDER}
        used_by = [(j_full, J_AT["k"] + 8), (j_full, J_AT["v"] + 8), (j_full, J_AT["r"] + 8), (j_full, J_AT["g"] + 8),
                   (m_full, M_WO + 8), (j_full, J_WFR + 8), (j_full, J_WFK + 8), (m_full, M_WFV + 8)]

        at_w = [view(SLOT * n, "p (k e) -> p k e", SLOT, k=KT) for n in range(4)]
        Q0 = SLOT * 4
        an = view(Q0, "p (k s) -> p k s", 4096, k=KT)
        keys = view(Q0 + 4096, "p (e s) -> p e s", 4096, e=KT)
        vals = view(Q0 + 8192, "p (s e) -> p s e", 4096, s=ST)
        qz = view(Q0 + 12288, "p (h t) -> p h t", 8192, h=AH)
        probs = [view(Q0 + 20480 + 4096 * n, "p (h s) -> p h s", 4096, h=HPT) for n in range(2)]
        asq = view(Q0 + 20480, "p (k s) -> p k s", 4096, k=KT)
        probs_t = view(Q0 + 28672, "p (s h t) -> p s h t", 4096, s=ST, h=HPT)
        ay = view(Q0 + 32768, "p (k t) -> p k t", 2048, k=KT)
        Q1 = Q0 + 34816
        mbias = view(Q1, None, SK)
        diag = view(Q1 + 1024, "p (h t) -> p h t", HPT * P, h=HPT)
        astd = view(Q1 + 1536, None, SQ)
        mask_u = view(Q1 + 1792, None, SK // 4).bitcast(U8)
        mx = view(Q1 + 2048, "p (n h) -> p n h", 2 * HPT, n=2)
        nmx = view(Q1 + 2056, "p (n h) -> p n h", 2 * HPT, n=2)
        den = view(Q1 + 2064, "p (n h) -> p n h", 2 * HPT, n=2)
        rden = view(Q1 + 2072, None, HPT)
        lnp = view(Q1 + 2076, None, 2 * KT)
        gate = view(Q1 + 2084, None, 2)
        xq = small[:, 0:2048].rearrange("p (k t) -> p k t", k=KT)
        ao = small[:, 2048:4096].rearrange("p (k t) -> p k t", k=KT)

        at_loaded = sem("at_loaded")
        cx_loaded = sem("cx_loaded")
        xq_loaded = sem("xq_loaded")
        ay_loaded = sem("ay_loaded")
        out_stored = sem("out_stored")
        at_const = sem("at_const")
        gate_ready = sem("gate_ready")
        max_turn = sem("max_turn")
        a_full = Count(sem("a_full"), A_PER)
        a_free = Count(sem("a_free"), A_PER, 2)
        d_full = Count(sem("d_full"), D_PER)
        d_free = Count(sem("d_free"), D_PER, 2)
        s_full = Count(sem("s_full"), A_HEAD)
        s_free = Count(sem("s_free"), A_HEAD, 2)
        mask_step = Count(sem("mask_step"), 2)
        asq_ready = Count(sem("asq_ready"), 2)
        arstd_ready = Count(sem("arstd_ready"), 1)
        axn_ready = Count(sem("axn_ready"), 2)
        an_ready = Count(sem("an_ready"), 2)
        mx_ready = Count(sem("mx_ready"), A_HEAD)
        nmx_ready = Count(sem("nmx_ready"), A_HEAD)
        den_ready = Count(sem("den_ready"), UNITS)
        diag_ready = Count(sem("diag_ready"), UNITS)

        def bank_a(n):
            return psum[:, 4 + n % 2, :]

        def bank_d(n):
            return psum[:, 6 + n % 2, :]

        def banks_s(n):
            return psum[:, 2 * (n % 2):2 * (n % 2) + 2, :]

        def d_head(u, h):
            return D_UNIT + (HPT + 1) * u + h

        def half(t, n):
            return t[:, :, HB * n:HB * n + HB, :]

        def half2(t, n):
            return half(t, n).rearrange("p k b t -> p k (b t)")

        def over(t, n):
            return t.rearrange("p (o c) -> p o c", o=1).broadcast_to((P, n, t.shape[1]))

        def kv_free(engine, it, step):
            if step >= 4:
                jh, n = (step - 4) // STEPS, (step - 4) % STEPS
                if n == S:
                    engine.wait_ge(m_full.sem, m_full.at(it, M_ACC + RING * jh + RING))
                else:
                    engine.wait_ge(acc_done.sem, acc_done.at(it, jh * S + n + 1))

        block = ctx.enter_context(nc.Block())

        @block.sync
        def _(sp):
            sp.dma_start(s_first[:], a["s_first"]).then_inc(state_loaded, 16)
            sp.dma_start(rows[:].rearrange("p r c -> p (r c)"), a["rows"]).then_inc(state_loaded, 16)
            sp.dma_start(pars[:], a["pars"][0]).then_inc(pars_loaded, 16)

            def x_half(to, chunk, n):
                return to[chunk].rearrange("p (k b t) -> p k b t", k=KT, b=B)[:, :, HB * n:HB * n + HB, :]

            for n in range(2):
                sp.dma_start(half(x, n), x_half(a["x"], 0, n)).then_inc(x_loaded[n], 16)
            sp.dma_start(small[:], a["small"][0]).then_inc(small_loaded, 16)
            sp.dma_start(a["xs"][1], a["x"][1]).then_inc(x_stored, 16)

            def layer_traffic(layer, last):
                after = None if last else sp.snap(layer + 1)
                for chunk in range(CHUNKS):
                    it = layer * CHUNKS + chunk if last else sp.snap(layer * CHUNKS + chunk)

                    def load_weight(n):
                        tiles, end = used_by[n - NSLOT] if n >= NSLOT else used_by[n - NSLOT + NW]
                        sp.wait_ge(tiles.sem, tiles.at(it, end if n >= NSLOT else end - tiles.per))
                        src = a["big"][layer, n] if last else a["big"][bass.ds(layer, 1), n, :, :].rearrange("o p n -> (o p) n")
                        sp.dma_start(ring[n % NSLOT], src).then_inc(slot_loaded[n % NSLOT], 16)

                    for n in range(WO + 1):
                        load_weight(n)
                        if n == WG and chunk == CHUNKS - 1 and not last:
                            sp.wait_ge(j_full.sem, j_full.at(it, J_AT["w"] + 8))
                            sp.dma_start(small[:], a["small"][bass.ds(after, 1), :, :].rearrange("o p n -> (o p) n")).then_inc(small_loaded, 16)
                    load_weight(WFR)
                    for n in range(GQ):
                        sp.wait_ge(og_ready.sem, og_ready.at(it, n + 1))
                        j = slice(S // GQ * n, S // GQ * (n + 1))
                        sp.dma_start(a["og"][:, j, :], att[:, j, :]).then_inc(og_stored, 16)
                    sp.wait_ge(og_stored, it * (16 * GQ) + 16 * GQ)
                    for b in range(B):
                        sp.dma_start(ogc[:, :, b, :], a["og"].rearrange("(b k h) j t -> b (h j) k t", b=B, k=KT)[b]).then_inc(og_loaded[b // HB], 16)
                    load_weight(WFK)
                    load_weight(WFV)
                    if chunk == CHUNKS - 1 and not last:
                        sp.wait_ge(fmix_ready.sem, fmix_ready.at(it, 4))
                        sp.dma_start(pars[:], a["pars"][bass.ds(after, 1), :, :].rearrange("o p n -> (o p) n")).then_inc(pars_loaded, 16)
                    sp.wait_ge(x_stored, it * 32 + 16)
                    for n in range(2):
                        sp.wait_ge(x_done.sem, x_done.at(it, n + 1))
                        sp.dma_start(x_half(a["xs"], chunk, n), half(x_new, n)).then_inc(x_stored, 16)
                        if not (last and chunk == CHUNKS - 1):
                            sp.dma_start(half(x, n), x_half(a["xs"], 1 - chunk, n)).then_inc(x_loaded[n], 16)

            with sp.Fori(0, LAYERS - 1) as layer:
                layer_traffic(layer, False)
            layer_traffic(LAYERS - 1, True)
            sp.wait_ge(x_stored, X_STORED)
            for n in range(4):
                sp.dma_start(at_w[n].rearrange("p k e -> p (k e)"), a["at_w"][n]).then_inc(at_loaded, 16)
            sp.dma_start(lnp, a["at_ln"]).then_inc(at_loaded, 16)
            sp.dma_start(gate[:, 0:1], a["gate"]).then_inc(at_loaded, 16)
            sp.sem_inc(out_stored, 16)

            def load_context(b):
                sp.dma_start(an.rearrange("p k s -> p (k s)"), a["ctx"][bass.ds(b, 1), :, :].rearrange("o p n -> (o p) n")).then_inc(cx_loaded, 16)
                sp.dma_start(mask_u, a["mask"][bass.ds(b, 1), :].broadcast_to((P, SK))).then_inc(cx_loaded, 16)

            def load_x(to, b, loaded):
                for c in range(CHUNKS):
                    sp.dma_start(to[:, :, c * TC:(c + 1) * TC],
                                 a["xs"][c].rearrange("p (k b t) -> p k b t", k=KT, b=B)[:, :, bass.ds(b, 1), :].rearrange("p k o t -> p k (o t)")).then_inc(loaded, 16)

            load_context(0)
            load_x(xq, 0, xq_loaded)

            def batch_traffic(b, last):
                after = None if last else sp.snap(b + 1)
                sp.wait_ge(out_stored, b * 16 + 16)
                load_x(ay, b, ay_loaded)
                if not last:
                    sp.wait_ge(d_free.sem, d_free.at(b, D_V + ST))
                    load_context(after)
                    load_x(xq, after, xq_loaded)
                sp.wait_ge(d_free.sem, d_free.at(b, D_PER))
                sp.dma_start(a["out"][bass.ds(b, 1), :, :].rearrange("o p n -> (o p) n"), ay.rearrange("p k t -> p (k t)")).then_inc(out_stored, 16)

            with sp.Fori(0, B - 1) as b:
                batch_traffic(b, False)
            batch_traffic(B - 1, True)
            sp.wait_ge(out_stored, 16 * (B + 1))

        @block.tensor
        def _(pe):
            mm = nc.tensor.matmul
            pe.sem_inc(m_full.sem, m_full.credit)
            pe.sem_inc(j_full.sem, j_full.credit)
            pe.wait_ge(const_ready, CONSTS)
            with pe.Fori(0, LAYERS) as layer:
                with pe.Fori(0, CHUNKS) as chunk:
                    it = pe.snap(layer * CHUNKS + chunk)

                    def tile_m(n):
                        pe.wait_ge(m_free.sem, m_free.at(it, n + 1 - RING))
                        return bank_m(n)

                    def tile_j(n):
                        pe.wait_ge(j_free.sem, j_free.at(it, n + 1 - RING))
                        return bank_j(n)

                    def weight(n):
                        pe.wait_ge(slot_loaded[n % NSLOT], it * (16 * SLOT_LOADS) + 16 * (n // NSLOT + 1))
                        return ring[n % NSLOT]

                    def stats(which, m0, j0, r0):
                        for b in range(B):
                            if b % HB == 0:
                                if which == 0:
                                    pe.wait_ge(x_loaded[b // HB], it * 16 + 16)
                                else:
                                    pe.wait_ge(m_free.sem, m_free.at(it, M_WO + KT * (b // HB) + KT))
                            t = tile_m(m0 + b)
                            for k in range(KT):
                                last = mm(t[:, 0:TC], ones[:], x[:, k, b, :], start=k == 0, stop=k == KT - 1)
                            m_full.inc(last)
                        pe.wait_ge(sq_ready.sem, sq_ready.at(it, 2 * which + 2))
                        t = tile_j(j0)
                        for k in range(KT):
                            for b in range(B):
                                last = mm(t[H * b:H * b + H, 0:TC], ones[:, 0:H], mix[1][:, k, b, :], start=k == 0, stop=k == KT - 1, skip_group_check=True)
                        j_full.inc(last)
                        pe.wait_ge(rstd_ready.sem, rstd_ready.at(it, which + 1))
                        for n in range(2):
                            t = tile_m(r0 + n)
                            for o in range(HB):
                                last = mm(t[:, o * TC:(o + 1) * TC], pick[:, HB * n + o, :], std, start=True, stop=True, skip_group_check=True)
                            m_full.inc(last)

                    stats(0, M_MEAN1, J_VAR1, M_RSTD1)
                    pe.wait_ge(small_loaded, layer * 16 + 16)
                    for n in range(2):
                        pe.wait_ge(lmix_ready.sem, lmix_ready.at(it, n + 1))
                        for part in range(2):
                            t = tile_j(J_W1 + 2 * n + part)
                            for k in range(KT):
                                last = mm(t, w1[:, k, DM * part:DM * part + P], half2(mix[1], n)[:, k, :], start=k == 0, stop=k == KT - 1)
                            j_full.inc(last)

                    def second_factor(q, n, k):
                        f = FAN[ORDER[q]]
                        if q == 0 and k == 0:
                            pe.wait_ge(j_free.sem, j_free.at(it, J_W1 + 2 * n + 2))
                        t = tile_m(M_MIX + 8 * q + 4 * n + k)
                        cols = slice(n * HALF, (n + 1) * HALF)
                        m_full.inc(mm(t, w2[:, f, P * k:P * k + P], (th_a if f < 4 else th_b)[:, cols], start=True, stop=True))

                    for n in range(2):
                        for k in range(KT):
                            second_factor(0, n, k)

                    def project(q, s, pair):
                        t = tile_j(J_AT[s] + pair)
                        for o in range(2):
                            i, cols = 2 * pair + o, slice(o * TC, (o + 1) * TC)
                            if s == "w":
                                for b in range(B):
                                    last = mm(t[H * b:H * b + H, cols], td2[:, i, :], tdh[:, b * TC:(b + 1) * TC], start=True, stop=True)
                            else:
                                for k in range(KT):
                                    for b in range(B):
                                        last = mm(t[H * b:H * b + H, cols], w[:, k, i, :], mix[q % 2][:, k, b, :], start=k == 0, stop=k == KT - 1,
                                                  skip_group_check=True)
                        j_full.inc(last)

                    for q, s in enumerate(ORDER):
                        pe.wait_ge(mix_ready.sem, mix_ready.at(it, 2 * q + 2))
                        if s == "w":
                            for b in range(B):
                                t = tile_j(J_AT["td"] + b)
                                for k in range(KT):
                                    last = mm(t[:, 0:TC], td1[:, k, :], mix[q % 2][:, k, b, :], start=k == 0, stop=k == KT - 1)
                                j_full.inc(last)
                        else:
                            w = weight({"k": WK, "v": WV, "r": WR, "g": WG}[s]).rearrange("p (k i h) -> p k i h", k=KT, i=S)
                        for pair in range(S // 2 if s != "g" else 0):
                            second_factor(q + 1, pair // KT, pair % KT)
                            if s == "w" and pair == 0:
                                pe.wait_ge(j_free.sem, j_free.at(it, J_AT["td"] + 4))
                            project(q, s, pair)

                    for jh in range(2):
                        tile_m(M_ACC + RING * jh + RING - 1)
                        for n in range(STEPS):
                            step = jh * STEPS + n
                            if step % 4 == 0 and step // 4 < S // 2:
                                project(STREAMS - 1, "g", step // 4)
                            pe.wait_ge(rs_ready.sem, rs_ready.at(it, step + 1))
                            for c in range(RING):
                                last = mm(bank_m(M_ACC + RING * jh + c), ident[:], kv[step % 4][:, 2 * c:2 * c + 2, 0:TC], start=n == 0, stop=n == STEPS - 1)
                                if n == STEPS - 1:
                                    m_full.inc(last)
                            if n < STEPS - 1:
                                acc_done.inc(last)

                    w = weight(WO).rearrange("p (k e) -> p k e", k=KT)
                    for n in range(2):
                        pe.wait_ge(og_loaded[n], it * (16 * HB) + 16 * HB)
                        for m in range(KT):
                            t = tile_m(M_WO + KT * n + m)
                            for k in range(KT):
                                last = mm(t, w[:, k, P * m:P * m + P], half2(ogc, n)[:, k, :], start=k == 0, stop=k == KT - 1)
                            m_full.inc(last)

                    stats(1, M_MEAN2, J_VAR2, M_RSTD2)
                    wr, wk = weight(WFR), weight(WFK)
                    for n, (w, j0) in enumerate(((wr, J_WFR), (wk, J_WFK))):
                        w = w.rearrange("p (k e) -> p k e", k=KT)
                        for c in range(2):
                            pe.wait_ge(fmix_ready.sem, fmix_ready.at(it, 2 * n + c + 1))
                            for m in range(KT):
                                t = tile_j(j0 + KT * c + m)
                                for k in range(KT):
                                    last = mm(t, w[:, k, P * m:P * m + P], half2(mix[n], c)[:, k, :], start=k == 0, stop=k == KT - 1)
                                j_full.inc(last)
                    w = weight(WFV).rearrange("p (k e) -> p k e", k=KT)
                    for c in range(2):
                        pe.wait_ge(kk_ready.sem, kk_ready.at(it, KT * c + KT))
                        for m in range(KT):
                            t = tile_m(M_WFV + KT * c + m)
                            for k in range(KT):
                                last = mm(t, w[:, k, P * m:P * m + P], kk[:, k, c * HALF:(c + 1) * HALF], start=k == 0, stop=k == KT - 1)
                            m_full.inc(last)
                    for c in (m_full, j_full, acc_done):
                        c.close()

            wq, wk, wv, wo = at_w
            pe.wait_ge(at_loaded, 6 * 16)
            pe.wait_ge(at_const, AT_CONSTS)
            with pe.Fori(0, B) as b:
                def tile_d(n):
                    pe.wait_ge(d_free.sem, d_free.at(b, n + 1 - 2))
                    return bank_d(n)

                def tile_a(n):
                    pe.wait_ge(a_free.sem, a_free.at(b, n + 1 - 2))
                    return bank_a(n)

                pe.wait_ge(cx_loaded, b * 32 + 32)
                for sh in range(2):
                    t = tile_d(D_MEAN + sh)
                    for k in range(KT):
                        last = mm(t, ones[:], an[:, k, sh * 512:sh * 512 + 512], start=k == 0, stop=k == KT - 1)
                    d_full.inc(last)
                pe.wait_ge(xq_loaded, b * (16 * CHUNKS) + 16 * CHUNKS)
                for e in range(KT):
                    t = tile_a(A_Q + e)
                    for k in range(KT):
                        last = mm(t, wq[:, k, P * e:P * e + P], xq[:, k, :], start=k == 0, stop=k == KT - 1)
                    a_full.inc(last)
                pe.wait_ge(asq_ready.sem, asq_ready.at(b, 2))
                t = tile_a(A_VAR)
                for k in range(KT):
                    for c in range(4):
                        last = mm(t[AD * c:AD * c + AD, 0:SQ], ones[:, 0:AD], asq[:, k, c * SQ:c * SQ + SQ], start=k == 0, stop=k == KT - 1, skip_group_check=True)
                a_full.inc(last)
                pe.wait_ge(arstd_ready.sem, arstd_ready.at(b, 1))
                for sh in range(2):
                    t = tile_d(D_RSTD + sh)
                    for o in range(2):
                        last = mm(t[:, o * SQ:o * SQ + SQ], pick[:, 2 * sh + o, :], astd, start=True, stop=True, skip_group_check=True)
                    d_full.inc(last)
                for sh in range(2):
                    pe.wait_ge(an_ready.sem, an_ready.at(b, sh + 1))
                    for e in range(KT):
                        t = tile_a(A_K + KT * sh + e)
                        for k in range(KT):
                            last = mm(t, wk[:, k, P * e:P * e + P], an[:, k, sh * 512:sh * 512 + 512], start=k == 0, stop=k == KT - 1)
                        a_full.inc(last)
                for st in range(ST):
                    t = tile_d(D_V + st)
                    for k in range(KT):
                        last = mm(t, an[:, k, P * st:P * st + P], wv[:, k, :], start=k == 0, stop=k == KT - 1)
                    d_full.inc(last)

                def scores(u, h):
                    e, q = u // TT, u % TT
                    pe.wait_ge(s_free.sem, s_free.at(b, HPT * u + h + 1 - 2))
                    t = banks_s(HPT * u + h)
                    for sh in range(2):
                        last = mm(t[:, sh, :], qz[:, HPT * e + h, P * q:P * q + P], keys[:, e, sh * 512:sh * 512 + 512], start=True, stop=True)
                    s_full.inc(last)

                def transposed(u, h):
                    if h == 0:
                        pe.wait_ge(diag_ready.sem, diag_ready.at(b, u + 1))
                    for n, (t, full) in enumerate(((tile_a(A_T + HPT * u + h), a_full), (None, d_full))):
                        if n == 1:
                            t = tile_d(d_head(u, h))
                        for o in range(4):
                            st = 4 * n + o
                            last = mm(t[:, P * o:P * o + P], probs[u % 2][:, h, P * st:P * st + P], diag[:, h, :], start=True, stop=True, skip_group_check=True)
                        full.inc(last)

                def weighted(u):
                    pe.wait_ge(a_free.sem, a_free.at(b, A_T + HPT * u + HPT))
                    t = tile_d(d_head(u, HPT))
                    pe.wait_ge(d_free.sem, d_free.at(b, d_head(u, HPT)))
                    e = u // TT
                    for st in range(ST):
                        for h in range(HPT):
                            last = mm(t[AD * h:AD * h + AD, 0:P], vals[:, st, (HPT * e + h) * AD:(HPT * e + h + 1) * AD], probs_t[:, st, h, :],
                                      start=st == 0, stop=st == ST - 1, skip_group_check=True)
                    d_full.inc(last)

                pe.wait_ge(a_free.sem, a_free.at(b, A_K + 2 * KT))
                for step in range(UNITS + 2):
                    if step >= 2:
                        weighted(step - 2)
                    for h in range(HPT):
                        if step < UNITS:
                            scores(step, h)
                        if 1 <= step <= UNITS:
                            transposed(step - 1, h)
                pe.wait_ge(d_free.sem, d_free.at(b, D_WO))
                for m in range(KT):
                    t = tile_d(D_WO + m)
                    for k in range(KT):
                        last = mm(t, wo[:, k, P * m:P * m + P], ao[:, k, :], start=k == 0, stop=k == KT - 1)
                    d_full.inc(last)
                for c in (a_full, d_full, s_full):
                    c.close()

        @block.scalar
        def _(act):
            f = nc.scalar.activation
            act.sem_inc(j_free.sem, j_free.credit)
            act.sem_inc(edge_kept.sem, edge_kept.credit)
            act.sem_inc(s_saved.sem, s_saved.credit)
            act.wait_ge(state_loaded, 32)
            act.wait_ge(const_ready, CONSTS)
            s_at = s_now[:].rearrange("p (i j) -> p i j", i=S)
            with act.Fori(0, LAYERS) as layer:
                act.wait_ge(pars_loaded, layer * 16 + 16)
                f(prev[0][:], rows[:, 1, :], ACT.Copy)
                f(prev[1][:], rows[:, 0, :], ACT.Copy)
                f(s_now[:], s_first[:], ACT.Copy).then_inc(layer_set, 1)
                act.wait_ge(layer_set, layer + 1)
                with act.Fori(0, CHUNKS) as chunk:
                    it = act.snap(layer * CHUNKS + chunk)

                    def full_j(n):
                        act.wait_ge(j_full.sem, j_full.at(it, n + 1))
                        return bank_j(n)

                    def layer_norm(which, m0, j0, lw, lb):
                        for n in range(2):
                            act.wait_ge(m_free.sem, m_free.at(it, m0 + HB * n + HB))
                            sq_ready.inc(f(half2(mix[1], n), half2(mix[0], n), ACT.Square))
                        act.wait_ge(edge_kept.sem, edge_kept.at(it, which - 2 + 1))
                        edge_set.inc(f(xa[:, :, :, 0:1], prev[which][:].rearrange("p (k b o) -> p k b o", k=KT, o=1), ACT.Copy))
                        t = full_j(j0)
                        j_free.inc(f(std, t[:, 0:TC], ACT.Sqrt, bias=eps[:]))
                        for n in range(2):
                            act.wait_ge(xn_ready.sem, xn_ready.at(it, 2 * which + n + 1))
                            for k in range(KT):
                                last = f(xa[:, k, HB * n:HB * n + HB, 1:TC + 1], mix[0][:, k, HB * n:HB * n + HB, :], ACT.Identity, scale=par(lw, k), bias=par(lb, k))
                            xa_ready.inc(last)
                        act.wait_ge(xa_ready.sem, xa_ready.at(it, 2 * which + 2))
                        edge_kept.inc(f(prev[which][:].rearrange("p (k b o) -> p k b o", k=KT, o=1), xa[:, :, :, TC:TC + 1], ACT.Copy))

                    layer_norm(0, M_MEAN1, J_VAR1, LN1W, LN1B)
                    for n in range(2):
                        cols = slice(n * HALF, (n + 1) * HALF)
                        t = full_j(J_W1 + 2 * n)
                        j_free.inc(f(th_a[:, cols], t, ACT.Tanh))
                        t = full_j(J_W1 + 2 * n + 1)
                        j_free.inc(f(th_b[:, cols], t, ACT.Tanh))
                    for s in ORDER[:-1]:
                        if s == "w":
                            for b in range(B):
                                t = full_j(J_AT["td"] + b)
                                j_free.inc(f(tdh[:, b * TC:(b + 1) * TC], t[:, 0:TC], ACT.Tanh))
                        if s == "r":
                            act.wait_ge(x_stored, it * 32 + 16)
                        for pair in range(S // 2):
                            t = full_j(J_AT[s] + pair).rearrange("p (i t) -> p i t", i=2)
                            if s == "w":
                                for o in range(2):
                                    last = f(hm["w"][:, 2 * pair + o, :], t[:, o, :], ACT.Exp, bias=par(TDEC, 2 * pair + o))
                                j_free.inc(last)
                            else:
                                j_free.inc(f(hm[s][:, 2 * pair:2 * pair + 2, :], t, ACT.Copy))
                        if s == "w":
                            act.wait_ge(j_free.sem, j_free.at(it, J_AT["w"] + 8))
                            w_ready.inc(f(hm["w"], hm["w"], ACT.Exp, scale=-1.0))

                    def set_scan(n):
                        jh, i = n // S, n % S
                        if n == 0:
                            act.wait_ge(s_saved.sem, s_saved.at(it, 0))
                            act.wait_ge(w_ready.sem, w_ready.at(it, 1))
                            act.wait_ge(mix_ready.sem, mix_ready.at(it, 2 * STREAMS))
                            act.wait_ge(ruk_step.sem, ruk_step.at(it, 2))
                        kv_free(act, it, jh * STEPS + i)
                        f(kv[(jh * STEPS + i) % 4][:, :, 0:1], s_at[:, i, JH * jh:JH * jh + JH].rearrange("p (j o) -> p j o", o=1), ACT.Copy)
                        if n >= 2:
                            act.wait_ge(scan_ready.sem, scan_ready.at(it, n - 1))
                        scan_set.inc(f(wt[n % 2][:, :, 1:TC + 1], over(hm["w"][:, i, :], JH), ACT.Copy))

                    set_scan(0)
                    set_scan(1)
                    for n in range(2 * S):
                        jh, i = n // S, n % S
                        act.wait_ge(scan_ready.sem, scan_ready.at(it, n + 1))
                        s_saved.inc(f(s_at[:, i, JH * jh:JH * jh + JH].rearrange("p (j o) -> p j o", o=1), s_ext[:, :, TC:TC + 1], ACT.Copy))
                        if n + 2 < 2 * S:
                            set_scan(n + 2)
                        if n % 4 == 0:
                            t = full_j(J_AT["g"] + n // 4).rearrange("p (i t) -> p i t", i=2)
                            j_free.inc(f(hm["g"][:, n // 2:n // 2 + 2, :], t, ACT.Silu))
                    act.wait_ge(gn_step.sem, gn_step.at(it, 2))
                    gn_act.inc(f(gsq, gd, ACT.Square))
                    act.wait_ge(gn_step.sem, gn_step.at(it, 3))
                    gn_act.inc(f(gstd, gsum, ACT.Sqrt, scale=1.0 / S, bias=eps[:]))
                    for n in range(GQ):
                        act.wait_ge(gn_step.sem, gn_step.at(it, 4 + n + 1))
                        for j in range(S // GQ * n, S // GQ * (n + 1)):
                            last = f(gd[:, j, :], gd[:, j, :], ACT.Identity, scale=par(GNW, j), bias=par(GNB, j))
                        gn_act.inc(last)

                    layer_norm(1, M_MEAN2, J_VAR2, LN2W, LN2B)
                    for j0, buf, fn in ((J_WFR, rr, ACT.Sigmoid), (J_WFK, kk, ACT.Relu)):
                        for c in range(2):
                            for m in range(KT):
                                t = full_j(j0 + KT * c + m)
                                j_free.inc(f(buf[:, m, c * HALF:(c + 1) * HALF], t, fn))
                    for c in (j_free, sq_ready, edge_set, edge_kept, xa_ready, w_ready, scan_set, s_saved, gn_act):
                        c.close()

            act.sem_inc(a_free.sem, a_free.credit)
            act.sem_inc(s_free.sem, s_free.credit)
            act.wait_ge(at_loaded, 6 * 16)
            f(gate[:, 1:2], gate[:, 0:1], ACT.Tanh).then_inc(gate_ready, 1)
            act.wait_ge(at_const, AT_CONSTS)
            with act.Fori(0, B) as b:
                def full_a(n):
                    act.wait_ge(a_full.sem, a_full.at(b, n + 1))
                    return bank_a(n)

                def square(sh):
                    cols = slice(sh * 512, sh * 512 + 512)
                    act.wait_ge(d_free.sem, d_free.at(b, D_MEAN + sh + 1))
                    asq_ready.inc(f(asq[:, :, cols], an[:, :, cols], ACT.Square))

                for e in range(KT):
                    if e < 2:
                        square(e)
                    t = full_a(A_Q + e)
                    for h in range(HPT):
                        rows_h = slice(AD * h, AD * h + AD)
                        last = f(qz[rows_h, HPT * e + h, :], t[rows_h, :], ACT.Copy)
                    a_free.inc(last)
                t = full_a(A_VAR)
                a_free.inc(f(astd, t[:, 0:SQ], ACT.Sqrt, bias=eps[:]))
                for sh in range(2):
                    cols = slice(sh * 512, sh * 512 + 512)
                    act.wait_ge(axn_ready.sem, axn_ready.at(b, sh + 1))
                    for k in range(KT):
                        last = f(an[:, k, cols], an[:, k, cols], ACT.Identity, scale=lnp[:, k:k + 1], bias=lnp[:, KT + k:KT + k + 1])
                    an_ready.inc(last)
                for sh in range(2):
                    for e in range(KT):
                        t = full_a(A_K + KT * sh + e)
                        a_free.inc(f(keys[:, e, sh * 512:sh * 512 + 512], t, ACT.Copy))
                for step in range(UNITS + 1):
                    for h in range(HPT):
                        if step < UNITS:
                            act.wait_ge(nmx_ready.sem, nmx_ready.at(b, HPT * step + h + 1))
                            s_free.inc(f(probs[step % 2][:, h, :].rearrange("p (a s) -> p a s", a=2), banks_s(HPT * step + h), ACT.Exp, scale=SCALE,
                                         bias=nmx[:, step % 2, h:h + 1], accum_out=den[:, step % 2, h:h + 1]))
                        if step >= 1:
                            u = step - 1
                            t = full_a(A_T + HPT * u + h)
                            a_free.inc(f(probs_t[:, 0:4, h, :], t.rearrange("p (s t) -> p s t", s=4), ACT.Copy))
                for c in (a_free, s_free, asq_ready, an_ready):
                    c.close()

        @block.vector
        def _(dve):
            tt = nc.vector.tensor_tensor
            stt = nc.vector.scalar_tensor_tensor
            nc.vector.memset(ones[:], 1.0 / E).then_inc(const_ready, 1)
            nc.vector.memset(eps[:], EPS).then_inc(const_ready, 1)
            nc.vector.memset(wt[1][:, :, 0:1], 0.0).then_inc(const_ready, 1)
            dve.wait_ge(const_ready, 5)
            nc.vector.tensor_copy(pick[:], ident[:].rearrange("p (b h) -> p b h", b=B)[:, :, 0:1].broadcast_to((P, B, P))).then_inc(const_ready, 1)
            dve.sem_inc(m_free.sem, m_free.credit)
            with dve.Fori(0, LAYERS) as layer:
                with dve.Fori(0, CHUNKS) as chunk:
                    it = dve.snap(layer * CHUNKS + chunk)

                    def full_m(n):
                        dve.wait_ge(m_full.sem, m_full.at(it, n + 1))
                        return bank_m(n)

                    def layer_norm(which, m0, j0, r0):
                        for b in range(B):
                            t = full_m(m0 + b)
                            m_free.inc(tt(mix[0][:, :, b, :], x[:, :, b, :], over(t[:, 0:TC], KT), ALU.subtract))
                        dve.wait_ge(j_free.sem, j_free.at(it, j0 + 1))
                        rstd_ready.inc(nc.vector.reciprocal(std, std))
                        for n in range(2):
                            t = full_m(r0 + n)
                            last = tt(half2(mix[0], n), half2(mix[0], n), over(t, KT), ALU.mult)
                            m_free.inc(last)
                            dve.wait_ge(m_free.sem, m_free.at(it, r0 + n + 1))
                            dve.sem_inc(xn_ready.sem, 1)
                            xn_ready.n += 1
                        for n in range(2):
                            dve.wait_ge(xa_ready.sem, xa_ready.at(it, 2 * which + n + 1))
                            h = xa[:, :, HB * n:HB * n + HB, :]
                            sx_ready.inc(tt(half(sx, n), h[:, :, :, 0:TC], h[:, :, :, 1:TC + 1], ALU.subtract))

                    def shifted_mix(to, which, n, at):
                        dve.wait_ge(sx_ready.sem, sx_ready.at(it, 2 * which + n + 1))
                        for k in range(KT):
                            last = stt(half(to, n)[:, k], half(sx, n)[:, k], par(at, k), half(xa, n)[:, k, :, 1:TC + 1], ALU.mult, ALU.add)
                        return last

                    layer_norm(0, M_MEAN1, J_VAR1, M_RSTD1)
                    dve.wait_ge(pars_loaded, layer * 16 + 16)
                    for n in range(2):
                        lmix_ready.inc(shifted_mix(mix[1], 0, n, MAAX))
                    for q, s in enumerate(ORDER):
                        if q >= 2:
                            dve.wait_ge(j_full.sem, j_full.at(it, j_end[ORDER[q - 2]]))
                        for n in range(2):
                            for k in range(KT):
                                t = full_m(M_MIX + 8 * q + 4 * n + k)
                                m_free.inc(stt(half2(mix[q % 2], n)[:, k, :], t, par(MAAS, KT * FAN[s] + k), half2(sx, n)[:, k, :], ALU.add, ALU.mult))
                    dve.wait_ge(j_free.sem, j_free.at(it, J_AT["r"] + 8))
                    dve.wait_ge(j_full.sem, j_full.at(it, J_AT["td"] + 4))
                    for i in range(S):
                        last = stt(kr2[:, i, :], hm["k"][:, i, :], par(UCOL, i), hm["r"][:, i, :], ALU.mult, ALU.mult)
                    ruk_step.inc(last)
                    dve.wait_ge(ruk_step.sem, ruk_step.at(it, 1))
                    ruk_step.inc(nc.vector.tensor_reduce(ruk, kr2.rearrange("p i t -> p t i"), AX_X, ALU.add))
                    dve.wait_ge(ruk_step.sem, ruk_step.at(it, 2))

                    ruk_step.inc(nc.vector.memset(wt[0][:, :, 0:1], 0.0))
                    dve.wait_ge(ruk_step.sem, ruk_step.at(it, 3))

                    def collect(jh):
                        for c in range(RING):
                            t = full_m(M_ACC + RING * jh + c)
                            m_free.inc(nc.vector.tensor_copy(att[:, JH * jh + 2 * c:JH * jh + 2 * c + 2, :].rearrange("p j t -> p (j t)"), t))

                    for n in range(2 * S):
                        jh, i = n // S, n % S
                        step = jh * STEPS + i
                        dve.wait_ge(kv_ready.sem, kv_ready.at(it, n + 1))
                        dve.wait_ge(scan_set.sem, scan_set.at(it, n + 1))
                        dve.wait_ge(s_saved.sem, s_saved.at(it, n))
                        if n:
                            dve.wait_ge(rs_ready.sem, rs_ready.at(it, (n - 1) // S * STEPS + (n - 1) % S + 1))
                        scan_ready.inc(nc.vector.tensor_tensor_scan(s_flat, wt_flat[n % 2], kv_flat[step % 4], 0.0, ALU.mult, ALU.add))
                        dve.wait_ge(scan_ready.sem, scan_ready.at(it, n + 1))
                        rs_ready.inc(tt(kv[step % 4][:, :, 0:TC], s_ext[:, :, 0:TC], over(hm["r"][:, i, :], JH), ALU.mult))
                        if i == S - 1:
                            kv_free(dve, it, step + 1)
                            rs_ready.inc(tt(kv[(step + 1) % 4][:, :, 0:TC], hm["v"][:, JH * jh:JH * jh + JH, :], over(ruk, JH), ALU.mult))
                        if n == S + 1:
                            collect(0)
                    collect(1)

                    dve.wait_ge(m_free.sem, m_free.at(it, M_ACC + 2 * RING))
                    dve.wait_ge(j_free.sem, j_free.at(it, J_AT["g"] + 8))
                    dve.wait_ge(s_saved.sem, s_saved.at(it, 2 * S))
                    gn_step.inc(nc.vector.tensor_reduce(gsum, att.rearrange("p j t -> p t j"), AX_X, ALU.add))
                    dve.wait_ge(gn_step.sem, gn_step.at(it, 1))
                    gn_step.inc(stt(gd, over(gsum, S), -1.0 / S, att, ALU.mult, ALU.add))
                    dve.wait_ge(gn_act.sem, gn_act.at(it, 1))
                    gn_step.inc(nc.vector.tensor_reduce(gsum, gsq.rearrange("p j t -> p t j"), AX_X, ALU.add))
                    dve.wait_ge(gn_act.sem, gn_act.at(it, 2))
                    gn_step.inc(nc.vector.reciprocal(gstd, gstd))
                    dve.wait_ge(gn_step.sem, gn_step.at(it, 4))
                    for n in range(GQ):
                        j = slice(S // GQ * n, S // GQ * (n + 1))
                        gn_step.inc(tt(gd[:, j, :], gd[:, j, :], over(gstd, S // GQ), ALU.mult))
                    for n in range(GQ):
                        dve.wait_ge(gn_act.sem, gn_act.at(it, 2 + n + 1))
                        j = slice(S // GQ * n, S // GQ * (n + 1))
                        og_ready.inc(tt(att[:, j, :], gd[:, j, :], hm["g"][:, j, :], ALU.mult))
                    for n in range(2):
                        for m in range(KT):
                            t = full_m(M_WO + KT * n + m)
                            m_free.inc(tt(half2(x, n)[:, m, :], half2(x, n)[:, m, :], t, ALU.add))

                    layer_norm(1, M_MEAN2, J_VAR2, M_RSTD2)
                    for to, at in ((mix[0], FMR), (mix[1], FMK)):
                        for n in range(2):
                            fmix_ready.inc(shifted_mix(to, 1, n, at))
                    for c in range(2):
                        for m in range(KT):
                            t = full_m(M_WFV + KT * c + m)
                            r = rr[:, m, c * HALF:(c + 1) * HALF]
                            m_free.inc(tt(r, r, t, ALU.mult))
                        for m in range(KT):
                            dve.wait_ge(m_free.sem, m_free.at(it, M_WFV + KT * c + m + 1))
                            last = tt(half2(x_new, c)[:, m, :], half2(x, c)[:, m, :], rr[:, m, c * HALF:(c + 1) * HALF], ALU.add)
                        x_done.inc(last)
                    for c in (m_free, rstd_ready, xn_ready, sx_ready, lmix_ready, ruk_step, scan_ready, rs_ready, gn_step, og_ready, fmix_ready, x_done):
                        c.close()

            dve.sem_inc(d_free.sem, d_free.credit)
            dve.wait_ge(x_stored, X_STORED)
            nc.vector.memset(qz, 0.0).then_inc(at_const, 1)
            dve.wait_ge(gate_ready, 1)
            with dve.Fori(0, B) as b:
                def full_d(n):
                    dve.wait_ge(d_full.sem, d_full.at(b, n + 1))
                    return bank_d(n)

                for sh in range(2):
                    cols = slice(sh * 512, sh * 512 + 512)
                    t = full_d(D_MEAN + sh)
                    d_free.inc(tt(an[:, :, cols], an[:, :, cols], over(t, KT), ALU.subtract))
                dve.wait_ge(cx_loaded, b * 32 + 32)
                mask_step.inc(nc.vector.tensor_scalar(mbias, mask_u, -1.0, 3e38, ALU.add, ALU.mult))
                dve.wait_ge(mask_step.sem, mask_step.at(b, 1))
                mask_step.inc(nc.vector.tensor_scalar(mbias, mbias, 10.0, None, ALU.mult))
                dve.wait_ge(a_free.sem, a_free.at(b, A_VAR + 1))
                arstd_ready.inc(nc.vector.reciprocal(astd, astd))
                for sh in range(2):
                    cols = slice(sh * 512, sh * 512 + 512)
                    t = full_d(D_RSTD + sh)
                    d_free.inc(tt(an[:, :, cols], an[:, :, cols], over(t, KT), ALU.mult))
                    dve.wait_ge(d_free.sem, d_free.at(b, D_RSTD + sh + 1))
                    dve.sem_inc(axn_ready.sem, 1)
                    axn_ready.n += 1
                for st in range(ST):
                    t = full_d(D_V + st)
                    d_free.inc(nc.vector.tensor_copy(vals[:, st, :], t))
                dve.wait_ge(mask_step.sem, mask_step.at(b, 2))
                for step in range(UNITS + 2):
                    if step >= 2:
                        u = step - 2
                        t = full_d(d_head(u, HPT))
                        d_free.inc(nc.vector.tensor_copy(ao[:, u // TT, P * (u % TT):P * (u % TT) + P], t[:, 0:P]))
                    for h in range(HPT):
                        if step < UNITS:
                            n = HPT * step + h
                            dve.wait_ge(s_full.sem, s_full.at(b, n + 1))
                            dve.sem_inc(max_turn, 1)
                            t = banks_s(n)
                            mx_ready.inc(nc.vector.tensor_tensor_reduce(t, t, mbias.rearrange("p (a s) -> p a s", a=2), 1.0, -3.4e38, ALU.add, ALU.max,
                                                                        accum_out=mx[:, step % 2, h:h + 1]))
                            dve.wait_ge(mx_ready.sem, mx_ready.at(b, n + 1))
                            nmx_ready.inc(nc.vector.tensor_scalar(nmx[:, step % 2, h:h + 1], mx[:, step % 2, h:h + 1], -SCALE, None, ALU.mult))
                        if 1 <= step <= UNITS:
                            t = full_d(d_head(step - 1, h))
                            d_free.inc(nc.vector.tensor_copy(probs_t[:, 4:8, h, :], t.rearrange("p (s t) -> p s t", s=4)))
                    if step < UNITS:
                        dve.wait_ge(s_free.sem, s_free.at(b, HPT * step + HPT))
                        den_ready.inc(nc.vector.reciprocal(rden, den[:, step % 2, :]))
                        dve.wait_ge(den_ready.sem, den_ready.at(b, step + 1))
                        diag_ready.inc(tt(diag, ident[:].rearrange("p (o c) -> p o c", o=1).broadcast_to((P, HPT, P)),
                                          rden.rearrange("p (h o) -> p h o", o=1).broadcast_to((P, HPT, P)), ALU.mult))
                dve.wait_ge(ay_loaded, b * (16 * CHUNKS) + 16 * CHUNKS)
                for m in range(KT):
                    t = full_d(D_WO + m)
                    d_free.inc(stt(ay[:, m, :], t, gate[:, 1:2], ay[:, m, :], ALU.mult, ALU.add))
                for c in (d_free, mask_step, arstd_ready, axn_ready, mx_ready, nmx_ready, den_ready, diag_ready):
                    c.close()

        @block.gpsimd
        def _(pool):
            nc.gpsimd.memset(ident[:], 0.0).then_inc(const_ready, 1)
            pool.wait_ge(const_ready, 4)
            nc.gpsimd.affine_select(out=ident[:], in_=ident[:], compare_op=ALU.not_equal, fill=1.0, base=0, pattern=[[-1, P]], channel_multiplier=1).then_inc(const_ready, 1)
            with pool.Fori(0, LAYERS) as layer:
                with pool.Fori(0, CHUNKS) as chunk:
                    it = pool.snap(layer * CHUNKS + chunk)
                    for q in range(STREAMS):
                        for n in range(2):
                            pool.wait_ge(m_free.sem, m_free.at(it, M_MIX + 8 * q + 4 * n + 4))
                            mix_ready.inc(nc.gpsimd.tensor_tensor(half(mix[q % 2], n), half(mix[q % 2], n), half(xa, n)[:, :, :, 1:TC + 1], ALU.add))
                    pool.wait_ge(j_free.sem, j_free.at(it, J_AT["v"] + 8))
                    pool.wait_ge(mix_ready.sem, mix_ready.at(it, 2 * STREAMS))
                    for n in range(2 * S):
                        jh, i = n // S, n % S
                        step = jh * STEPS + i
                        kv_free(pool, it, step)
                        kv_ready.inc(nc.gpsimd.tensor_tensor(kv[step % 4][:, :, 1:TC + 1], hm["v"][:, JH * jh:JH * jh + JH, :], over(hm["k"][:, i, :], JH), ALU.mult))
                    for c in range(2):
                        for m in range(KT):
                            pool.wait_ge(j_free.sem, j_free.at(it, J_WFK + KT * c + m + 1))
                            t = kk[:, m, c * HALF:(c + 1) * HALF]
                            kk_ready.inc(nc.gpsimd.tensor_tensor(t, t, t, ALU.mult))
                    for c in (mix_ready, kv_ready, kk_ready):
                        c.close()


def kernel(**inputs):
    import concourse.bacc as bacc
    from concourse.bass_utils import run_bass_kernel_spmd

    def arr(name):
        return np.asarray(inputs[name])

    def cols(v):
        return np.reshape(v, (KT, P)).T

    def per_head(v):
        return np.tile(np.reshape(v, (H, S)), (B, 1))

    def channel_major(wt):
        n = wt.shape[1]
        return wt.reshape(KT, P, n).transpose(1, 0, 2).reshape(P, KT * n)

    def by_position(wt):
        return wt.reshape(wt.shape[0], H, S).transpose(0, 2, 1).reshape(wt.shape[0], E)

    names = [dict(td1="decay_w1", td2="decay_w2", u="faaaa", fk="ffn_Wk", fr="ffn_Wr", fv="ffn_Wv")] + 2 * [dict(td1="td_w1", td2="td_w2", u="u", fk="Wfk", fr="Wfr", fv="Wfv")]
    small, pars, big = [], [], []
    for n, name in enumerate(names):
        def p(key):
            return arr(f"L{n}_xattn_{name.get(key, key)}")

        stack = p("maa_stack").reshape(STREAMS, E)
        par = [cols(p("ln1_w")), cols(p("ln1_b")), cols(p("maa_x"))] + [cols(stack[s]) for s in range(STREAMS)]
        par += [cols(p("ln2_w")), cols(p("ln2_b")), cols(p("ffn_maa_k")), cols(p("ffn_maa_r"))]
        par += [per_head(p("time_decay")), per_head(p("u").reshape(E)), per_head(p("gn_w")), per_head(p("gn_b"))]
        pars.append(np.concatenate(par, axis=1))
        w2 = np.zeros((P, STREAMS, E), np.float32)
        for f in range(STREAMS):
            row = DM * min(f, 3)
            w2[row:row + DM, f] = p("maa_w2")[f]
        td1, td2 = np.zeros((E, P), np.float32), np.zeros((P, E), np.float32)
        td1[:, :DD], td2[:DD] = p("td1"), by_position(p("td2"))
        small.append(np.concatenate([channel_major(p("maa_w1")), w2.reshape(P, STREAMS * E), channel_major(td1), td2], axis=1))
        big.append(np.stack([channel_major(by_position(p(w).T)) for w in ("Wk", "Wv", "Wr", "Wg")] + [channel_major(p(w).T) for w in ("Wo", "fr", "fk", "fv")]))
    x = arr("x")
    context = arr("ctx_2048")
    mask = arr("mask_BxS2_bf1").view(np.uint8)
    arrays = {
        "x": x.reshape(B, CHUNKS, TC, KT, P).transpose(1, 4, 3, 0, 2).reshape(CHUNKS, P, KT * COLS),
        "rows": context[:, 0:2].reshape(B, 2, KT, P).transpose(3, 1, 2, 0).reshape(P, 2 * KT * B),
        "s_first": context[:, 2:2 + S].reshape(B * H, S * S),
        "small": np.stack(small),
        "pars": np.stack(pars),
        "big": np.stack(big),
        "ctx": context.transpose(0, 2, 1).reshape(B, KT, P, SK).transpose(0, 2, 1, 3).reshape(B, P, KT * SK),
        "mask": mask,
        "at_w": np.stack([channel_major(arr(f"L3_xattn_{w}").T) for w in ("Wq", "Wk", "Wv", "Wo")]),
        "at_ln": np.concatenate([cols(arr("L3_xattn_ln_gamma")), cols(arr("L3_xattn_ln_beta"))], axis=1),
        "gate": np.tile(arr("L3_xattn_gate").reshape(1, 1), (P, 1)),
    }
    arrays = {k: np.ascontiguousarray(v) for k, v in arrays.items()}
    nc = bacc.Bacc("TRN2", target_bir_lowering=False, num_devices=1)
    aps = {k: nc.dram_tensor(f"{k}_dram", v.shape, mybir.dt.from_np(v.dtype), kind="ExternalInput").ap() for k, v in arrays.items()}
    aps["og"] = nc.dram_tensor("og_dram", (B * H, S, TC), F32).ap()
    aps["xs"] = nc.dram_tensor("xs_dram", (CHUNKS, P, KT * COLS), F32).ap()
    aps["out"] = nc.dram_tensor("out_dram", (B, P, KT * T), F32, kind="ExternalOutput").ap()
    build(nc, aps)
    r = run_bass_kernel_spmd(nc, [{f"{k}_dram": v for k, v in arrays.items()}], core_ids=[0])
    out = r.results[0]["out_dram"]
    return np.ascontiguousarray(out.reshape(B, P, KT, T).transpose(0, 3, 2, 1).reshape(B, T, E))
```

```python
from contextlib import ExitStack

import numpy as np
import concourse.bass as bass
from concourse import mybir

F32 = mybir.dt.float32
F32R = mybir.dt.float32r
U8 = mybir.dt.uint8
ALU = mybir.AluOpType
ACT = mybir.ActivationFunctionType
AX_X = mybir.AxisListType.X

P = 128
LAYERS = 3
B, T, E, H = 4, 512, 512, 32
S = E // H
KT = E // P
CHUNKS = 2
TC = T // CHUNKS
COLS = B * TC
HALF = COLS // 2
HB = B // 2
DM, DD = 32, 64
STREAMS = 5
EPS = 1e-5
JH = 8
STEPS = S + 1

AH = 16
AD = E // AH
SK = 1024
ST = SK // P
TT = T // P
HPT = P // AD
SCALE = AD ** -0.5
SQ = SK // 4

LN1W, LN1B, MAAX, PARS1 = 0, 4, 8, 12
MAAS, LN2W, LN2B, FMK, FMR, TDEC, UCOL, GNW, GNB, PARS = 0, 20, 24, 28, 32, 36, 52, 68, 84, 100
W1_AT, W2_AT, TD1_AT, TD2_AT, SMALL = 0, 640, 3200, 3712, 4224
SLOT = KT * E
WK, WV, WR, WG, WO, WFR, WFK, WFV = range(8)
NW = 8
NSLOT = 2
SLOT_LOADS = NW // NSLOT
ORDER = ["k", "v", "r", "w", "g"]
FAN = {"k": 0, "w": 1, "v": 2, "r": 3, "g": 4}

M_MIX, M_ACC, M_MEAN1, M_RSTD1, M_WFV, M_CHUNK = 0, 40, (48, 49, 50, 51), (55, 57), 68, 76
M_WO, M_MEAN2, M_RSTD2 = (52, 53, 54, 56, 58, 61, 62, 64), (59, 60, 65, 66), (63, 67)
J_W1, J_PROJ, J_GSUM, J_GVAR, J_VAR1, J_WFK, J_CHUNK = 0, 3, 45, 46, (49, 50), 61, 69
J_VAR2, J_WFR = (51, 53), (52, 54, 55, 56, 57, 58, 59, 60)
MIX_AHEAD = 12
G_STEPS = (0, 0, 0, 7, 14, 21)
G_OUT = (0, 1, 2, 8, 15, 22)
SET_AT = 5
RING = 4
GQ = 4
J_G = (39, 40, 41, 42, 43, 44, 47, 48)
GN_ORDER = (0, 1, 3, 2)
J_AT = {"k": J_PROJ, "v": J_PROJ + 8, "r": J_PROJ + 16, "td": J_PROJ + 24, "w": J_PROJ + 28}

CONSTS = 5
X_STORED = 16 * (1 + 2 * LAYERS * CHUNKS)
UNITS = KT * TT
Q_PART, K_PART = (0, 0, 1, 1), (0, 1, 0, 1)
A_VAR, A_T, A_PER = 0, 1, 1 + HPT * UNITS
A_HEAD = HPT * UNITS


def projected(step):
    j, part = step // TT, step % TT
    tiles = [("k", j + 1, part)] if part < 2 and j + 1 < KT else []
    return tiles + ([("q", j + 2)] if part == 1 and j + 2 < KT else [])


D_ORDER = [("mean", 0), ("mean", 1), ("q", 0), ("q", 1), ("rstd", 0), ("rstd", 1), ("k", 0, 0), ("k", 0, 1)] + [("v", st) for st in range(ST)]
for _step in range(UNITS + 2):
    D_ORDER += [("out", _step - 2)] if _step >= 2 else []
    D_ORDER += [("t", _step - 1, h) for h in range(HPT)] if 1 <= _step <= UNITS else []
    D_ORDER += projected(_step)
D_ORDER += [("wo", m) for m in range(KT)]
D_AT = {tile: n for n, tile in enumerate(D_ORDER)}
D_PER = len(D_ORDER)


class Count:

    def __init__(self, sem, per, credit=0):
        self.sem, self.per, self.credit, self.n = sem, per, credit, 0

    def inc(self, instruction, by=1):
        self.n += by
        instruction.then_inc(self.sem, by)

    def at(self, turn, n):
        return turn * self.per + (n + self.credit)

    def close(self):
        assert self.n == self.per, (self.sem, self.n, self.per)


def build(nc, a):
    ctx = ExitStack()
    with ctx:
        mem = ctx.enter_context(nc.sbuf_tensor("mem", [P, 4096 * 6], F32))
        psum = ctx.enter_context(nc.psum_tensor("psum", [P, 8, 512], F32))

        def sb(name, shape, dt=F32):
            return ctx.enter_context(nc.sbuf_tensor(name, shape, dt))

        def sem(name):
            return ctx.enter_context(nc.semaphore(name))

        def view(at, pattern=None, size=None, **dims):
            v = mem[:, at:at + size] if at < 4096 * 6 else mem2[:, at - 4096 * 6:at - 4096 * 6 + size]
            return v.rearrange(pattern, **dims) if pattern else v

        small = sb("small", [P, SMALL])
        pars = sb("pars", [P, PARS])
        pars1 = sb("pars1", [P, PARS1])
        lnp = sb("lnp", [P, 2 * KT])
        gate = sb("gate", [P, 2])
        ident = sb("ident", [P, P])
        ones = sb("ones", [P, P])
        pick = sb("pick", [P, B, P])
        eps = sb("eps", [P, 1])
        s_first = sb("s_first", [P, S * S])
        s_now = sb("s_now", [P, S * S])
        edges = sb("edges", [P, 2, 2, KT * B])
        w1 = small[:, W1_AT:W1_AT + 640].rearrange("p (k f) -> p k f", k=KT)
        w2 = small[:, W2_AT:W2_AT + STREAMS * E].rearrange("p (f e) -> p f e", f=STREAMS)
        td1 = small[:, TD1_AT:TD1_AT + KT * P].rearrange("p (k f) -> p k f", k=KT)
        td2 = small[:, TD2_AT:TD2_AT + E].rearrange("p (i h) -> p i h", i=S)

        with nc.sbuf_tensor("mem2", [P, 22840], F32) as mem2:
            pass
        side = ctx.enter_context(nc.sbuf_tensor("side", [P, 3 * 4096], F32))
        rest = ctx.enter_context(nc.sbuf_tensor("rest", [P, 22840 - 3 * 4096], F32))

        x = view(0, "p (k b t) -> p k b t", 4096, k=KT, b=B)
        hm = {s: view(4096 + 4096 * n, "p (i t) -> p i t", 4096, i=S) for n, s in enumerate("krwvg")}
        rr = view(4096 * 2, "p (m c) -> p m c", 4096, m=KT)
        x_new = view(4096 * 2, "p (k b t) -> p k b t", 4096, k=KT, b=B)
        kk = view(4096 * 1, "p (m c) -> p m c", 4096, m=KT)
        th_a = view(4096 * 5, "p (b t) -> p b t", COLS, b=B)
        th_b = view(4096 * 5 + COLS, None, COLS)
        tdh = view(4096 * 5 + 2 * COLS, None, COLS)
        xl = view(4096 * 3, "p (k b t) -> p k b t", 4096, k=KT, b=B)
        xl_sq = view(4096 * 1, "p (k b t) -> p k b t", 4096, k=KT, b=B)
        A = 4096 * 6
        xa = view(A, "p (k b t) -> p k b t", KT * B * (TC + 1), k=KT, b=B)
        sx = view(A + 4112, "p (k b t) -> p k b t", 4096, k=KT, b=B)
        mix = [view(A + at, "p (k b t) -> p k b t", 4096, k=KT, b=B) for at in (12336, 8224)]
        ROW = JH * (TC + 1)
        kv_flat = [view(A + ROW * n, None, ROW) for n in range(4)]
        s_flat = view(A + 8224, None, ROW)
        wt_flat = [view(A + at, None, ROW) for at in (10280, 16688)]
        kv = [t.rearrange("p (j t) -> p j t", j=JH) for t in kv_flat]
        s_ext = s_flat.rearrange("p (j t) -> p j t", j=JH)
        wt = [t.rearrange("p (j t) -> p j t", j=JH) for t in wt_flat]
        kr2 = view(A + 16688, "p (i t) -> p i t", JH * TC, i=JH)
        ruk = view(A + 16432, None, TC)
        ruk2 = view(4096 * 5 + 3 * COLS, "p (n t) -> p n t", 2 * TC, n=2)
        std = [ruk, view(A + 16688, None, TC)]
        att = hm["v"]
        gd = view(A, "p (j t) -> p j t", 4096, j=S)
        gsq = view(A + 4096, "p (j t) -> p j t", 4096, j=S)
        ogc = view(A + 4096, "p (k b t) -> p k b t", 4096, k=KT, b=B)
        gsum = view(A + 8224, None, TC)
        gstd = view(A + 8224 + TC, None, TC)
        R = A + 18744
        ring = [view(R + SLOT * n, None, SLOT) for n in range(NSLOT)]

        def par(at, n=0):
            return pars[:, at + n:at + n + 1]

        def par1(at, n=0):
            return pars1[:, at + n:at + n + 1]

        def bank_m(n):
            return psum[:, n % RING, :]

        def bank_j(n):
            return psum[:, RING + n % RING, :]

        const_ready = sem("const_ready")
        state_loaded = sem("state_loaded")
        small_loaded = sem("small_loaded")
        pars_loaded = sem("pars_loaded")
        pars1_loaded = sem("pars1_loaded")
        xl_loaded = [sem(f"xl_loaded{n}") for n in range(2)]
        x_loaded = [sem(f"x_loaded{n}") for n in range(2)]
        og_stored = sem("og_stored")
        og_loaded = [sem(f"og_loaded{n}") for n in range(2)]
        x_stored = sem("x_stored")
        slot_loaded = [sem(f"slot_loaded{n}") for n in range(NSLOT)]
        m_full = Count(sem("m_full"), M_CHUNK, M_CHUNK)
        m_free = Count(sem("m_free"), M_CHUNK, RING)
        j_full = Count(sem("j_full"), J_CHUNK, J_CHUNK)
        j_free = Count(sem("j_free"), J_CHUNK, RING)
        layer_set = sem("layer_set")
        edge_set = Count(sem("edge_set"), 2)
        edge_kept = Count(sem("edge_kept"), 2, 1)
        sq_ready = Count(sem("sq_ready"), 4)
        rstd_ready = Count(sem("rstd_ready"), 4)
        xn_ready = Count(sem("xn_ready"), 4 * (KT - 1))
        xa_ready = Count(sem("xa_ready"), 4 * KT)
        sx_ready = Count(sem("sx_ready"), 4 * KT)
        lmix_ready = Count(sem("lmix_ready"), 2)
        mix_ready = Count(sem("mix_ready"), 2 * STREAMS)
        w_ready = Count(sem("w_ready"), 8)
        ruk_step = Count(sem("ruk_step"), 7)
        own_ready = Count(sem("own_ready"), 1)
        th_zero = Count(sem("th_zero"), 1)
        kv_ready = Count(sem("kv_ready"), 2 * S)
        scan_set = Count(sem("scan_set"), 2 * S)
        scan_ready = Count(sem("scan_ready"), 2 * S)
        s_saved = Count(sem("s_saved"), 2 * S, 1)
        rs_ready = Count(sem("rs_ready"), 2 * STEPS - 1)
        acc_done = Count(sem("acc_done"), 2 * S)
        gn_step = Count(sem("gn_step"), 1 + 2 * GQ)
        gn_act = Count(sem("gn_act"), 2 * GQ - 1)
        og_ready = Count(sem("og_ready"), GQ)
        fmix_ready = Count(sem("fmix_ready"), 4)
        kk_ready = Count(sem("kk_ready"), 8)
        x_done = Count(sem("x_done"), 2)
        first_m_full = Count(sem("first_m_full"), 6)
        first_m_free = Count(sem("first_m_free"), 6, RING)
        first_j_full = Count(sem("first_j_full"), 2)
        first_j_free = Count(sem("first_j_free"), 2, RING)
        first_sq = Count(sem("first_sq"), 2)
        first_rstd = Count(sem("first_rstd"), 2)
        first_xn = Count(sem("first_xn"), 2 * (KT - 1))
        first_xa = Count(sem("first_xa"), 2 * KT)
        first_sx = Count(sem("first_sx"), 2 * KT)
        j_end = {s: J_AT[s] + 8 for s in ORDER[:STREAMS - 2]}
        used_by = [(j_full, J_AT["k"] + 8), (j_full, J_AT["v"] + 8), (j_full, J_AT["r"] + 8), (j_full, J_G[-1] + 1),
                   (m_full, M_WO[-1] + 1), (j_full, J_WFR[-1] + 1), (j_full, J_WFK + 8), (m_full, M_WFV + 8)]

        class Norm:

            def __init__(self, turn, m, j, halves, channels, tiles, halves0, channels0, src, diff, squares):
                self.turn, self.src, self.diff, self.squares = turn, src, diff, squares
                self.m_full, self.m_free = m
                self.j_full, self.j_free = j
                self.sq, self.rstd = halves
                self.xn, self.xa, self.sx = channels
                self.mean, self.spread, self.var = tiles
                self.halves0, self.channels0 = halves0, channels0

            def half_at(self, n):
                return self.halves0 + n + 1

            def channel_at(self, n, k):
                return self.channels0 + KT * n + k + 1

            def xn_at(self, n, k):
                return self.halves0 * (KT - 1) + (KT - 1) * n + k + 1

        def norm1(it):
            return Norm(it, (m_full, m_free), (j_full, j_free), (sq_ready, rstd_ready), (xn_ready, xa_ready, sx_ready), (M_MEAN1, M_RSTD1, J_VAR1),
                        0, 2 * KT, xl, xl, xl_sq)

        def norm2(it):
            return Norm(it, (m_full, m_free), (j_full, j_free), (sq_ready, rstd_ready), (xn_ready, xa_ready, sx_ready), (M_MEAN2, M_RSTD2, J_VAR2),
                        2, 0, x, mix[0], mix[1])

        def norm_first():
            return Norm(0, (first_m_full, first_m_free), (first_j_full, first_j_free), (first_sq, first_rstd), (first_xn, first_xa, first_sx),
                        ((0, 1, 2, 3), (4, 5), (0, 1)), 0, 0, xl, xl, xl_sq)

        at_w = [view(4096 * 4 + SLOT * n, "p (k e) -> p k e", SLOT, k=KT) for n in range(4)]
        an = view(4096 * 3, "p (k s) -> p k s", 4096, k=KT)
        vals = view(0, "p (s e) -> p s e", 4096, s=ST)
        k_part = [view(4096 + SK * n, None, SK) for n in range(2)]
        q_part = [[view(4096 + 2 * SK + T * (2 * e + n), None, T) for n in range(2)] for e in range(2)]
        k_side = [side[:, 4096 * n:4096 * n + 4096].rearrange("p (h s) -> p h s", h=HPT) for n in range(2)]
        q_side = [side[:, 8192 + 2048 * n:10240 + 2048 * n].rearrange("p (h t) -> p h t", h=HPT) for n in range(2)]
        ay = view(A, "p (k t) -> p k t", 2048, k=KT)
        probs = [view(A + 12288 + 4096 * n, "p (h s) -> p h s", 4096, h=HPT) for n in range(2)]
        asq = view(A + 12288, "p (k s) -> p k s", 4096, k=KT)
        probs_t = view(8192, "p (s h t) -> p s h t", 4096, s=ST, h=HPT)
        Q1 = A + 20480
        mbias = view(Q1, None, SK)
        diag = view(Q1 + 1024, "p (h t) -> p h t", HPT * P, h=HPT)
        astd = view(Q1 + 1536, None, SQ)
        mask_u = view(Q1 + 1792, None, SK // 4).bitcast(U8)
        mx = view(Q1 + 2048, "p (n h) -> p n h", 2 * HPT, n=2)
        nmx = view(Q1 + 2056, "p (n h) -> p n h", 2 * HPT, n=2)
        den = view(Q1 + 2064, "p (n h) -> p n h", 2 * HPT, n=2)
        rden = view(Q1 + 2072, None, HPT)
        xq = small[:, 0:2048].rearrange("p (k t) -> p k t", k=KT)
        ao = small[:, 2048:4096].rearrange("p (k t) -> p k t", k=KT)

        at_loaded = sem("at_loaded")
        cx_loaded = sem("cx_loaded")
        xq_loaded = sem("xq_loaded")
        ay_loaded = sem("ay_loaded")
        mask_loaded = sem("mask_loaded")
        out_stored = sem("out_stored")
        part_ready = Count(sem("part_ready"), 3 * KT)
        side_loaded = [sem(f"side_loaded{n}") for n in range(2)]
        gate_ready = sem("gate_ready")
        max_turn = sem("max_turn")
        a_full = Count(sem("a_full"), A_PER)
        a_free = Count(sem("a_free"), A_PER, 2)
        d_full = Count(sem("d_full"), D_PER)
        d_free = Count(sem("d_free"), D_PER, 2)
        s_full = Count(sem("s_full"), A_HEAD)
        s_free = Count(sem("s_free"), A_HEAD, 2)
        mask_step = Count(sem("mask_step"), 2)
        asq_ready = Count(sem("asq_ready"), 2)
        arstd_ready = Count(sem("arstd_ready"), 1)
        an_ready = Count(sem("an_ready"), 2)
        mx_ready = Count(sem("mx_ready"), A_HEAD)
        nmx_ready = Count(sem("nmx_ready"), A_HEAD)
        den_ready = Count(sem("den_ready"), UNITS)
        diag_ready = Count(sem("diag_ready"), UNITS)

        def bank_a(n):
            return psum[:, 4 + n % 2, :]

        def bank_d(n):
            return psum[:, 6 + n % 2, :]

        def banks_s(n):
            return psum[:, 2 * (n % 2):2 * (n % 2) + 2, :]

        part_order = [tile for tile in D_ORDER if tile[0] in "kq"]

        def part(tile, n):
            if tile[0] == "k":
                return k_part[n][:, tile[2] * 512:tile[2] * 512 + 512]
            return q_part[tile[1] % 2][n]

        def sides(b, e):
            return b * (16 * 2 * HPT * HPT * (KT // 2)) + 16 * 2 * HPT * HPT * (e // 2 + 1)

        def half(t, n):
            return t[:, :, HB * n:HB * n + HB, :]

        def half2(t, n):
            return half(t, n).rearrange("p k b t -> p k (b t)")

        def over(t, n):
            return t.rearrange("p (o c) -> p o c", o=1).broadcast_to((P, n, t.shape[1]))

        def scan_step(n):
            return n // S * STEPS + n % S + (n == 2 * S - 1)

        def kv_free(engine, it, step):
            if step >= 4:
                jh, n = (step - 4) // STEPS, (step - 4) % STEPS
                if n == S:
                    engine.wait_ge(m_full.sem, m_full.at(it, M_ACC + RING * jh + RING))
                else:
                    engine.wait_ge(acc_done.sem, acc_done.at(it, jh * S + n + 1))

        block = ctx.enter_context(nc.Block())

        @block.sync
        def _(sp):
            sp.dma_start(s_first[:], a["s_first"]).then_inc(state_loaded, 16)
            sp.dma_start(edges[:, :, 0, :], a["rows"].rearrange("p (r c) -> p r c", r=2)).then_inc(state_loaded, 16)
            sp.dma_start(pars1[:], a["pars1"][0]).then_inc(pars1_loaded, 16)

            def x_half(to, chunk, n):
                return to[chunk].rearrange("p (k b t) -> p k b t", k=KT, b=B)[:, :, HB * n:HB * n + HB, :]

            for n in range(2):
                sp.dma_start(half(xl, n), x_half(a["x"], 0, n)).then_inc(xl_loaded[n], 16)
            sp.dma_start(small[:], a["small"][0]).then_inc(small_loaded, 16)
            sp.dma_start(pars[:], a["pars"][0]).then_inc(pars_loaded, 16)
            for n in range(2):
                sp.dma_start(half(x, n), x_half(a["x"], 0, n)).then_inc(x_loaded[n], 16)
            sp.dma_start(a["xs"][1], a["x"][1]).then_inc(x_stored, 16)

            def load_context(b):
                sp.dma_start(an.rearrange("p k s -> p (k s)"), a["ctx"][bass.ds(b, 1), :, :].rearrange("o p n -> (o p) n")).then_inc(cx_loaded, 16)

            def load_mask(b):
                sp.dma_start(mask_u, a["mask"][bass.ds(b, 1), :].broadcast_to((P, SK))).then_inc(mask_loaded, 16)

            def layer_traffic(layer, last):
                after = None if last else sp.snap(layer + 1)
                for chunk in range(CHUNKS):
                    it = layer * CHUNKS + chunk if last else sp.snap(layer * CHUNKS + chunk)

                    def load_weight(n):
                        tiles, end = used_by[n - NSLOT] if n >= NSLOT else used_by[n - NSLOT + NW]
                        sp.wait_ge(tiles.sem, tiles.at(it, end if n >= NSLOT else end - tiles.per))
                        src = a["big"][layer, n] if last else a["big"][bass.ds(layer, 1), n, :, :].rearrange("o p n -> (o p) n")
                        sp.dma_start(ring[n % NSLOT], src).then_inc(slot_loaded[n % NSLOT], 16)

                    if chunk == CHUNKS - 1:
                        sp.wait_ge(lmix_ready.sem, lmix_ready.at(it, 2))
                        if last:
                            sp.sem_inc(pars1_loaded, 16)
                        else:
                            sp.dma_start(pars1[:], a["pars1"][bass.ds(after, 1), :, :].rearrange("o p n -> (o p) n")).then_inc(pars1_loaded, 16)
                    for n in range(WO + 1):
                        load_weight(n)
                        if n == WG and chunk == CHUNKS - 1 and not last:
                            sp.wait_ge(j_full.sem, j_full.at(it, J_AT["w"] + 8))
                            sp.dma_start(small[:], a["small"][bass.ds(after, 1), :, :].rearrange("o p n -> (o p) n")).then_inc(small_loaded, 16)
                    sp.wait_ge(scan_set.sem, scan_set.at(it, 2 * S))
                    for n in range(2):
                        sp.dma_start(half(xl, n), x_half(a["xs"], 1 - chunk, n)).then_inc(xl_loaded[n], 16)
                    for n in range(GQ):
                        sp.wait_ge(og_ready.sem, og_ready.at(it, n + 1))
                        j = slice(S // GQ * GN_ORDER[n], S // GQ * (GN_ORDER[n] + 1))
                        sp.dma_start(a["og"][:, j, :], att[:, j, :]).then_inc(og_stored, 16)
                    sp.wait_ge(og_stored, it * (16 * GQ) + 16 * GQ)
                    for b in range(B):
                        sp.dma_start(ogc[:, :, b, :], a["og"].rearrange("(b k h) j t -> b (h j) k t", b=B, k=KT)[b]).then_inc(og_loaded[b // HB], 16)
                    for n in (WFR, WFK, WFV):
                        load_weight(n)
                    if chunk == CHUNKS - 1 and not last:
                        sp.wait_ge(fmix_ready.sem, fmix_ready.at(it, 4))
                        sp.dma_start(pars[:], a["pars"][bass.ds(after, 1), :, :].rearrange("o p n -> (o p) n")).then_inc(pars_loaded, 16)
                    if chunk == CHUNKS - 1 and last:
                        sp.wait_ge(xa_ready.sem, xa_ready.at(it, xa_ready.per))
                        sp.wait_ge(og_loaded[1], (it + 1) * (16 * HB))
                        for n in range(4):
                            sp.dma_start(at_w[n].rearrange("p k e -> p (k e)"), a["at_w"][n]).then_inc(at_loaded, 16)
                        sp.dma_start(lnp[:], a["at_ln"]).then_inc(at_loaded, 16)
                        sp.dma_start(gate[:, 0:1], a["gate"]).then_inc(at_loaded, 16)
                        load_context(0)
                    for n in range(2):
                        sp.wait_ge(x_done.sem, x_done.at(it, n + 1))
                        sp.dma_start(x_half(a["xs"], chunk, n), half(x_new, n)).then_inc(x_stored, 16)
                        if not (last and chunk == CHUNKS - 1):
                            sp.dma_start(half(x, n), x_half(a["xs"], 1 - chunk, n)).then_inc(x_loaded[n], 16)

            with sp.Fori(0, LAYERS - 1) as layer:
                layer_traffic(layer, False)
            layer_traffic(LAYERS - 1, True)
            sp.wait_ge(x_stored, X_STORED)
            def load_x(to, b, loaded):
                for c in range(CHUNKS):
                    sp.dma_start(to[:, :, c * TC:(c + 1) * TC],
                                 a["xs"][c].rearrange("p (k b t) -> p k b t", k=KT, b=B)[:, :, bass.ds(b, 1), :].rearrange("p k o t -> p k (o t)")).then_inc(loaded, 16)

            load_x(xq, 0, xq_loaded)
            load_mask(0)
            sp.sem_inc(out_stored, 16)

            def side_by_side(b, e):
                sp.wait_ge(d_free.sem, d_free.at(b, D_AT["k", e, 1] + 1))
                for g in range(HPT):
                    for h in range(HPT):
                        to, of = slice(AD * g, AD * g + AD), slice(AD * h, AD * h + AD)
                        sp.dma_start(k_side[e % 2][to, h, :], k_part[K_PART[g]][of, :]).then_inc(side_loaded[e % 2], 16)
                        sp.dma_start(q_side[e % 2][to, h, :], q_part[e % 2][Q_PART[g]][of, :]).then_inc(side_loaded[e % 2], 16)

            def batch_traffic(b, last):
                after = None if last else sp.snap(b + 1)
                sp.wait_ge(out_stored, b * 16 + 16)
                for e in range(KT):
                    side_by_side(b, e)
                    if e == KT - 2 and not last:
                        sp.wait_ge(d_free.sem, d_free.at(b, D_AT["q", KT - 1] + 1))
                        load_x(xq, after, xq_loaded)
                if not last:
                    load_context(after)
                    load_mask(after)
                sp.wait_ge(s_full.sem, s_full.at(b, HPT * TT * (KT - 1)))
                load_x(ay, b, ay_loaded)
                sp.wait_ge(d_free.sem, d_free.at(b, D_PER))
                sp.dma_start(a["out"][bass.ds(b, 1), :, :].rearrange("o p n -> (o p) n"), ay.rearrange("p k t -> p (k t)")).then_inc(out_stored, 16)

            with sp.Fori(0, B - 1) as b:
                batch_traffic(b, False)
            batch_traffic(B - 1, True)
            sp.wait_ge(out_stored, 16 * (B + 1))

        @block.tensor
        def _(pe):
            mm = nc.tensor.matmul
            pe.sem_inc(m_full.sem, m_full.credit)
            pe.sem_inc(j_full.sem, j_full.credit)
            pe.wait_ge(const_ready, CONSTS)

            def norm_tile(norm, n):
                pe.wait_ge(norm.m_free.sem, norm.m_free.at(norm.turn, n + 1 - RING))
                return bank_m(n)

            def means(norm, n):
                for b in range(HB * n, HB * n + HB):
                    t = norm_tile(norm, norm.mean[b])
                    for k in range(KT):
                        last = mm(t[:, 0:TC], ones[:], norm.src[:, k, b, :], start=k == 0, stop=k == KT - 1)
                    norm.m_full.inc(last)

            def variances(norm, n):
                pe.wait_ge(norm.sq.sem, norm.sq.at(norm.turn, norm.half_at(n)))
                pe.wait_ge(norm.j_free.sem, norm.j_free.at(norm.turn, norm.var[n] + 1 - RING))
                t = bank_j(norm.var[n])
                for k in range(KT):
                    for q in range(P // H):
                        last = mm(t[H * q:H * q + H, 0:TC], ones[:, 0:H], norm.squares[:, k, HB * n + q % HB, :], start=k == 0, stop=k == KT - 1, skip_group_check=True)
                norm.j_full.inc(last)

            def spread(norm, n):
                pe.wait_ge(norm.rstd.sem, norm.rstd.at(norm.turn, norm.half_at(n)))
                t = norm_tile(norm, norm.spread[n])
                for o in range(HB):
                    last = mm(t[:, o * TC:(o + 1) * TC], pick[:, o, :], std[n], start=True, stop=True, skip_group_check=True)
                norm.m_full.inc(last)

            norm = norm_first()
            for n in range(2):
                pe.wait_ge(xl_loaded[n], 16)
                means(norm, n)
            for n in range(2):
                variances(norm, n)
            for n in range(2):
                spread(norm, n)
            with pe.Fori(0, LAYERS) as layer:
                with pe.Fori(0, CHUNKS) as chunk:
                    it = pe.snap(layer * CHUNKS + chunk)

                    def tile_m(n):
                        pe.wait_ge(m_free.sem, m_free.at(it, n + 1 - RING))
                        return bank_m(n)

                    def tile_j(n):
                        pe.wait_ge(j_free.sem, j_free.at(it, n + 1 - RING))
                        return bank_j(n)

                    def weight(n):
                        pe.wait_ge(slot_loaded[n % NSLOT], it * (16 * SLOT_LOADS) + 16 * (n // NSLOT + 1))
                        return ring[n % NSLOT]

                    pe.wait_ge(small_loaded, layer * 16 + 16)
                    def first_factor(n):
                        pe.wait_ge(lmix_ready.sem, lmix_ready.at(it, n + 1))
                        t = tile_j(J_W1 + 1 + n)
                        for k in range(KT):
                            last = mm(t, w1[:, k, 0:P], half2(mix[1], n)[:, k, :], start=k == 0, stop=k == KT - 1)
                        j_full.inc(last)

                    def second_factor(q, n, k):
                        f = FAN[ORDER[q]]
                        if k == 0 and q < 2:
                            pe.wait_ge(j_free.sem, j_free.at(it, J_W1 + 2 + n if q else J_W1 + 1))
                        t = tile_m(M_MIX + 8 * q + 4 * n + k)
                        th = th_b[:, n * HALF:(n + 1) * HALF] if q else th_a[:, HB * n:HB * n + HB, :]
                        m_full.inc(mm(t, w2[:, f, P * k:P * k + P], th, start=True, stop=True))

                    def second_factors(first, end):
                        for n in range(first, end):
                            second_factor(n // 8, n % 8 // KT, n % KT)

                    pe.wait_ge(lmix_ready.sem, lmix_ready.at(it, 2))
                    t = tile_j(J_W1)
                    for k in range(KT):
                        for b in range(B):
                            last = mm(t[DM * b:DM * b + DM, 0:TC], w1[:, k, P:], mix[1][:, k, b, :], start=k == 0, stop=k == KT - 1, skip_group_check=True)
                    j_full.inc(last)
                    first_factor(0)
                    second_factors(0, KT)
                    first_factor(1)
                    second_factors(KT, MIX_AHEAD)

                    def project(q, s, pair):
                        t = tile_j(J_G[pair] if s == "g" else J_AT[s] + pair)
                        for o in range(2):
                            i, cols = 2 * pair + o, slice(o * TC, (o + 1) * TC)
                            if s == "w":
                                for b in range(B):
                                    last = mm(t[H * b:H * b + H, cols], td2[:, i, :], tdh[:, b * TC:(b + 1) * TC], start=True, stop=True)
                            else:
                                for k in range(KT):
                                    for b in range(B):
                                        last = mm(t[H * b:H * b + H, cols], w[:, k, i, :], mix[q % 2][:, k, b, :], start=k == 0, stop=k == KT - 1,
                                                  skip_group_check=True)
                        j_full.inc(last)

                    for q, s in enumerate(ORDER):
                        pe.wait_ge(mix_ready.sem, mix_ready.at(it, 2 * q + 2))
                        if s == "w":
                            for b in range(B):
                                t = tile_j(J_AT["td"] + b)
                                for k in range(KT):
                                    last = mm(t[:, 0:TC], td1[:, k, :], mix[q % 2][:, k, b, :], start=k == 0, stop=k == KT - 1)
                                j_full.inc(last)
                                ahead = MIX_AHEAD + 8 * q + b
                                second_factors(ahead, ahead + 1)
                        else:
                            w = weight({"k": WK, "v": WV, "r": WR, "g": WG}[s]).rearrange("p (k i h) -> p k i h", k=KT, i=S)
                        for pair in range(S // 2 if s != "g" else 0):
                            if s == "w" and pair == 0:
                                pe.wait_ge(j_free.sem, j_free.at(it, J_AT["td"] + 4))
                            project(q, s, pair)
                            if q < ORDER.index("w"):
                                ahead = MIX_AHEAD + 8 * q + pair
                                second_factors(ahead, ahead + 1)

                    def position_sums(jh):
                        for j in range(JH * jh, JH * jh + JH):
                            if j % 2 == 0:
                                pe.wait_ge(m_free.sem, m_free.at(it, M_ACC + j // 2 + 1))
                            last = mm(bank_j(J_GSUM)[:, 0:TC], ident[:], att[:, j, :], start=j == 0, stop=j == S - 1, skip_group_check=True)
                        if jh == 1:
                            j_full.inc(last)

                    for jh in range(2):
                        tile_m(M_ACC + RING * jh + RING - 1)
                        for n in range(STEPS):
                            step = jh * STEPS + n
                            for pair in range(len(G_STEPS)):
                                if G_STEPS[pair] == step:
                                    project(STREAMS - 1, "g", pair)
                            if step == 2 * STEPS - 9:
                                tile_j(J_GSUM)
                                position_sums(0)
                            if step == 2 * STEPS - 2:
                                pe.wait_ge(own_ready.sem, own_ready.at(it, 1))
                            else:
                                pe.wait_ge(rs_ready.sem, rs_ready.at(it, min(step + 1, 2 * STEPS - 1)))
                            for c in range(RING):
                                last = mm(bank_m(M_ACC + RING * jh + c), ident[:], kv[step % 4][:, 2 * c:2 * c + 2, 0:TC], start=n == 0, stop=n == STEPS - 1)
                                if n == STEPS - 1:
                                    m_full.inc(last)
                            if n < STEPS - 1:
                                acc_done.inc(last)

                    norm = norm1(it)
                    position_sums(1)
                    pe.wait_ge(xl_loaded[0], it * 16 + 32)
                    means(norm, 0)
                    t = tile_j(J_GVAR)
                    for n in range(GQ):
                        pe.wait_ge(gn_act.sem, gn_act.at(it, n + 1))
                        for j in range(S // GQ * n, S // GQ * (n + 1)):
                            last = mm(t[:, 0:TC], ident[:], gsq[:, j, :], start=j == 0, stop=j == S - 1)
                    j_full.inc(last)
                    for pair in range(len(G_STEPS), S // 2):
                        project(STREAMS - 1, "g", pair)
                    pe.wait_ge(xl_loaded[1], it * 16 + 32)
                    means(norm, 1)

                    wo_l = weight(WO).rearrange("p (k e) -> p k e", k=KT)

                    def output(n):
                        c, m = n // KT, n % KT
                        if m == 0:
                            pe.wait_ge(og_loaded[c], it * (16 * HB) + 16 * HB)
                        t = tile_m(M_WO[n])
                        for k in range(KT):
                            last = mm(t, wo_l[:, k, P * m:P * m + P], half2(ogc, c)[:, k, :], start=k == 0, stop=k == KT - 1)
                        m_full.inc(last)

                    output(0)
                    variances(norm, 0)
                    output(1)
                    variances(norm, 1)
                    output(2)
                    spread(norm, 0)
                    output(3)
                    spread(norm, 1)
                    output(4)
                    norm = norm2(it)
                    pe.wait_ge(m_free.sem, m_free.at(it, M_WO[KT - 1] + 1))
                    means(norm, 0)
                    output(KT + 1)
                    variances(norm, 0)
                    output(KT + 2)
                    spread(norm, 0)
                    output(KT + 3)
                    pe.wait_ge(m_free.sem, m_free.at(it, M_WO[2 * KT - 1] + 1))
                    means(norm, 1)
                    wr, wk = weight(WFR), weight(WFK)
                    for n, (w, tiles) in enumerate(((wr, J_WFR), (wk, range(J_WFK, J_WFK + 8)))):
                        w = w.rearrange("p (k e) -> p k e", k=KT)
                        for c in range(2):
                            pe.wait_ge(fmix_ready.sem, fmix_ready.at(it, 2 * n + c + 1))
                            for m in range(KT):
                                if n == 0 and c == 0 and m == 1:
                                    variances(norm, 1)
                                if n == 0 and c == 0 and m == 2:
                                    spread(norm, 1)
                                t = tile_j(tiles[KT * c + m])
                                for k in range(KT):
                                    last = mm(t, w[:, k, P * m:P * m + P], half2(mix[n], c)[:, k, :], start=k == 0, stop=k == KT - 1)
                                j_full.inc(last)
                    w = weight(WFV).rearrange("p (k e) -> p k e", k=KT)
                    for c in range(2):
                        pe.wait_ge(kk_ready.sem, kk_ready.at(it, KT * c + KT))
                        for m in range(KT):
                            t = tile_m(M_WFV + KT * c + m)
                            for k in range(KT):
                                last = mm(t, w[:, k, P * m:P * m + P], kk[:, k, c * HALF:(c + 1) * HALF], start=k == 0, stop=k == KT - 1)
                            m_full.inc(last)
                    for c in (m_full, j_full, acc_done):
                        c.close()

            wq, wk, wv, wo = at_w
            pe.wait_ge(at_loaded, 6 * 16)
            with pe.Fori(0, B) as b:
                def tile_d(n):
                    pe.wait_ge(d_free.sem, d_free.at(b, n + 1 - 2))
                    return bank_d(n)

                def tile_a(n):
                    pe.wait_ge(a_free.sem, a_free.at(b, n + 1 - 2))
                    return bank_a(n)

                pe.wait_ge(cx_loaded, b * 16 + 16)
                for sh in range(2):
                    t = tile_d(D_AT["mean", sh])
                    for k in range(KT):
                        last = mm(t, ones[:], an[:, k, sh * 512:sh * 512 + 512], start=k == 0, stop=k == KT - 1)
                    d_full.inc(last)
                def project_tile(tile):
                    t = tile_d(D_AT[tile])
                    e = tile[1]
                    for k in range(KT):
                        if tile[0] == "k":
                            last = mm(t, wk[:, k, P * e:P * e + P], an[:, k, tile[2] * 512:tile[2] * 512 + 512], start=k == 0, stop=k == KT - 1)
                        else:
                            last = mm(t, wq[:, k, P * e:P * e + P], xq[:, k, :], start=k == 0, stop=k == KT - 1)
                    d_full.inc(last)

                pe.wait_ge(xq_loaded, b * (16 * CHUNKS) + 16 * CHUNKS)
                project_tile(("q", 0))
                pe.wait_ge(asq_ready.sem, asq_ready.at(b, 2))
                t = tile_a(A_VAR)
                for k in range(KT):
                    for c in range(4):
                        last = mm(t[AD * c:AD * c + AD, 0:SQ], ones[:, 0:AD], asq[:, k, c * SQ:c * SQ + SQ], start=k == 0, stop=k == KT - 1, skip_group_check=True)
                a_full.inc(last)
                project_tile(("q", 1))
                pe.wait_ge(arstd_ready.sem, arstd_ready.at(b, 1))
                for sh in range(2):
                    t = tile_d(D_AT["rstd", sh])
                    for o in range(2):
                        last = mm(t[:, o * SQ:o * SQ + SQ], pick[:, 2 * sh + o, :], astd, start=True, stop=True, skip_group_check=True)
                    d_full.inc(last)
                for sh in range(2):
                    pe.wait_ge(an_ready.sem, an_ready.at(b, sh + 1))
                    project_tile(("k", 0, sh))
                for st in range(ST):
                    t = tile_d(D_AT["v", st])
                    for k in range(KT):
                        last = mm(t, an[:, k, P * st:P * st + P], wv[:, k, :], start=k == 0, stop=k == KT - 1)
                    d_full.inc(last)

                def scores(u, h):
                    e, q = u // TT, u % TT
                    if q == 0 and h == 0:
                        pe.wait_ge(side_loaded[e % 2], sides(b, e))
                    pe.wait_ge(s_free.sem, s_free.at(b, HPT * u + h + 1 - 2))
                    t = banks_s(HPT * u + h)
                    for sh in range(2):
                        last = mm(t[:, sh, :], q_side[e % 2][:, h, P * q:P * q + P].bitcast(F32R), k_side[e % 2][:, h, sh * 512:sh * 512 + 512].bitcast(F32R),
                                  start=True, stop=True)
                    s_full.inc(last)

                def transposed(u, h):
                    if h == 0:
                        pe.wait_ge(diag_ready.sem, diag_ready.at(b, u + 1))
                    for n, (t, full) in enumerate(((tile_a(A_T + HPT * u + h), a_full), (None, d_full))):
                        if n == 1:
                            t = tile_d(D_AT["t", u, h])
                        for o in range(4):
                            st = 4 * n + o
                            last = mm(t[:, P * o:P * o + P], probs[u % 2][:, h, P * st:P * st + P], diag[:, h, :], start=True, stop=True, skip_group_check=True)
                        full.inc(last)

                def weighted(u):
                    pe.wait_ge(a_free.sem, a_free.at(b, A_T + HPT * u + HPT))
                    t = tile_d(D_AT["out", u])
                    pe.wait_ge(d_free.sem, d_free.at(b, D_AT["t", u, HPT - 1] + 1))
                    e = u // TT
                    for st in range(ST):
                        for h in range(HPT):
                            last = mm(t[AD * h:AD * h + AD, 0:P], vals[:, st, (HPT * e + h) * AD:(HPT * e + h + 1) * AD], probs_t[:, st, h, :],
                                      start=st == 0, stop=st == ST - 1, skip_group_check=True)
                    d_full.inc(last)

                for step in range(UNITS + 2):
                    for h in range(HPT):
                        if step < UNITS:
                            scores(step, h)
                        if h == 0 and step >= 2:
                            weighted(step - 2)
                        if 1 <= step <= UNITS:
                            transposed(step - 1, h)
                    for tile in projected(step):
                        project_tile(tile)
                pe.wait_ge(d_free.sem, d_free.at(b, D_AT["wo", 0]))
                for m in range(KT):
                    t = tile_d(D_AT["wo", m])
                    for k in range(KT):
                        last = mm(t, wo[:, k, P * m:P * m + P], ao[:, k, :], start=k == 0, stop=k == KT - 1)
                    d_full.inc(last)
                for c in (a_full, d_full, s_full):
                    c.close()

        @block.scalar
        def _(act):
            f = nc.scalar.activation
            act.sem_inc(j_free.sem, j_free.credit)
            act.sem_inc(first_j_free.sem, first_j_free.credit)
            act.sem_inc(s_saved.sem, s_saved.credit)
            act.wait_ge(state_loaded, 32)
            act.wait_ge(const_ready, CONSTS)
            s_at = s_now[:].rearrange("p (i j) -> p i j", i=S)

            def squares(norm, n):
                act.wait_ge(norm.m_free.sem, norm.m_free.at(norm.turn, norm.mean[HB * n + HB - 1] + 1))
                norm.sq.inc(f(half2(norm.squares, n), half2(norm.diff, n), ACT.Square))

            def deviations(norm, n):
                act.wait_ge(norm.j_full.sem, norm.j_full.at(norm.turn, norm.var[n] + 1))
                norm.j_free.inc(f(std[n], bank_j(norm.var[n])[:, 0:TC], ACT.Sqrt, bias=eps[:]))

            def edge(which, slot):
                return edges[:, which, bass.ds(slot, 1), :].rearrange("p s (k b o) -> p (s k) b o", k=KT, o=1)

            def affine(norm, n, scale, bias):
                for k in range(KT):
                    if k < KT - 1:
                        act.wait_ge(norm.xn.sem, norm.xn.at(norm.turn, norm.xn_at(n, k)))
                    else:
                        act.wait_ge(norm.m_free.sem, norm.m_free.at(norm.turn, norm.spread[n] + 1))
                    norm.xa.inc(f(xa[:, k, HB * n:HB * n + HB, 1:TC + 1], norm.diff[:, k, HB * n:HB * n + HB, :], ACT.Identity, scale=scale(k), bias=bias(k)))

            def keep_edge(norm, which):
                act.wait_ge(norm.xa.sem, norm.xa.at(norm.turn, norm.channel_at(1, KT - 1)))
                return f(edge(which, 1), xa[:, :, :, TC:TC + 1], ACT.Copy)

            norm = norm_first()
            for n in range(2):
                squares(norm, n)
            for n in range(2):
                deviations(norm, n)
            act.wait_ge(pars1_loaded, 16)
            f(xa[:, :, :, 0:1], edge(1, 0), ACT.Copy)
            for n in range(2):
                affine(norm, n, lambda k: par1(LN1W, k), lambda k: par1(LN1B, k))
            keep_edge(norm, 1).then_inc(edge_kept.sem, 1)
            with act.Fori(0, LAYERS) as layer:
                act.wait_ge(pars_loaded, layer * 16 + 16)
                f(s_now[:], s_first[:], ACT.Copy).then_inc(layer_set, 1)
                act.wait_ge(layer_set, layer + 1)
                with act.Fori(0, CHUNKS) as chunk:
                    it = act.snap(layer * CHUNKS + chunk)

                    def full_j(n):
                        act.wait_ge(j_full.sem, j_full.at(it, n + 1))
                        return bank_j(n)

                    slot1 = act.snap(chunk * -1 + 1)
                    it_layer = act.snap(layer + chunk)
                    t = full_j(J_W1)
                    act.wait_ge(th_zero.sem, th_zero.at(it, 1))
                    for b in range(B):
                        rows = slice(DM * b, DM * b + DM)
                        last = f(th_a[rows, b, :], t[rows, 0:TC], ACT.Tanh)
                    j_free.inc(last)
                    for n in range(2):
                        j_free.inc(f(th_b[:, n * HALF:(n + 1) * HALF], full_j(J_W1 + 1 + n), ACT.Tanh))

                    def decay(pair):
                        act.wait_ge(j_free.sem, j_free.at(it, J_AT["w"] + pair + 1))
                        w_ready.inc(f(hm["w"][:, 2 * pair:2 * pair + 2, :], hm["w"][:, 2 * pair:2 * pair + 2, :], ACT.Exp, scale=-1.0))

                    def set_scan(n):
                        jh, i = n // S, n % S
                        if n == 0:
                            act.wait_ge(s_saved.sem, s_saved.at(it, 0))
                            act.wait_ge(w_ready.sem, w_ready.at(it, 1))
                            act.wait_ge(mix_ready.sem, mix_ready.at(it, 2 * STREAMS))
                        if n == 1:
                            act.wait_ge(w_ready.sem, w_ready.at(it, 8))
                            act.wait_ge(ruk_step.sem, ruk_step.at(it, 7))
                        kv_free(act, it, scan_step(n))
                        f(kv[scan_step(n) % 4][:, :, 0:1], s_at[:, i, JH * jh:JH * jh + JH].rearrange("p (j o) -> p j o", o=1), ACT.Copy)
                        if n >= 2:
                            act.wait_ge(scan_ready.sem, scan_ready.at(it, n - 1))
                        scan_set.inc(f(wt[n % 2][:, :, 1:TC + 1], over(hm["w"][:, i, :], JH), ACT.Copy))

                    for s in ORDER[:-1]:
                        if s == "w":
                            for b in range(B):
                                t = full_j(J_AT["td"] + b)
                                j_free.inc(f(tdh[:, b * TC:(b + 1) * TC], t[:, 0:TC], ACT.Tanh))
                        if s == "r":
                            act.wait_ge(x_stored, it * 32 + 16)
                        for pair in range(S // 2):
                            t = full_j(J_AT[s] + pair).rearrange("p (i t) -> p i t", i=2)
                            if s == "w":
                                for o in range(2):
                                    last = f(hm["w"][:, 2 * pair + o, :], t[:, o, :], ACT.Exp, bias=par(TDEC, 2 * pair + o))
                                j_free.inc(last)
                                if pair:
                                    decay(pair - 1)
                                if pair == SET_AT:
                                    set_scan(0)
                            else:
                                j_free.inc(f(hm[s][:, 2 * pair:2 * pair + 2, :], t, ACT.Copy))
                        if s == "w":
                            decay(S // 2 - 1)

                    def collect(jh):
                        for c in range(RING):
                            act.wait_ge(m_full.sem, m_full.at(it, M_ACC + RING * jh + c + 1))
                            m_free.inc(f(att[:, JH * jh + 2 * c:JH * jh + 2 * c + 2, :].rearrange("p j t -> p (j t)"), bank_m(M_ACC + RING * jh + c), ACT.Copy))

                    def gate_out(pair):
                        t = full_j(J_G[pair]).rearrange("p (i t) -> p i t", i=2)
                        j_free.inc(f(hm["g"][:, 2 * pair:2 * pair + 2, :], t, ACT.Silu))

                    set_scan(1)
                    for n in range(2 * S):
                        jh, i = n // S, n % S
                        act.wait_ge(scan_ready.sem, scan_ready.at(it, n + 1))
                        s_saved.inc(f(s_at[:, i, JH * jh:JH * jh + JH].rearrange("p (j o) -> p j o", o=1), s_ext[:, :, TC:TC + 1], ACT.Copy))
                        if n + 2 < 2 * S:
                            set_scan(n + 2)
                        if n in G_OUT:
                            gate_out(G_OUT.index(n))
                        if n == S:
                            collect(0)
                    collect(1)

                    t = full_j(J_GSUM)
                    j_free.inc(f(gsum, t[:, 0:TC], ACT.Copy, scale=-1.0 / S))
                    for n in range(GQ):
                        j = slice(S // GQ * n, S // GQ * (n + 1))
                        act.wait_ge(gn_step.sem, gn_step.at(it, n + 1))
                        gn_act.inc(f(gsq[:, j, :], gd[:, j, :], ACT.Square))
                    t = full_j(J_GVAR)
                    j_free.inc(f(gstd, t[:, 0:TC], ACT.Sqrt, scale=1.0 / S, bias=eps[:]))
                    squares(norm1(it), 0)
                    gate_out(S // 2 - 2)
                    for n in range(GQ - 1):
                        act.wait_ge(gn_step.sem, gn_step.at(it, GQ + 1 + n + 1))
                        for j in range(S // GQ * n, S // GQ * (n + 1)):
                            last = f(gd[:, j, :], gd[:, j, :], ACT.Identity, scale=par(GNW, j), bias=par(GNB, j))
                        gn_act.inc(last)
                        if n == 1:
                            gate_out(S // 2 - 1)

                    norm = norm1(it)
                    squares(norm, 1)
                    for n in range(2):
                        deviations(norm, n)
                    norm = norm2(it)
                    squares(norm, 0)
                    deviations(norm, 0)
                    act.wait_ge(edge_kept.sem, edge_kept.at(it, 0))
                    edge_set.inc(f(xa[:, :, :, 0:1], edge(0, chunk), ACT.Copy))
                    affine(norm, 0, lambda k: par(LN2W, k), lambda k: par(LN2B, k))
                    squares(norm, 1)

                    def feed(tiles, n, buf, fn):
                        c, m = n // KT, n % KT
                        t = full_j(tiles[n])
                        j_free.inc(f(buf[:, m, c * HALF:(c + 1) * HALF], t, fn))

                    for n in range(2 * KT):
                        if n == 1:
                            deviations(norm, 1)
                        if n == 2:
                            affine(norm, 1, lambda k: par(LN2W, k), lambda k: par(LN2B, k))
                            edge_kept.inc(keep_edge(norm, 0))
                        feed(J_WFR, n, rr, ACT.Sigmoid)
                    norm = norm1(it)
                    act.wait_ge(fmix_ready.sem, fmix_ready.at(it, 4))
                    act.wait_ge(edge_kept.sem, edge_kept.at(it, 1))
                    act.wait_ge(pars1_loaded, it_layer * 16 + 16)
                    edge_set.inc(f(xa[:, :, :, 0:1], edge(1, slot1), ACT.Copy))
                    for n in range(2 * KT):
                        if n % 2 == 0 and n < 4:
                            affine(norm, n // 2, lambda k: par1(LN1W, k), lambda k: par1(LN1B, k))
                        feed(range(J_WFK, J_WFK + 8), n, kk, ACT.Relu)
                    edge_kept.inc(keep_edge(norm, 1))
                    for c in (j_free, gn_act, sq_ready, edge_set, edge_kept, xa_ready, w_ready, scan_set, s_saved):
                        c.close()

            act.sem_inc(a_free.sem, a_free.credit)
            act.sem_inc(s_free.sem, s_free.credit)
            act.wait_ge(at_loaded, 6 * 16)
            f(gate[:, 1:2], gate[:, 0:1], ACT.Tanh).then_inc(gate_ready, 1)
            with act.Fori(0, B) as b:
                def full_a(n):
                    act.wait_ge(a_full.sem, a_full.at(b, n + 1))
                    return bank_a(n)

                def square(sh):
                    cols = slice(sh * 512, sh * 512 + 512)
                    act.wait_ge(d_free.sem, d_free.at(b, D_AT["mean", sh] + 1))
                    asq_ready.inc(f(asq[:, :, cols], an[:, :, cols], ACT.Square))

                def first_part(tile):
                    act.wait_ge(d_full.sem, d_full.at(b, D_AT[tile] + 1))
                    part_ready.inc(f(part(tile, 0).bitcast(F32R), bank_d(D_AT[tile]), ACT.Copy))

                square(0)
                first_part(("q", 0))
                square(1)
                t = full_a(A_VAR)
                a_free.inc(f(astd, t[:, 0:SQ], ACT.Sqrt, bias=eps[:]))
                first_part(("q", 1))
                for sh in range(2):
                    cols = slice(sh * 512, sh * 512 + 512)
                    act.wait_ge(d_free.sem, d_free.at(b, D_AT["rstd", sh] + 1))
                    for k in range(KT):
                        last = f(an[:, k, cols], an[:, k, cols], ACT.Identity, scale=lnp[:, k:k + 1], bias=lnp[:, KT + k:KT + k + 1])
                    an_ready.inc(last)
                for sh in range(2):
                    first_part(("k", 0, sh))
                for step in range(UNITS + 1):
                    for h in range(HPT):
                        if step < UNITS:
                            act.wait_ge(nmx_ready.sem, nmx_ready.at(b, HPT * step + h + 1))
                            s_free.inc(f(probs[step % 2][:, h, :].rearrange("p (a s) -> p a s", a=2), banks_s(HPT * step + h), ACT.Exp, scale=SCALE,
                                         bias=nmx[:, step % 2, h:h + 1], accum_out=den[:, step % 2, h:h + 1]))
                        if step >= 1:
                            u = step - 1
                            t = full_a(A_T + HPT * u + h)
                            a_free.inc(f(probs_t[:, 0:4, h, :], t.rearrange("p (s t) -> p s t", s=4), ACT.Copy))
                    for tile in projected(step):
                        first_part(tile)
                for c in (part_ready, a_free, s_free, asq_ready, an_ready):
                    c.close()

        @block.vector
        def _(dve):
            tt = nc.vector.tensor_tensor
            stt = nc.vector.scalar_tensor_tensor
            nc.vector.memset(ones[:], 1.0 / E).then_inc(const_ready, 1)
            nc.vector.memset(eps[:], EPS).then_inc(const_ready, 1)
            dve.wait_ge(const_ready, 4)
            nc.vector.tensor_copy(pick[:], ident[:].rearrange("p (b h) -> p b h", b=B)[:, :, 0:1].broadcast_to((P, B, P))).then_inc(const_ready, 1)
            dve.sem_inc(m_free.sem, m_free.credit)
            dve.sem_inc(first_m_free.sem, first_m_free.credit)

            def centre(norm, n):
                for b in range(HB * n, HB * n + HB):
                    dve.wait_ge(norm.m_full.sem, norm.m_full.at(norm.turn, norm.mean[b] + 1))
                    norm.m_free.inc(tt(norm.diff[:, :, b, :], norm.src[:, :, b, :], over(bank_m(norm.mean[b])[:, 0:TC], KT), ALU.subtract))

            def invert(norm, n):
                dve.wait_ge(norm.j_free.sem, norm.j_free.at(norm.turn, norm.var[n] + 1))
                norm.rstd.inc(nc.vector.reciprocal(std[n], std[n]))

            def scale(norm, n):
                dve.wait_ge(norm.m_full.sem, norm.m_full.at(norm.turn, norm.spread[n] + 1))
                for k in range(KT):
                    last = tt(half2(norm.diff, n)[:, k, :], half2(norm.diff, n)[:, k, :], bank_m(norm.spread[n]), ALU.mult)
                    (norm.xn if k < KT - 1 else norm.m_free).inc(last)

            def normalise(norm):
                for n in range(2):
                    centre(norm, n)
                for n in range(2):
                    invert(norm, n)
                for n in range(2):
                    scale(norm, n)

            def shift(norm, n):
                for k in range(KT):
                    dve.wait_ge(norm.xa.sem, norm.xa.at(norm.turn, norm.channel_at(n, k)))
                    h = xa[:, k, HB * n:HB * n + HB, :]
                    norm.sx.inc(tt(half(sx, n)[:, k], h[:, :, 0:TC], h[:, :, 1:TC + 1], ALU.subtract))

            def shifted_mix(norm, to, n, factor):
                for k in range(KT):
                    dve.wait_ge(norm.sx.sem, norm.sx.at(norm.turn, norm.channel_at(n, k)))
                    last = stt(half(to, n)[:, k], half(sx, n)[:, k], factor(k), half(xa, n)[:, k, :, 1:TC + 1], ALU.mult, ALU.add)
                return last

            norm = norm_first()
            normalise(norm)
            for n in range(2):
                shift(norm, n)
            for n in range(2):
                shifted_mix(norm, mix[1], n, lambda k: par1(MAAX, k)).then_inc(lmix_ready.sem, 1)
            with dve.Fori(0, LAYERS) as layer:
                with dve.Fori(0, CHUNKS) as chunk:
                    it = dve.snap(layer * CHUNKS + chunk)

                    def full_m(n):
                        dve.wait_ge(m_full.sem, m_full.at(it, n + 1))
                        return bank_m(n)

                    dve.wait_ge(pars_loaded, layer * 16 + 16)
                    for q, s in enumerate(ORDER):
                        if q >= 2:
                            dve.wait_ge(j_full.sem, j_full.at(it, j_end[ORDER[q - 2]]))
                        for n in range(2):
                            for k in range(KT):
                                t = full_m(M_MIX + 8 * q + 4 * n + k)
                                m_free.inc(stt(half2(mix[q % 2], n)[:, k, :], t, par(MAAS, KT * FAN[s] + k), half2(sx, n)[:, k, :], ALU.add, ALU.mult))
                            dve.wait_ge(m_free.sem, m_free.at(it, M_MIX + 8 * q + 4 * n + 4))
                            mix_ready.inc(tt(half(mix[q % 2], n), half(mix[q % 2], n), half(xa, n)[:, :, :, 1:TC + 1], ALU.add))
                            if s == "g":
                                if n == 0:
                                    dve.wait_ge(j_free.sem, j_free.at(it, J_AT["r"] + 8))
                                for i in range(JH):
                                    last = stt(kr2[:, i, :], hm["k"][:, JH * n + i, :], par(UCOL, JH * n + i), hm["r"][:, JH * n + i, :], ALU.mult, ALU.mult)
                                ruk_step.inc(last)
                                dve.wait_ge(ruk_step.sem, ruk_step.at(it, 2 * n + 1))
                                ruk_step.inc(nc.vector.tensor_reduce(ruk2[:, n, :], kr2.rearrange("p i t -> p t i"), AX_X, ALU.add))
                                dve.wait_ge(ruk_step.sem, ruk_step.at(it, 2 * n + 2))
                    ruk_step.inc(tt(ruk, ruk2[:, 0, :], ruk2[:, 1, :], ALU.add))
                    ruk_step.inc(nc.vector.memset(wt[1][:, :, 0:1], 0.0))
                    dve.wait_ge(j_full.sem, j_full.at(it, J_AT["td"] + 4))
                    ruk_step.inc(nc.vector.memset(wt[0][:, :, 0:1], 0.0))
                    dve.wait_ge(ruk_step.sem, ruk_step.at(it, 7))

                    for n in range(2 * S):
                        jh, i = n // S, n % S
                        step = scan_step(n)
                        dve.wait_ge(kv_ready.sem, kv_ready.at(it, n + 1))
                        dve.wait_ge(scan_set.sem, scan_set.at(it, n + 1))
                        dve.wait_ge(s_saved.sem, s_saved.at(it, n))
                        if n:
                            dve.wait_ge(rs_ready.sem, rs_ready.at(it, (n - 1) // S * STEPS + (n - 1) % S + 1))
                        scan_ready.inc(nc.vector.tensor_tensor_scan(s_flat, wt_flat[n % 2], kv_flat[step % 4], 0.0, ALU.mult, ALU.add))
                        dve.wait_ge(scan_ready.sem, scan_ready.at(it, n + 1))
                        rs_ready.inc(tt(kv[step % 4][:, :, 0:TC], s_ext[:, :, 0:TC], over(hm["r"][:, i, :], JH), ALU.mult))
                        if n == S - 1:
                            kv_free(dve, it, step + 1)
                            rs_ready.inc(tt(kv[(step + 1) % 4][:, :, 0:TC], hm["v"][:, JH * jh:JH * jh + JH, :], over(ruk, JH), ALU.mult))

                    dve.wait_ge(s_saved.sem, s_saved.at(it, 2 * S))
                    dve.wait_ge(j_free.sem, j_free.at(it, J_GSUM + 1))
                    for n in range(GQ):
                        j = slice(S // GQ * n, S // GQ * (n + 1))
                        gn_step.inc(tt(gd[:, j, :], att[:, j, :], over(gsum, S // GQ), ALU.add))
                    norm = norm1(it)
                    centre(norm, 0)
                    dve.wait_ge(j_free.sem, j_free.at(it, J_GVAR + 1))
                    gn_step.inc(nc.vector.reciprocal(gstd, gstd))
                    dve.wait_ge(gn_step.sem, gn_step.at(it, GQ + 1))
                    for n in range(GQ - 1):
                        j = slice(S // GQ * n, S // GQ * (n + 1))
                        gn_step.inc(tt(gd[:, j, :], gd[:, j, :], over(gstd, S // GQ), ALU.mult))
                    own = range(S - S // GQ, S)
                    for j in own:
                        last = stt(gd[:, j, :], gd[:, j, :], par(GNW, j), gstd, ALU.mult, ALU.mult)
                    gn_step.inc(last)
                    for n in range(GQ):
                        if GN_ORDER[n] == GQ - 1:
                            dve.wait_ge(j_free.sem, j_free.at(it, J_G[-1] + 1))
                            dve.wait_ge(gn_step.sem, gn_step.at(it, 2 * GQ + 1))
                            for j in own:
                                last = stt(att[:, j, :], gd[:, j, :], par(GNB, j), hm["g"][:, j, :], ALU.add, ALU.mult)
                            og_ready.inc(last)
                        else:
                            dve.wait_ge(gn_act.sem, gn_act.at(it, GQ + GN_ORDER[n] + 1))
                            j = slice(S // GQ * GN_ORDER[n], S // GQ * (GN_ORDER[n] + 1))
                            og_ready.inc(tt(att[:, j, :], gd[:, j, :], hm["g"][:, j, :], ALU.mult))
                    centre(norm, 1)

                    def residual(n):
                        c, m = n // KT, n % KT
                        if m == 0:
                            dve.wait_ge(x_loaded[c], it * 16 + 16)
                        t = full_m(M_WO[n])
                        m_free.inc(tt(half2(x, c)[:, m, :], half2(x, c)[:, m, :], t, ALU.add))

                    def feed_mix(to, at, n):
                        fmix_ready.inc(shifted_mix(norm, to, n, lambda k: par(at, k)))

                    residual(0)
                    invert(norm, 0)
                    residual(1)
                    invert(norm, 1)
                    residual(2)
                    scale(norm, 0)
                    residual(3)
                    scale(norm, 1)
                    residual(4)
                    norm = norm2(it)
                    dve.wait_ge(m_free.sem, m_free.at(it, M_WO[KT - 1] + 1))
                    centre(norm, 0)
                    residual(KT + 1)
                    invert(norm, 0)
                    residual(KT + 2)
                    scale(norm, 0)
                    residual(KT + 3)
                    shift(norm, 0)
                    feed_mix(mix[0], FMR, 0)
                    dve.wait_ge(m_free.sem, m_free.at(it, M_WO[2 * KT - 1] + 1))
                    centre(norm, 1)
                    invert(norm, 1)
                    scale(norm, 1)
                    shift(norm, 1)
                    feed_mix(mix[0], FMR, 1)
                    dve.wait_ge(j_full.sem, j_full.at(it, J_VAR2[1] + 1))
                    feed_mix(mix[1], FMK, 0)
                    feed_mix(mix[1], FMK, 1)
                    norm = norm1(it)
                    for n in range(2):
                        shift(norm, n)
                    dve.wait_ge(j_full.sem, j_full.at(it, J_WFK + 8))
                    for n in range(2):
                        lmix_ready.inc(shifted_mix(norm, mix[1], n, lambda k: par1(MAAX, k)))
                    for c in range(2):
                        for m in range(KT):
                            t = full_m(M_WFV + KT * c + m)
                            r = rr[:, m, c * HALF:(c + 1) * HALF]
                            m_free.inc(tt(r, r, t, ALU.mult))
                        for m in range(KT):
                            dve.wait_ge(m_free.sem, m_free.at(it, M_WFV + KT * c + m + 1))
                            last = tt(half2(x_new, c)[:, m, :], half2(x, c)[:, m, :], rr[:, m, c * HALF:(c + 1) * HALF], ALU.add)
                        x_done.inc(last)
                    for c in (m_free, rstd_ready, xn_ready, sx_ready, lmix_ready, ruk_step, scan_ready, rs_ready, gn_step, og_ready, fmix_ready, x_done):
                        c.close()

            dve.sem_inc(d_free.sem, d_free.credit)
            dve.wait_ge(gate_ready, 1)
            with dve.Fori(0, B) as b:
                def full_d(n):
                    dve.wait_ge(d_full.sem, d_full.at(b, n + 1))
                    return bank_d(n)

                for sh in range(2):
                    cols = slice(sh * 512, sh * 512 + 512)
                    t = full_d(D_AT["mean", sh])
                    d_free.inc(tt(an[:, :, cols], an[:, :, cols], over(t, KT), ALU.subtract))
                def second_part(tile):
                    n = part_order.index(tile)
                    dve.wait_ge(part_ready.sem, part_ready.at(b, n + 1))
                    d_free.inc(tt(part(tile, 1).bitcast(F32R), bank_d(D_AT[tile]), part(tile, 0).bitcast(F32R).bitcast(F32), ALU.subtract))

                second_part(("q", 0))
                dve.wait_ge(mask_loaded, b * 16 + 16)
                mask_step.inc(nc.vector.tensor_scalar(mbias, mask_u, -1.0, 3e38, ALU.add, ALU.mult))
                dve.wait_ge(mask_step.sem, mask_step.at(b, 1))
                mask_step.inc(nc.vector.tensor_scalar(mbias, mbias, 10.0, None, ALU.mult))
                dve.wait_ge(a_free.sem, a_free.at(b, A_VAR + 1))
                arstd_ready.inc(nc.vector.reciprocal(astd, astd))
                second_part(("q", 1))
                for sh in range(2):
                    cols = slice(sh * 512, sh * 512 + 512)
                    t = full_d(D_AT["rstd", sh])
                    d_free.inc(tt(an[:, :, cols], an[:, :, cols], over(t, KT), ALU.mult))
                for sh in range(2):
                    second_part(("k", 0, sh))
                for st in range(ST):
                    t = full_d(D_AT["v", st])
                    d_free.inc(nc.vector.tensor_copy(vals[:, st, :], t))
                dve.wait_ge(mask_step.sem, mask_step.at(b, 2))
                for step in range(UNITS + 2):
                    for h in range(HPT):
                        if step < UNITS:
                            n = HPT * step + h
                            dve.wait_ge(s_full.sem, s_full.at(b, n + 1))
                            dve.sem_inc(max_turn, 1)
                            t = banks_s(n)
                            mx_ready.inc(nc.vector.tensor_tensor_reduce(t, t, mbias.rearrange("p (a s) -> p a s", a=2), 1.0, -3.4e38, ALU.add, ALU.max,
                                                                        accum_out=mx[:, step % 2, h:h + 1]))
                            dve.wait_ge(mx_ready.sem, mx_ready.at(b, n + 1))
                            nmx_ready.inc(nc.vector.tensor_scalar(nmx[:, step % 2, h:h + 1], mx[:, step % 2, h:h + 1], -SCALE, None, ALU.mult))
                        if h == 0 and step >= 2:
                            u = step - 2
                            t = full_d(D_AT["out", u])
                            d_free.inc(nc.vector.tensor_copy(ao[:, u // TT, P * (u % TT):P * (u % TT) + P], t[:, 0:P]))
                        if 1 <= step <= UNITS:
                            t = full_d(D_AT["t", step - 1, h])
                            d_free.inc(nc.vector.tensor_copy(probs_t[:, 4:8, h, :], t.rearrange("p (s t) -> p s t", s=4)))
                    if step < UNITS:
                        dve.wait_ge(s_free.sem, s_free.at(b, HPT * step + HPT))
                        den_ready.inc(nc.vector.reciprocal(rden, den[:, step % 2, :]))
                        dve.wait_ge(den_ready.sem, den_ready.at(b, step + 1))
                        diag_ready.inc(tt(diag, ident[:].rearrange("p (o c) -> p o c", o=1).broadcast_to((P, HPT, P)),
                                          rden.rearrange("p (h o) -> p h o", o=1).broadcast_to((P, HPT, P)), ALU.mult))
                    for tile in projected(step):
                        second_part(tile)
                dve.wait_ge(ay_loaded, b * (16 * CHUNKS) + 16 * CHUNKS)
                for m in range(KT):
                    t = full_d(D_AT["wo", m])
                    d_free.inc(stt(ay[:, m, :], t, gate[:, 1:2], ay[:, m, :], ALU.mult, ALU.add))
                for c in (d_free, mask_step, arstd_ready, mx_ready, nmx_ready, den_ready, diag_ready):
                    c.close()

        @block.gpsimd
        def _(pool):
            nc.gpsimd.memset(ident[:], 0.0).then_inc(const_ready, 1)
            pool.wait_ge(const_ready, 3)
            nc.gpsimd.affine_select(out=ident[:], in_=ident[:], compare_op=ALU.not_equal, fill=1.0, base=0, pattern=[[-1, P]], channel_multiplier=1).then_inc(const_ready, 1)
            with pool.Fori(0, LAYERS) as layer:
                with pool.Fori(0, CHUNKS) as chunk:
                    it = pool.snap(layer * CHUNKS + chunk)
                    th_zero.inc(nc.gpsimd.memset(th_a, 0.0))
                    pool.wait_ge(j_free.sem, j_free.at(it, J_AT["v"] + 8))
                    pool.wait_ge(mix_ready.sem, mix_ready.at(it, 2 * STREAMS))
                    for n in range(2 * S):
                        jh, i = n // S, n % S
                        step = scan_step(n)
                        kv_free(pool, it, step)
                        kv_ready.inc(nc.gpsimd.tensor_tensor(kv[step % 4][:, :, 1:TC + 1], hm["v"][:, JH * jh:JH * jh + JH, :], over(hm["k"][:, i, :], JH), ALU.mult))
                    step = 2 * STEPS - 2
                    kv_free(pool, it, step)
                    own_ready.inc(nc.gpsimd.tensor_tensor(kv[step % 4][:, :, 0:TC], hm["v"][:, JH * jh:JH * jh + JH, :], over(ruk, JH), ALU.mult))
                    for c in range(2):
                        for m in range(KT):
                            pool.wait_ge(j_free.sem, j_free.at(it, J_WFK + KT * c + m + 1))
                            t = kk[:, m, c * HALF:(c + 1) * HALF]
                            kk_ready.inc(nc.gpsimd.tensor_tensor(t, t, t, ALU.mult))
                    for c in (th_zero, kv_ready, own_ready, kk_ready):
                        c.close()


def kernel(**inputs):
    import concourse.bacc as bacc
    from concourse.bass_utils import run_bass_kernel_spmd

    def arr(name):
        return np.asarray(inputs[name])

    def cols(v):
        return np.reshape(v, (KT, P)).T

    def per_head(v):
        return np.tile(np.reshape(v, (H, S)), (B, 1))

    def channel_major(wt):
        n = wt.shape[1]
        return wt.reshape(KT, P, n).transpose(1, 0, 2).reshape(P, KT * n)

    def by_position(wt):
        return wt.reshape(wt.shape[0], H, S).transpose(0, 2, 1).reshape(wt.shape[0], E)

    names = [dict(td1="decay_w1", td2="decay_w2", u="faaaa", fk="ffn_Wk", fr="ffn_Wr", fv="ffn_Wv")] + 2 * [dict(td1="td_w1", td2="td_w2", u="u", fk="Wfk", fr="Wfr", fv="Wfv")]
    small, pars1, pars, big = [], [], [], []
    for n, name in enumerate(names):
        def p(key):
            return arr(f"L{n}_xattn_{name.get(key, key)}")

        stack = p("maa_stack").reshape(STREAMS, E)
        pars1.append(np.concatenate([cols(p("ln1_w")), cols(p("ln1_b")), cols(p("maa_x"))], axis=1))
        par = [cols(stack[s]) for s in range(STREAMS)]
        par += [cols(p("ln2_w")), cols(p("ln2_b")), cols(p("ffn_maa_k")), cols(p("ffn_maa_r"))]
        par += [per_head(p("time_decay")), per_head(p("u").reshape(E)), per_head(p("gn_w")), per_head(p("gn_b"))]
        pars.append(np.concatenate(par, axis=1))
        w1 = p("maa_w1").reshape(E, STREAMS, DM)[:, [FAN[s] for s in ORDER[1:] + ORDER[:1]]].reshape(E, STREAMS * DM)
        w2 = np.zeros((P, STREAMS, E), np.float32)
        w2[:, FAN[ORDER[0]]] = np.tile(p("maa_w2")[FAN[ORDER[0]]], (P // DM, 1))
        for q, s in enumerate(ORDER[1:]):
            w2[DM * q:DM * q + DM, FAN[s]] = p("maa_w2")[FAN[s]]
        td1, td2 = np.zeros((E, P), np.float32), np.zeros((P, E), np.float32)
        td1[:, :DD], td2[:DD] = p("td1"), by_position(p("td2"))
        small.append(np.concatenate([channel_major(w1), w2.reshape(P, STREAMS * E), channel_major(td1), td2], axis=1))
        big.append(np.stack([channel_major(by_position(p(w).T)) for w in ("Wk", "Wv", "Wr", "Wg")] + [channel_major(p(w).T) for w in ("Wo", "fr", "fk", "fv")]))
    x = arr("x")
    context = arr("ctx_2048")
    mask = arr("mask_BxS2_bf1").view(np.uint8)
    arrays = {
        "x": x.reshape(B, CHUNKS, TC, KT, P).transpose(1, 4, 3, 0, 2).reshape(CHUNKS, P, KT * COLS),
        "rows": context[:, 0:2].reshape(B, 2, KT, P).transpose(3, 1, 2, 0).reshape(P, 2 * KT * B),
        "s_first": context[:, 2:2 + S].reshape(B * H, S * S),
        "small": np.stack(small),
        "pars1": np.stack(pars1),
        "pars": np.stack(pars),
        "big": np.stack(big),
        "ctx": context.transpose(0, 2, 1).reshape(B, KT, P, SK).transpose(0, 2, 1, 3).reshape(B, P, KT * SK),
        "mask": mask,
        "at_w": np.stack([channel_major(arr(f"L3_xattn_{w}").T) for w in ("Wq", "Wk", "Wv", "Wo")]),
        "at_ln": np.concatenate([cols(arr("L3_xattn_ln_gamma")), cols(arr("L3_xattn_ln_beta"))], axis=1),
        "gate": np.tile(arr("L3_xattn_gate").reshape(1, 1), (P, 1)),
    }
    arrays = {k: np.ascontiguousarray(v) for k, v in arrays.items()}
    nc = bacc.Bacc("TRN2", target_bir_lowering=False, num_devices=1)
    aps = {k: nc.dram_tensor(f"{k}_dram", v.shape, mybir.dt.from_np(v.dtype), kind="ExternalInput").ap() for k, v in arrays.items()}
    aps["og"] = nc.dram_tensor("og_dram", (B * H, S, TC), F32).ap()
    aps["xs"] = nc.dram_tensor("xs_dram", (CHUNKS, P, KT * COLS), F32).ap()
    aps["out"] = nc.dram_tensor("out_dram", (B, P, KT * T), F32, kind="ExternalOutput").ap()
    build(nc, aps)
    r = run_bass_kernel_spmd(nc, [{f"{k}_dram": v for k, v in arrays.items()}], core_ids=[0])
    out = r.results[0]["out_dram"]
    return np.ascontiguousarray(out.reshape(B, P, KT, T).transpose(0, 3, 2, 1).reshape(B, T, E))
```
